# Optimizing a Trainium2 kernel written in Bass

```python
import numpy as np
import jax
import jax.numpy as jnp

def _softmax(x, axis=-1):
    return jax.nn.softmax(x, axis=axis)

def _gelu(x):
    return jax.nn.gelu(x, approximate=True)

def _silu(x):
    return jax.nn.silu(x)

def _sigmoid(x):
    return jax.nn.sigmoid(x)

def _layernorm(x, axis=-1, eps=1e-05):
    m = jnp.mean(x, axis=axis, keepdims=True)
    v = jnp.var(x, axis=axis, keepdims=True)
    return (x - m) / jnp.sqrt(v + eps)

def _scatter_add(tgt, idx, src, axis=0):
    return tgt.at[idx].add(src)

def _segment_sum(src, seg, n):
    return jax.ops.segment_sum(src, seg, n)
kernel_name = 'mk_lm_tower_d1_tok_ids512_r4_6e5a39'

def setup_inputs(seed: int=0):
    np.random.seed(seed)
    _w = jnp.asarray

    def _rec_inputs():
        import jax
        import jax.numpy as jnp
        _rk = jax.random.key(seed)
        x = jax.random.randint(jax.random.fold_in(_rk, 1), (2, 1024), 0, 128, jnp.int32)
        mask_BS_i1_0 = jnp.where(jnp.ones((2, 1024), dtype=bool), 1, 0).astype(jnp.int32)
        itok_BS_0_999 = jax.random.randint(jax.random.fold_in(_rk, 22), (2, 1024), 0, 250, jnp.int32)
        itok_BS_0_63 = jax.random.randint(jax.random.fold_in(_rk, 23), (2, 1024), 0, 64, jnp.int32)
        mask_BS_i0_1 = jnp.where(jnp.ones((2, 1024), dtype=bool), 0, 1).astype(jnp.int32)
        mask_BS_b0_1 = jnp.logical_not(jnp.ones((2, 1024), dtype=bool))
        return (x, mask_BS_i1_0, itok_BS_0_999, itok_BS_0_63, mask_BS_i0_1, mask_BS_b0_1)
    x, mask_BS_i1_0, itok_BS_0_999, itok_BS_0_63, mask_BS_i0_1, mask_BS_b0_1 = _rec_inputs()

    def _L0_tok_setup():
        import jax, jax.numpy as jnp
        import numpy as np
        B, S, D, H, W, L, V, FF = (8, 1024, 192, 12, 128, 2, 128, 768)
        G_IDX = (0,)

        def _ln(x, g, b):
            m = x.mean(-1, keepdims=True)
            v = ((x - m) ** 2).mean(-1, keepdims=True)
            return (x - m) * jax.lax.rsqrt(v + 1e-05) * g + b

        def _band_blocks(t, w):
            b, h, s, dh = t.shape
            nb = s // w
            tp = jnp.pad(t, ((0, 0), (0, 0), (w, w), (0, 0))).reshape(b, h, nb + 2, w, dh)
            return jnp.concatenate([tp[:, :, 0:nb], tp[:, :, 1:nb + 1], tp[:, :, 2:nb + 2]], axis=3)

        def _longformer_attn(x, att_mask, Wq, bq, Wk, bk, Wv, bv, Wo, bo, w, gidx):
            b, s, d = x.shape
            dh = d // H
            proj = lambda Wm, bm: (x @ Wm.T + bm).reshape(b, s, H, dh).transpose(0, 2, 1, 3)
            q = proj(Wq, bq) / np.float32(np.sqrt(dh))
            k = proj(Wk, bk)
            v = proj(Wv, bv)
            nb = s // w
            qb = q.reshape(b, H, nb, w, dh)
            kb = _band_blocks(k, w)
            vb = _band_blocks(v, w)
            sb = jnp.einsum('bhnqd,bhnkd->bhnqk', qb, kb)
            i = jnp.arange(w)[:, None]
            jj = jnp.arange(3 * w)[None, :]
            allowed = (jj - i >= 0) & (jj - i <= 2 * w)
            pos = jnp.arange(nb)[:, None] * w - w + jj
            valid = (pos >= 0) & (pos < s)
            key_bias = jnp.where(att_mask != 0, -10000.0, 0.0)
            kbias = jnp.pad(key_bias, ((0, 0), (w, w)), constant_values=-1000000000.0).reshape(b, nb + 2, w)
            kbb = jnp.concatenate([kbias[:, 0:nb], kbias[:, 1:nb + 1], kbias[:, 2:nb + 2]], axis=2)
            bias = jnp.where(allowed[None, None] & valid[None, :, None, :], kbb[:, :, None, :], -1000000000.0)
            sb = sb + bias[:, None]
            sb_flat = sb.reshape(b, H, s, 3 * w)
            g = jnp.asarray(gidx)
            ng = g.shape[0]
            kg = k[:, :, g]
            vg = v[:, :, g]
            sg = jnp.einsum('bhsd,bhgd->bhsg', q, kg)
            probs = jax.nn.softmax(jnp.concatenate([sg, sb_flat], axis=-1), axis=-1)
            pg = probs[..., :ng]
            pb = probs[..., ng:].reshape(b, H, nb, w, 3 * w)
            out = jnp.einsum('bhnqk,bhnkd->bhnqd', pb, vb).reshape(b, H, s, dh)
            out = out + jnp.einsum('bhsg,bhgd->bhsd', pg, vg)
            qg = q[:, :, g]
            sfull = jnp.einsum('bhgd,bhsd->bhgs', qg, k) + jnp.where(att_mask < 0, -10000.0, 0.0)[:, None, None, :]
            og = jnp.einsum('bhgs,bhsd->bhgd', jax.nn.softmax(sfull, axis=-1), v)
            out = out.at[:, :, g].set(og)
            out = out.transpose(0, 2, 1, 3).reshape(b, s, d)
            return out @ Wo.T + bo
        key = jax.random.key(seed)
        ks = jax.random.split(key, 32)
        sc = 0.02
        inp = {'call': jax.random.randint(ks[0], (B, S), 0, V), 'entry': jax.random.randint(ks[1], (B, S), 0, 2), 'time': jax.random.randint(ks[2], (B, S), 0, 250), 'proc': jax.random.randint(ks[3], (B, S), 0, 64), 'pid': jax.random.randint(ks[4], (B, S), 0, 64), 'tid': jax.random.randint(ks[5], (B, S), 0, 64), 'ret': jax.random.randint(ks[6], (B, S), 0, 2), 'pad_mask': jnp.zeros((B, S), dtype=bool), 'chk': 0, 'emb': jax.random.normal(ks[7], (V, D), jnp.float32) * sc, 'Wq': jax.random.normal(ks[8], (L, D, D), jnp.float32) * sc, 'bq': jnp.zeros((L, D), jnp.float32), 'Wk': jax.random.normal(ks[9], (L, D, D), jnp.float32) * sc, 'bk': jnp.zeros((L, D), jnp.float32), 'Wv': jax.random.normal(ks[10], (L, D, D), jnp.float32) * sc, 'bv': jnp.zeros((L, D), jnp.float32), 'Wo': jax.random.normal(ks[11], (L, D, D), jnp.float32) * sc, 'bo': jnp.zeros((L, D), jnp.float32), 'W1': jax.random.normal(ks[12], (L, FF, D), jnp.float32) * sc, 'b1': jnp.zeros((L, FF), jnp.float32), 'W2': jax.random.normal(ks[13], (L, D, FF), jnp.float32) * sc, 'b2': jnp.zeros((L, D), jnp.float32), 'g1': jnp.ones((L, D), jnp.float32), 'beta1': jnp.zeros((L, D), jnp.float32), 'g2': jnp.ones((L, D), jnp.float32), 'beta2': jnp.zeros((L, D), jnp.float32), 'gf': jnp.ones((D,), jnp.float32), 'betaf': jnp.zeros((D,), jnp.float32), 'Wc': jax.random.normal(ks[14], (V, D), jnp.float32) * sc, 'bc': jnp.zeros((V,), jnp.float32)}
        return inp
    _L0_tok_all = _L0_tok_setup()
    _L0_tok_in = {k: v for k, v in _L0_tok_all.items() if k in ('emb', 'Wq', 'bq', 'Wk', 'bk', 'Wv', 'bv', 'Wo', 'bo', 'W1', 'b1', 'W2', 'b2', 'g1', 'beta1', 'g2', 'beta2', 'gf', 'betaf', 'Wc', 'bc')}
    del _L0_tok_all

    def _L0_attn_setup():
        import jax, jax.numpy as jnp
        import numpy as np
        from jax import lax
        D = 128
        K = 5
        HID = 2 * D
        EPS = 1e-05

        def layernorm(x, g, b):
            mu = jnp.mean(x, axis=-1, keepdims=True)
            var = jnp.mean((x - mu) ** 2, axis=-1, keepdims=True)
            return (x - mu) * lax.rsqrt(var + EPS) * g + b

        def retention_core(xn, decay_logit, W_out, b_out, conv_w, conv_b):
            B, T, _ = xn.shape
            a = jax.nn.sigmoid(decay_logit)

            def step(s, xt):
                s = a * s + (1.0 - a) * xt
                return (s, s)
            s0 = jnp.zeros((B, D), xn.dtype)
            _, ss = lax.scan(step, s0, jnp.swapaxes(xn, 0, 1))
            ss = jnp.swapaxes(ss, 0, 1)
            y_ret = jnp.einsum('btd,ed->bte', ss, W_out) + b_out
            xc = jnp.swapaxes(xn, 1, 2)
            pad = (K - 1) // 2
            y_loc = lax.conv_general_dilated(xc, conv_w, window_strides=(1,), padding=[(pad, pad)], feature_group_count=D, dimension_numbers=('NCH', 'OIH', 'NCH'))
            y_loc = jnp.swapaxes(y_loc + conv_b[None, :, None], 1, 2)
            return y_ret + y_loc
        key = jax.random.key(seed)
        ks = jax.random.split(key, 16)
        B, T = (8, 1024)
        sc = lambda fan: 1.0 / np.sqrt(fan)
        return {'x': jax.random.normal(ks[0], (B, T, D), jnp.float32), 'decay_logit': jnp.zeros((D,), jnp.float32), 'W_out': jax.random.uniform(ks[1], (D, D), jnp.float32, -sc(D), sc(D)), 'b_out': jax.random.uniform(ks[2], (D,), jnp.float32, -sc(D), sc(D)), 'conv_w': jax.random.uniform(ks[3], (D, 1, K), jnp.float32, -sc(K), sc(K)), 'conv_b': jax.random.uniform(ks[4], (D,), jnp.float32, -sc(K), sc(K)), 'ln1_g': jnp.ones((D,), jnp.float32), 'ln1_b': jnp.zeros((D,), jnp.float32), 'ln2_g': jnp.ones((D,), jnp.float32), 'ln2_b': jnp.zeros((D,), jnp.float32), 'W1': jax.random.uniform(ks[5], (HID, D), jnp.float32, -sc(D), sc(D)), 'b1': jax.random.uniform(ks[6], (HID,), jnp.float32, -sc(D), sc(D)), 'W2': jax.random.uniform(ks[7], (D, HID), jnp.float32, -sc(HID), sc(HID)), 'b2': jax.random.uniform(ks[8], (D,), jnp.float32, -sc(HID), sc(HID))}
    _L0_attn_all = _L0_attn_setup()
    _L0_attn_in = {k: v for k, v in _L0_attn_all.items() if k in ('decay_logit', 'W_out', 'b_out', 'conv_w', 'conv_b', 'ln1_g', 'ln1_b', 'ln2_g', 'ln2_b', 'W1', 'b1', 'W2', 'b2')}
    del _L0_attn_all

    def _L0_ffn_setup():
        import jax, jax.numpy as jnp
        import numpy as np
        B, S, D, H, E = (4, 256, 128, 512, 8)
        key = jax.random.key(seed)
        ks = jax.random.split(key, 7)
        scale = 1.0 / np.sqrt(D)
        return {'x': jax.random.normal(ks[0], (B, S, D), dtype=jnp.float32), 'Wg': jax.random.normal(ks[1], (D, E), dtype=jnp.float32) * scale, 'bg': jnp.zeros((E,), dtype=jnp.float32), 'W1': jax.random.normal(ks[2], (E, D, H), dtype=jnp.float32) * scale, 'b1': jnp.zeros((E, H), dtype=jnp.float32), 'W2': jax.random.normal(ks[3], (E, H, D), dtype=jnp.float32) * (1.0 / np.sqrt(H)), 'b2': jnp.zeros((E, D), dtype=jnp.float32)}
    _L0_ffn_all = _L0_ffn_setup()
    _L0_ffn_in = {k: v for k, v in _L0_ffn_all.items() if k in ('Wg', 'bg', 'W1', 'b1', 'W2', 'b2')}
    del _L0_ffn_all
    return {'x': x, 'mask_BS_i1_0': mask_BS_i1_0, 'itok_BS_0_999': itok_BS_0_999, 'itok_BS_0_63': itok_BS_0_63, 'mask_BS_i0_1': mask_BS_i0_1, 'mask_BS_b0_1': mask_BS_b0_1, 'L0_tok_emb': _L0_tok_in['emb'], 'L0_tok_Wq': _L0_tok_in['Wq'], 'L0_tok_bq': _L0_tok_in['bq'], 'L0_tok_Wk': _L0_tok_in['Wk'], 'L0_tok_bk': _L0_tok_in['bk'], 'L0_tok_Wv': _L0_tok_in['Wv'], 'L0_tok_bv': _L0_tok_in['bv'], 'L0_tok_Wo': _L0_tok_in['Wo'], 'L0_tok_bo': _L0_tok_in['bo'], 'L0_tok_W1': _L0_tok_in['W1'], 'L0_tok_b1': _L0_tok_in['b1'], 'L0_tok_W2': _L0_tok_in['W2'], 'L0_tok_b2': _L0_tok_in['b2'], 'L0_tok_g1': _L0_tok_in['g1'], 'L0_tok_beta1': _L0_tok_in['beta1'], 'L0_tok_g2': _L0_tok_in['g2'], 'L0_tok_beta2': _L0_tok_in['beta2'], 'L0_tok_gf': _L0_tok_in['gf'], 'L0_tok_betaf': _L0_tok_in['betaf'], 'L0_tok_Wc': _L0_tok_in['Wc'], 'L0_tok_bc': _L0_tok_in['bc'], 'L0_attn_decay_logit': _L0_attn_in['decay_logit'], 'L0_attn_W_out': _L0_attn_in['W_out'], 'L0_attn_b_out': _L0_attn_in['b_out'], 'L0_attn_conv_w': _L0_attn_in['conv_w'], 'L0_attn_conv_b': _L0_attn_in['conv_b'], 'L0_attn_ln1_g': _L0_attn_in['ln1_g'], 'L0_attn_ln1_b': _L0_attn_in['ln1_b'], 'L0_attn_ln2_g': _L0_attn_in['ln2_g'], 'L0_attn_ln2_b': _L0_attn_in['ln2_b'], 'L0_attn_W1': _L0_attn_in['W1'], 'L0_attn_b1': _L0_attn_in['b1'], 'L0_attn_W2': _L0_attn_in['W2'], 'L0_attn_b2': _L0_attn_in['b2'], 'L0_ffn_Wg': _L0_ffn_in['Wg'], 'L0_ffn_bg': _L0_ffn_in['bg'], 'L0_ffn_W1': _L0_ffn_in['W1'], 'L0_ffn_b1': _L0_ffn_in['b1'], 'L0_ffn_W2': _L0_ffn_in['W2'], 'L0_ffn_b2': _L0_ffn_in['b2']}

def reference(x, mask_BS_i1_0, itok_BS_0_999, itok_BS_0_63, mask_BS_i0_1, mask_BS_b0_1, L0_tok_emb, L0_tok_Wq, L0_tok_bq, L0_tok_Wk, L0_tok_bk, L0_tok_Wv, L0_tok_bv, L0_tok_Wo, L0_tok_bo, L0_tok_W1, L0_tok_b1, L0_tok_W2, L0_tok_b2, L0_tok_g1, L0_tok_beta1, L0_tok_g2, L0_tok_beta2, L0_tok_gf, L0_tok_betaf, L0_tok_Wc, L0_tok_bc, L0_attn_decay_logit, L0_attn_W_out, L0_attn_b_out, L0_attn_conv_w, L0_attn_conv_b, L0_attn_ln1_g, L0_attn_ln1_b, L0_attn_ln2_g, L0_attn_ln2_b, L0_attn_W1, L0_attn_b1, L0_attn_W2, L0_attn_b2, L0_ffn_Wg, L0_ffn_bg, L0_ffn_W1, L0_ffn_b1, L0_ffn_W2, L0_ffn_b2):
    import jax
    import jax.numpy as jnp

    def _L0_tok_ref(call, entry, time, proc, pid, tid, ret, pad_mask, chk, emb, Wq, bq, Wk, bk, Wv, bv, Wo, bo, W1, b1, W2, b2, g1, beta1, g2, beta2, gf, betaf, Wc, bc):
        import jax, jax.numpy as jnp
        import numpy as np
        B, S, D, H, W, L, V, FF = (8, 1024, 192, 12, 128, 2, 128, 768)
        G_IDX = (0,)

        def _ln(x, g, b):
            m = x.mean(-1, keepdims=True)
            v = ((x - m) ** 2).mean(-1, keepdims=True)
            return (x - m) * jax.lax.rsqrt(v + 1e-05) * g + b

        def _band_blocks(t, w):
            b, h, s, dh = t.shape
            nb = s // w
            tp = jnp.pad(t, ((0, 0), (0, 0), (w, w), (0, 0))).reshape(b, h, nb + 2, w, dh)
            return jnp.concatenate([tp[:, :, 0:nb], tp[:, :, 1:nb + 1], tp[:, :, 2:nb + 2]], axis=3)

        def _longformer_attn(x, att_mask, Wq, bq, Wk, bk, Wv, bv, Wo, bo, w, gidx):
            b, s, d = x.shape
            dh = d // H
            proj = lambda Wm, bm: (x @ Wm.T + bm).reshape(b, s, H, dh).transpose(0, 2, 1, 3)
            q = proj(Wq, bq) / np.float32(np.sqrt(dh))
            k = proj(Wk, bk)
            v = proj(Wv, bv)
            nb = s // w
            qb = q.reshape(b, H, nb, w, dh)
            kb = _band_blocks(k, w)
            vb = _band_blocks(v, w)
            sb = jnp.einsum('bhnqd,bhnkd->bhnqk', qb, kb)
            i = jnp.arange(w)[:, None]
            jj = jnp.arange(3 * w)[None, :]
            allowed = (jj - i >= 0) & (jj - i <= 2 * w)
            pos = jnp.arange(nb)[:, None] * w - w + jj
            valid = (pos >= 0) & (pos < s)
            key_bias = jnp.where(att_mask != 0, -10000.0, 0.0)
            kbias = jnp.pad(key_bias, ((0, 0), (w, w)), constant_values=-1000000000.0).reshape(b, nb + 2, w)
            kbb = jnp.concatenate([kbias[:, 0:nb], kbias[:, 1:nb + 1], kbias[:, 2:nb + 2]], axis=2)
            bias = jnp.where(allowed[None, None] & valid[None, :, None, :], kbb[:, :, None, :], -1000000000.0)
            sb = sb + bias[:, None]
            sb_flat = sb.reshape(b, H, s, 3 * w)
            g = jnp.asarray(gidx)
            ng = g.shape[0]
            kg = k[:, :, g]
            vg = v[:, :, g]
            sg = jnp.einsum('bhsd,bhgd->bhsg', q, kg)
            probs = jax.nn.softmax(jnp.concatenate([sg, sb_flat], axis=-1), axis=-1)
            pg = probs[..., :ng]
            pb = probs[..., ng:].reshape(b, H, nb, w, 3 * w)
            out = jnp.einsum('bhnqk,bhnkd->bhnqd', pb, vb).reshape(b, H, s, dh)
            out = out + jnp.einsum('bhsg,bhgd->bhsd', pg, vg)
            qg = q[:, :, g]
            sfull = jnp.einsum('bhgd,bhsd->bhgs', qg, k) + jnp.where(att_mask < 0, -10000.0, 0.0)[:, None, None, :]
            og = jnp.einsum('bhgs,bhsd->bhgd', jax.nn.softmax(sfull, axis=-1), v)
            out = out.at[:, :, g].set(og)
            out = out.transpose(0, 2, 1, 3).reshape(b, s, d)
            return out @ Wo.T + bo
        x = emb[call]
        g = jnp.asarray(G_IDX)
        att_mask = jnp.zeros((call.shape[0], call.shape[1]), jnp.float32).at[:, g].set(10000.0)
        att_mask = jnp.where(pad_mask, -10000.0, att_mask)
        for l in range(L):
            a = _longformer_attn(x, att_mask, Wq[l], bq[l], Wk[l], bk[l], Wv[l], bv[l], Wo[l], bo[l], W, G_IDX)
            x = _ln(x + a, g1[l], beta1[l])
            h = jax.nn.relu(x @ W1[l].T + b1[l]) @ W2[l].T + b2[l]
            x = _ln(x + h, g2[l], beta2[l])
        x = _ln(x, gf, betaf)
        return x @ Wc.T + bc

    def _L0_attn_ref(x, decay_logit, W_out, b_out, conv_w, conv_b, ln1_g, ln1_b, ln2_g, ln2_b, W1, b1, W2, b2):
        import jax, jax.numpy as jnp
        import numpy as np
        from jax import lax
        D = 128
        K = 5
        HID = 2 * D
        EPS = 1e-05

        def layernorm(x, g, b):
            mu = jnp.mean(x, axis=-1, keepdims=True)
            var = jnp.mean((x - mu) ** 2, axis=-1, keepdims=True)
            return (x - mu) * lax.rsqrt(var + EPS) * g + b

        def retention_core(xn, decay_logit, W_out, b_out, conv_w, conv_b):
            B, T, _ = xn.shape
            a = jax.nn.sigmoid(decay_logit)

            def step(s, xt):
                s = a * s + (1.0 - a) * xt
                return (s, s)
            s0 = jnp.zeros((B, D), xn.dtype)
            _, ss = lax.scan(step, s0, jnp.swapaxes(xn, 0, 1))
            ss = jnp.swapaxes(ss, 0, 1)
            y_ret = jnp.einsum('btd,ed->bte', ss, W_out) + b_out
            xc = jnp.swapaxes(xn, 1, 2)
            pad = (K - 1) // 2
            y_loc = lax.conv_general_dilated(xc, conv_w, window_strides=(1,), padding=[(pad, pad)], feature_group_count=D, dimension_numbers=('NCH', 'OIH', 'NCH'))
            y_loc = jnp.swapaxes(y_loc + conv_b[None, :, None], 1, 2)
            return y_ret + y_loc
        y = retention_core(layernorm(x, ln1_g, ln1_b), decay_logit, W_out, b_out, conv_w, conv_b)
        x = x + y
        h = layernorm(x, ln2_g, ln2_b)
        h = jax.nn.gelu(jnp.einsum('btd,hd->bth', h, W1) + b1, approximate=False)
        y = jnp.einsum('bth,dh->btd', h, W2) + b2
        return x + y

    def _L0_ffn_ref(x, Wg, bg, W1, b1, W2, b2):
        import jax, jax.numpy as jnp
        import numpy as np
        B, S, D, H, E = (4, 256, 128, 512, 8)
        b, s, d = x.shape
        xf = x.reshape(-1, d)
        logits = xf @ Wg + bg
        scores = jax.nn.softmax(logits, axis=-1)
        top_s, top_i = jax.lax.top_k(scores, 1)
        idx = top_i[:, 0]
        sc = top_s[:, 0]
        n_experts = Wg.shape[1]
        out = jnp.zeros_like(xf)
        for e in range(n_experts):
            h = jax.nn.relu(xf @ W1[e] + b1[e]) @ W2[e] + b2[e]
            out = jnp.where((idx == e)[:, None], h, out)
        out = out * sc[:, None]
        return out.reshape(b, s, d)
    h = _L0_tok_ref(x, mask_BS_i1_0, itok_BS_0_999, itok_BS_0_63, itok_BS_0_63, itok_BS_0_63, mask_BS_i0_1, mask_BS_b0_1, 0, L0_tok_emb, L0_tok_Wq, L0_tok_bq, L0_tok_Wk, L0_tok_bk, L0_tok_Wv, L0_tok_bv, L0_tok_Wo, L0_tok_bo, L0_tok_W1, L0_tok_b1, L0_tok_W2, L0_tok_b2, L0_tok_g1, L0_tok_beta1, L0_tok_g2, L0_tok_beta2, L0_tok_gf, L0_tok_betaf, L0_tok_Wc, L0_tok_bc)
    h = h + _L0_attn_ref(_layernorm(h, axis=-1), L0_attn_decay_logit, L0_attn_W_out, L0_attn_b_out, L0_attn_conv_w, L0_attn_conv_b, L0_attn_ln1_g, L0_attn_ln1_b, L0_attn_ln2_g, L0_attn_ln2_b, L0_attn_W1, L0_attn_b1, L0_attn_W2, L0_attn_b2)
    h = h + _L0_ffn_ref(_layernorm(h, axis=-1), L0_ffn_Wg, L0_ffn_bg, L0_ffn_W1, L0_ffn_b1, L0_ffn_W2, L0_ffn_b2)
    return h

_drawn_inputs = setup_inputs


def setup_inputs(seed=0):
    import zlib

    import numpy as np

    out = dict(_drawn_inputs(seed))
    spreads = {'L0_tok_bq': (0.0, 2.0),
     'L0_tok_bk': (0.0, 2.0),
     'L0_tok_bv': (0.0, 0.1),
     'L0_tok_bo': (0.0, 0.1),
     'L0_tok_b1': (0.0, 0.1),
     'L0_tok_b2': (0.0, 0.1),
     'L0_tok_g1': (1.0, 0.2),
     'L0_tok_beta1': (0.0, 0.1),
     'L0_tok_g2': (1.0, 0.2),
     'L0_tok_beta2': (0.0, 0.1),
     'L0_tok_gf': (1.0, 0.2),
     'L0_tok_betaf': (0.0, 0.1),
     'L0_tok_bc': (0.0, 0.1),
     'L0_attn_decay_logit': (0.0, 0.8),
     'L0_attn_ln1_g': (1.0, 0.2),
     'L0_attn_ln1_b': (0.0, 0.1),
     'L0_attn_ln2_g': (1.0, 0.2),
     'L0_attn_ln2_b': (0.0, 0.296),
     'L0_ffn_bg': (0.0, 0.352),
     'L0_ffn_b1': (0.0, 0.693),
     'L0_ffn_b2': (0.0, 0.456)}
    factors = {'L0_tok_Wq': 43.358, 'L0_tok_Wk': 41.483, 'L0_attn_b1': 3.531}
    for name, (base, spread) in spreads.items():
        noise = np.random.default_rng([zlib.crc32(name.encode()), seed]).standard_normal(out[name].shape)
        drawn = base * np.exp(spread * noise) if base else spread * noise
        out[name] = jnp.asarray(drawn.astype(out[name].dtype))
    for name, factor in factors.items():
        out[name] = (out[name] * factor).astype(out[name].dtype)
    return out
```

```python
from contextlib import ExitStack

import numpy as np

import concourse.bass as bass
from concourse import mybir

ALU = mybir.AluOpType
ACT = mybir.ActivationFunctionType
AX = mybir.AxisListType
F32 = mybir.dt.float32
BF16 = mybir.dt.bfloat16
F16 = mybir.dt.float16
I32 = mybir.dt.int32
U8 = mybir.dt.uint8

P = 128
B, T = 2, 1024
NB = T // P
CH = 512
NC = T // CH
BPC = CH // P
L, D, H, FF = 2, 192, 12, 768
DH = D // H
DLO, DHI = P, D - P
DM = 128
HID = 256
KC = 5
E, EH = 8, 512
EPS = 1e-5
BAND_OUT = -1e9
KB_HI, KB_LO = -9984.0, -16.0

Q_ROWS = ((0, 16, 32), (48, 64), (80,))
K_ROWS = ((0, 48, 80), (16, 64), (32,))
NPIECE = 96
R_BIAS = 96
R_FULL = 98
R_MAX = 100
K_NAT = 100
K_ALL = 103
VW = 3 * DH + 1
HH = H // 2
LEAD = 20
PV_LAG = 2
U = NB * H


def window(n):
    return [m for m in (n - 1, n, n + 1) if 0 <= m < NB]


def program(nc, x, pad, emb, wqkv, wo, w1, w2, rw, lnl, lnf, wc, ident, band, cols, decay, convw, wout, bo2,
            ln12, aw1, ab1, aw2, ab2, wg, bg, mw1, mb1, mw2, mb2, out):
    with ExitStack() as ctx:
        def sb(name, shape, dt):
            return ctx.enter_context(nc.sbuf_tensor(name, shape, dt))

        work_sems = []

        def sem(name, work=True):
            s = ctx.enter_context(nc.semaphore(name))
            if work:
                work_sems.append(s)
            return s

        ps = [ctx.enter_context(nc.psum_tensor(f"bank{i}", [P, CH], F32)) for i in range(8)]
        psb = [p[:, :].bitcast(BF16) for p in ps]

        stack = sb("stack", [P, 2 * H, T], BF16)
        nat = sb("nat", [P, NB, 2 * H, NPIECE], BF16)
        vst = sb("vst", [P, NB, H, VW], BF16)
        xa = sb("xa", [P, T], F32)
        xb = sb("xb", [P, T], F32)
        ata = sb("ata", [P, T], F32)
        atb = sb("atb", [P, T], F32)
        wqa = sb("wqa", [P, 3 * D], F32)
        wqb = sb("wqb", [P, 3 * D], F32)
        woa = sb("woa", [P, D], F32)
        wob = sb("wob", [P, D], F32)
        w1a = sb("w1a", [P, FF], F32)
        w1b = sb("w1b", [P, FF], F32)
        w2s = sb("w2s", [P, FF // P, D], F32)
        rwb = sb("rwb", [P, D], F32)
        lna = sb("lna", [P, 4], F32)
        lnb = sb("lnb", [P, 4], F32)
        lfa = sb("lfa", [P, 2], F32)
        lfb = sb("lfb", [P, 2], F32)
        wca = sb("wca", [P, DM], F32)
        wcb = sb("wcb", [P, DM], F32)
        embs = sb("embs", [P, D], F32)
        idf = sb("idf", [P, P], F32)
        idb = sb("idb", [P, P], BF16)
        bandf = sb("bandf", [P, 2, P], F32)
        bandb = sb("bandb", [P, 2, P], BF16)
        colc = sb("colc", [P, 4], F32)
        bm = sb("bm", [P, D], F32)
        ones = sb("ones", [P, P], F32)
        onesb = sb("onesb", [P, P], BF16)
        epst = sb("epst", [P, 1], F32)
        kbrow = sb("kbrow", [1, 4, T], BF16)
        padu = sb("padu", [1, T // 4], I32)
        res = sb("res", [P, 2, 2 * D], F32)
        resv = sb("resv", [P, 2, D], F32)
        k0s = sb("k0s", [P, H], BF16)
        q0s = sb("q0s", [P, H, H], BF16)
        v0b = sb("v0b", [P, H, DH], F32)
        v0t = sb("v0t", [P, 2, H, DH], F32)
        p32 = sb("p32", [P, 3, 3 * P], F32)
        p1 = sb("p1", [P, 4, 3 * P], F16)
        p2 = sb("p2", [P, 4, 3 * P], F16)
        nmx = sb("nmx", [P, 3, H], F32)
        nm = sb("nm", [P, H], F32)
        nmr = sb("nmr", [P, H], F32)
        mcat = sb("mcat", [P, 3, H], BF16)
        mtr = sb("mtr", [3 * H, 2, P], BF16)
        dg0 = sb("dg0", [P, 4, H], F32)
        eg = sb("eg", [P, 4, H], F32)
        pvt = sb("pvt", [P, 2, 4, HH, DH], F32)
        den = sb("den", [P, 2, 2, HH], F32)
        att = sb("att", [P, 2, D], F32)
        fst = sb("fst", [H, 4], F32)
        f1 = sb("f1", [P, NB, H], F16)
        f2 = sb("f2", [P, NB, H], F16)
        og = sb("og", [H, 3, D], F32)
        stt_ = sb("bnst", [P, 4, 6], F32)
        mv = sb("mv", [P, 4, 2], F32)
        ve = sb("ve", [P, 4], F32)
        rstd = sb("rstd", [P, 4], F32)
        zt = sb("zt", [P, 2, D], F32)
        hid = sb("hid", [P, FF // P, CH], F32)
        dcol = sb("dcol", [P, 4], F32)
        cw = sb("cw", [P, KC], F32)
        diag = sb("diag", [P, KC, DM], F32)
        wos = sb("wos", [P, DM], F32)
        bo2s = sb("bo2s", [2, DM], F32)
        l12 = sb("l12", [P, 4], F32)
        aw1s = sb("aw1s", [P, HID], F32)
        ab1s = sb("ab1s", [P, 2], F32)
        aw2s = sb("aw2s", [P, 2, DM], F32)
        ab2s = sb("ab2s", [1, DM], F32)
        wgs = sb("wgs", [P, E], F32)
        bgs = sb("bgs", [1, E], F32)
        mb1s = sb("mb1s", [P, E, EH // P], F32)
        mb2s = sb("mb2s", [E, DM], F32)
        gt = sb("gt", [P, 6, NB, E], F32)
        gs = sb("gs", [P, 4, NB], F32)
        selt = ata[0:E, :]

        room = stack[:, :, :].rearrange("p a t -> p (a t)").bitcast(F32)

        def part(i, n=T):
            return room[:, i * T:i * T + n]

        h0 = part(0)
        x1 = part(1)
        st = part(2)
        d1 = part(3)
        gl = part(4, 2 * T)
        xm = part(6)
        eh = part(7, 4 * CH * 2 // 2)
        acc = part(9)
        ht = part(10)
        mw = nat[:, :, :, :].rearrange("p a b c -> p (a b c)").bitcast(F32)
        mw1s = mw[:, 0:E * EH].rearrange("p (e m) -> p e m", e=E)
        mw2s = mw[:, E * EH:2 * E * EH].rearrange("p (e j m) -> p e j m", e=E, j=EH // P)
        xn = sb("xn", [P, T + KC - 1], F32)
        idsi = hid[:, 0:2, :].rearrange("p a b -> p (a b)").bitcast(I32)
        oneh = hid[:, 2:4, :].rearrange("p a b -> p (a b)")
        pfull = hid[0:H, 0:4, :].rearrange("p (i a) b -> p i (a b)", i=2)
        padw = (ata[0:1, :], atb[0:1, :])

        arrive = sem("arrive", False)
        go = sem("go", False)
        spare = sem("spare", False)
        const_in = sem("const_in", False)
        setup = sem("setup", False)
        stage = sem("stage")
        ids_in = sem("ids_in")
        pad_in = sem("pad_in")
        kb_out = sem("kb_out")
        onehot_ready = sem("onehot_ready")
        padf_ready = sem("padf_ready")
        emb_mm = sem("emb_mm")
        emb_cp = sem("emb_cp")
        dve_own = sem("dve_own")
        act_own = sem("act_own")
        pool_own = sem("pool_own")
        wqkv_in = sem("wqkv_in")
        wrest_in = sem("wrest_in")
        qk_mm = sem("qk_mm")
        v_mm = sem("v_mm")
        qk_p1 = sem("qk_p1")
        qk_res = sem("qk_res")
        qk_p2 = sem("qk_p2")
        v_p1 = sem("v_p1")
        v_res = sem("v_res")
        v_p2 = sem("v_p2")
        nat_ready = sem("nat_ready")
        tr_mm = sem("tr_mm")
        ev_act = sem("ev_act")
        ev_dve = sem("ev_dve")
        glob_ready = sem("glob_ready")
        v0_mm = sem("v0_mm")
        v0_ready = sem("v0_ready")
        nat_mm = sem("nat_mm")
        max_done = sem("max_done")
        sg_mm = sem("sg_mm")
        m_ready = sem("m_ready")
        mt_mm = sem("mt_mm")
        mt_copied = sem("mt_copied")
        m_in = [sem(f"m_in{i}") for i in range(2)]
        dg_ready = sem("dg_ready")
        eg_ready = sem("eg_ready")
        t_mm = sem("t_mm")
        p32_ready = sem("p32_ready")
        p1_ready = sem("p1_ready")
        p2_pool = sem("p2_pool")
        p2_dve = sem("p2_dve")
        pv_mm = sem("pv_mm")
        pvg_ready = sem("pvg_ready")
        comb = sem("comb")
        at_mm = sem("at_mm")
        at_copied = sem("at_copied")
        f_mm = sem("f_mm")
        f_max = sem("f_max")
        f_exp = sem("f_exp")
        f_norm = sem("f_norm")
        ft_mm = sem("ft_mm")
        f1_ready = sem("f1_ready")
        f2_ready = sem("f2_ready")
        og_mm = sem("og_mm")
        og_ready = sem("og_ready")
        oc_mm = sem("oc_mm")
        oc_copied = sem("oc_copied")
        y_mm = sem("y_mm")
        y_stats = sem("y_stats")
        y_rstd = sem("y_rstd")
        z_ready = sem("z_ready")
        z_mm = sem("z_mm")
        ln_out = sem("ln_out")
        h_mm = sem("h_mm")
        h_relu = sem("h_relu")
        h0_kept = sem("h0_kept")
        s_ready = sem("s_ready")
        g_mm = sem("g_mm")
        g_ready = sem("g_ready")
        lg_mm = sem("lg_mm")
        lg_sub = sem("lg_sub")
        lg_exp = sem("lg_exp")
        sel_ready = sem("sel_ready")
        st_mm = sem("st_mm")
        st_copied = sem("st_copied")
        a0_mm = sem("a0_mm")
        e_mm = sem("e_mm")
        e_relu = sem("e_relu")
        ey_mm = sem("ey_mm")
        acc_done = sem("acc_done")
        o_ready = sem("o_ready")
        o_out = sem("o_out")
        mw_in = sem("mw_in")

        first, last = min(s.num for s in work_sems), max(s.num for s in work_sems)
        assert last - first + 1 == len(work_sems)
        ROUNDS = 1 + L + 1

        class Link:

            def __init__(self, eng, own):
                self.eng, self.own, self.count = eng, own, 0

            def link(self, ins):
                self.count += 1
                ins.then_inc(self.own, 1)
                self.eng.wait_ge(self.own, self.count)

            def restart(self):
                self.count = 0

        class Stages:

            def __init__(self, eng):
                self.eng, self.count = eng, 0

            def meet(self):
                self.count += 1
                self.eng.drain().then_inc(stage, 1)
                self.eng.wait_ge(stage, 4 * self.count)

            def restart(self):
                self.count = 0

        def end_round(eng, r, clears=False):
            eng.drain().then_inc(arrive, 1)
            eng.wait_ge(arrive, 5 * r + 5)
            eng.sem_inc(spare, 1)
            if clears:
                eng.sem_clear(range(first, last + 1))
            eng.drain().then_inc(go, 1)
            eng.wait_ge(go, 5 * r + 5)
            eng.sem_inc(spare, 1)

        def blk(n, k=1):
            return slice(n * P, (n + k) * P)

        def half(b):
            return slice(b * HH, (b + 1) * HH)

        block = ctx.enter_context(nc.Block())

        @block.sync
        def _(sp):
            def load_qkv(l):
                w = wqkv[bass.ds(l, 1), :, :].rearrange("o k n -> (o k) n")
                sp.dma_start(wqa[:, :], w[0:DLO, :]).then_inc(wqkv_in, 16)
                sp.dma_start(wqb[0:DHI + 1, :], w[DLO:D + 1, :]).then_inc(wqkv_in, 16)

            def load_rest(l):
                o = wo[bass.ds(l, 1), :, :].rearrange("o k n -> (o k) n")
                a = w1[bass.ds(l, 1), :, :].rearrange("o k n -> (o k) n")
                b = w2[bass.ds(l, 1), :, :].rearrange("o k n -> (o k) n")
                r = rw[bass.ds(l, 1), :, :].rearrange("o k n -> (o k) n")
                g = lnl[bass.ds(l, 1), :, :].rearrange("o k n -> (o k) n")
                for dst, src in ((woa[:, :], o[0:DLO, :]), (wob[0:DHI + 1, :], o[DLO:D + 1, :]),
                                 (w1a[:, :], a[0:DLO, :]), (w1b[0:DHI + 1, :], a[DLO:D + 1, :]),
                                 (w2s[:, :, :], b.rearrange("(j p) n -> p j n", p=P)),
                                 (rwb[0:DHI + 1, :], r[DLO:D + 1, :]),
                                 (lna[:, :], g[0:DLO, :]), (lnb[0:DHI, :], g[DLO:D, :])):
                    sp.dma_start(dst, src).then_inc(wrest_in, 16)

            consts = [
                (idf[:, :], ident), (bandf[:, :, :], band), (colc[:, :], cols), (embs[:, :], emb),
                (lfa[:, :], lnf[0:DLO, :]), (lfb[0:DHI, :], lnf[DLO:D, :]),
                (wca[:, :], wc[0:DLO, :]), (wcb[0:DHI + 1, :], wc[DLO:D + 1, :]),
                (dcol[:, 0:1], decay), (cw[:, :], convw), (wos[:, :], wout), (bo2s[:, :], bo2),
                (l12[:, :], ln12), (aw1s[:, :], aw1), (ab1s[:, :], ab1), (aw2s[:, :, :], aw2), (ab2s[:, :], ab2),
                (wgs[:, :], wg), (bgs[:, :], bg), (mb1s[:, :, :], mb1), (mb2s[:, :], mb2),
            ]
            for dst, src in consts:
                sp.dma_start(dst, src).then_inc(const_in, 16)
            sp.wait_ge(const_in, 16 * len(consts))
            sp.sem_inc(setup, 1)
            sp.wait_ge(setup, 5)

            with sp.Fori(0, B) as b:
                sp.dma_start(idsi, x[bass.ds(b, 1), :].to_broadcast([P, T])).then_inc(ids_in, 16)
                sp.dma_start(padu[:, :], pad[bass.ds(b, 1), :]).then_inc(pad_in, 16)
                load_qkv(0)
                load_rest(0)
                sp.wait_ge(padf_ready, 2)
                for h in range(H):
                    sp.dma_start(stack[R_BIAS:R_MAX, H + h, :], kbrow[0:1, :, :]).then_inc(kb_out, 16)
                sp.wait_ge(kb_out, 16 * H)
                sp.wait_ge(ids_in, 16)
                sp.wait_ge(wqkv_in, 32)
                sp.wait_ge(wrest_in, 128)
                end_round(sp, b * ROUNDS)

                with sp.Fori(0, L) as l:
                    for n in range(NB):
                        sp.wait_ge(mt_copied, n + 1)
                        for i in range(3):
                            sp.dma_start(stack[R_MAX + i:R_MAX + i + 1, 0:H, blk(n)],
                                         mtr[i * H:(i + 1) * H, n % 2, :]).then_inc(m_in[n % 2], 16)
                    sp.wait_ge(m_in[0], 48 * NB // 2)
                    sp.wait_ge(m_in[1], 48 * NB // 2)
                    load_qkv(1 - l)
                    sp.wait_ge(wqkv_in, 32)
                    sp.wait_ge(stage, 4 * 3)
                    load_rest(1 - l)
                    sp.wait_ge(wrest_in, 128)
                    end_round(sp, b * ROUNDS + 1 + l)

                sp.dma_start(mw1s, mw1).then_inc(mw_in, 16)
                sp.dma_start(mw2s, mw2).then_inc(mw_in, 16)
                for n in range(NB):
                    sp.wait_ge(o_ready, n + 1)
                    sp.dma_start(out[bass.ds(b, 1), blk(n), :].rearrange("o p m -> (o p) m"),
                                 acc[:, blk(n)]).then_inc(o_out, 16)
                sp.wait_ge(o_out, 16 * NB)
                sp.wait_ge(mw_in, 32)
                end_round(sp, b * ROUNDS + 1 + L)

        @block.gpsimd
        def _(pool):
            ch = Link(pool, pool_own)
            sg = Stages(pool)
            pool.wait_ge(const_in, 16 * 21)
            for t, value in ((xb[DHI:DHI + 1, :], 1.0), (atb[DHI:DHI + 1, :], 1.0), (ones[:, :], 1.0), (onesb[:, :], 1.0),
                             (q0s[:, :, :], 0.0), (epst[:, :], EPS), (xn[:, :], 0.0), (bm[:, :], 1.0),
                             (vst[:, :, :, 3 * DH:VW], 1.0)):
                ch.link(nc.gpsimd.memset(t, value))
            ch.link(nc.gpsimd.affine_select(out=bm[:, :], in_=bm[:, :], compare_op=ALU.is_ge, fill=0.0, base=0,
                                            pattern=[[1, D]], channel_multiplier=-DH))
            ch.link(nc.gpsimd.affine_select(out=bm[:, :], in_=bm[:, :], compare_op=ALU.is_ge, fill=0.0, base=DH - 1,
                                            pattern=[[-1, D]], channel_multiplier=DH))
            pool.sem_clear(pool_own)
            pool.drain().then_inc(setup, 1)
            pool.wait_ge(setup, 5)

            def rstd_of(j):
                pool.wait_ge(y_stats, j + 1)
                ch.link(nc.gpsimd.tensor_tensor(ve[:, j % 4:j % 4 + 1], mv[:, j % 4, 1:2], epst[:, :], ALU.add))
                nc.gpsimd.tensor_tensor(rstd[:, j % 4:j % 4 + 1], ve[:, j % 4:j % 4 + 1], colc[:, 3:4],
                                        ALU.pow).then_inc(y_rstd, 1)

            with pool.Fori(0, B) as b:
                ch.restart()
                ch.link(nc.gpsimd.memset(stack[R_BIAS:K_ALL, H:2 * H, :], 1.0))
                ch.link(nc.gpsimd.memset(stack[R_BIAS:K_ALL, 0:H, :], 0.0))
                nc.gpsimd.memset(stack[R_BIAS:R_FULL, 0:H, :], 1.0)
                pool.drain().then_inc(padf_ready, 1)
                end_round(pool, b * ROUNDS, True)

                with pool.Fori(0, L) as l:
                    ch.restart()
                    sg.restart()
                    sg.meet()
                    for s in range(U + 14):
                        u = s - 1
                        if 0 <= u < U and u % 4 != 3:
                            pool.wait_ge(p1_ready, u + 1)
                            if u >= 4:
                                pool.wait_ge(pv_mm, u - 3)
                            w = len(window(u // H)) * P
                            nc.gpsimd.tensor_tensor(p2[:, u % 4, 0:w], p32[:, u % 3, 0:w], p1[:, u % 4, 0:w],
                                                    ALU.subtract).then_inc(p2_pool, 1)
                        n, r = divmod(s, H)
                        for g, at in ((0, 0), (1, 6)):
                            if r == at and n < NB:
                                k = 2 * n + g
                                if g == 0:
                                    pool.wait_ge(eg_ready, n + 1)
                                if k == 0:
                                    pool.wait_ge(v0_ready, 1)
                                if k >= 2:
                                    pool.wait_ge(comb, k - 1)
                                nc.gpsimd.tensor_tensor(
                                    pvt[:, g, 0, :, :], v0b[:, half(g), :],
                                    eg[:, n % 4, half(g)].unsqueeze(2).to_broadcast([P, HH, DH]),
                                    ALU.mult).then_inc(pvg_ready, 1)
                    sg.meet()
                    for j in range(2 * NB):
                        rstd_of(j)
                    sg.meet()
                    end_round(pool, b * ROUNDS + 1 + l, True)

                ch.restart()
                sg.restart()
                for j in range(NB):
                    rstd_of(j)
                sg.meet()
                for j in range(NB, 3 * NB):
                    rstd_of(j)
                sg.meet()
                for j in range(3 * NB, 4 * NB):
                    rstd_of(j)
                sg.meet()
                for j in range(4 * NB, 5 * NB):
                    rstd_of(j)
                sg.meet()
                sg.meet()
                end_round(pool, b * ROUNDS + 1 + L, True)

        @block.scalar
        def _(act):
            sg = Stages(act)
            act.wait_ge(const_in, 16 * 21)
            nc.scalar.activation(idb[:, :], idf[:, :], ACT.Copy)
            nc.scalar.activation(bandb[:, :, :], bandf[:, :, :], ACT.Copy)
            act.drain().then_inc(setup, 1)
            act.wait_ge(setup, 5)

            def norm_out(j, k, dst, gb):
                act.wait_ge(z_mm, j + 1)
                bank = ps[4 + j % 2]
                for i, (d, (g, o)) in enumerate(zip(dst, gb)):
                    ins = nc.scalar.activation(d, bank[0:d.shape[0], i * P:(i + 1) * P], ACT.Identity, bias=o, scale=g)
                ins.then_inc(ln_out, 1)

            def norm_out_d(n):
                act.wait_ge(z_mm, NB + n + 1)
                nc.scalar.activation(xn[:, 2 + n * P:2 + (n + 1) * P], ps[4 + n % 2][:, 0:P], ACT.Identity,
                                     bias=l12[:, 1:2], scale=l12[:, 0:1]).then_inc(ln_out, 1)

            with act.Fori(0, B) as b:
                for c in range(NC):
                    act.wait_ge(emb_mm, c + 1)
                    nc.scalar.activation(xa[:, c * CH:(c + 1) * CH], ps[2 * c][:, :], ACT.Copy)
                    nc.scalar.activation(xb[0:DHI, c * CH:(c + 1) * CH], ps[2 * c + 1][0:DHI, :], ACT.Copy)
                end_round(act, b * ROUNDS)

                with act.Fori(0, L) as l:
                    sg.restart()
                    for n in range(NB):
                        act.wait_ge(qk_mm, n + 1)
                        nc.scalar.activation(nat[:, n, :, 0:DH],
                                             ps[n % 2][:, 0:2 * D].rearrange("p (h d) -> p h d", d=DH),
                                             ACT.Copy).then_inc(qk_p1, 1)
                        act.wait_ge(v_mm, n + 1)
                        nc.scalar.activation(vst[:, n, :, 0:DH],
                                             ps[2 + n % 2][:, 0:D].rearrange("p (h d) -> p h d", d=DH),
                                             ACT.Copy).then_inc(v_p1, 1)
                        act.wait_ge(qk_res, n + 1)
                        r = res[:, n % 2, :].rearrange("p (h d) -> p h d", d=DH)
                        nc.scalar.activation(nat[:, n, 0:H, Q_ROWS[1][0]:Q_ROWS[1][0] + DH], r[:, 0:H, :], ACT.Copy)
                        nc.scalar.activation(nat[:, n, H:2 * H, K_ROWS[1][0]:K_ROWS[1][0] + DH], r[:, H:2 * H, :],
                                             ACT.Copy).then_inc(qk_p2, 1)
                        act.wait_ge(v_res, n + 1)
                        nc.scalar.activation(vst[:, n, :, DH:2 * DH],
                                             resv[:, n % 2, :].rearrange("p (h d) -> p h d", d=DH),
                                             ACT.Copy).then_inc(v_p2, 1)
                    for k in range(0, 2 * H, 2):
                        act.wait_ge(tr_mm, k + 1)
                        nc.scalar.activation(stack[0:NPIECE, k, :], psb[4 + k % 4][0:NPIECE, :],
                                             ACT.Copy).then_inc(ev_act, 1)
                    sg.meet()
                    for s in range(-LEAD, U + 14):
                        for n in range(NB):
                            if s == H * n - 5:
                                act.wait_ge(mt_mm, n + 1)
                                if n >= 2:
                                    act.wait_ge(m_in[n % 2], 48 * (n // 2))
                                nc.scalar.activation(mtr[:, n % 2, :], psb[5][0:3 * H, 64:64 + P],
                                                     ACT.Copy).then_inc(mt_copied, 1)
                                act.wait_ge(dg_ready, n + 1)
                                nc.scalar.activation(eg[:, n % 4, :], dg0[:, n % 4, :], ACT.Exp).then_inc(eg_ready, 1)
                        if 0 <= s < U:
                            w = len(window(s // H)) * P
                            act.wait_ge(t_mm, s + 1)
                            if s >= 4:
                                act.wait_ge(pv_mm, s - 3)
                            nc.scalar.activation(p32[:, s % 3, 0:w], ps[2 + s % 3][:, 0:w], ACT.Exp).then_inc(p32_ready, 1)
                            nc.scalar.activation(p1[:, s % 4, 0:w], ps[2 + s % 3][:, 0:w], ACT.Exp).then_inc(p1_ready, 1)
                        for n in range(NB):
                            if s == H * (n + 1) + 9:
                                act.wait_ge(at_mm, n + 1)
                                nc.scalar.activation(ata[:, blk(n)], ps[5][:, P:2 * P], ACT.Copy)
                                nc.scalar.activation(atb[0:DHI, blk(n)], ps[5][0:DHI, 2 * P:3 * P],
                                                     ACT.Copy).then_inc(at_copied, 1)
                    act.wait_ge(f_max, 1)
                    nc.scalar.activation(pfull[:, 0, 0:CH], ps[0][0:H, :], ACT.Exp, bias=fst[:, 0:1],
                                         accum_out=fst[:, 1:2]).then_inc(f_exp, 1)
                    nc.scalar.activation(pfull[:, 0, CH:T], ps[1][0:H, :], ACT.Exp, bias=fst[:, 0:1],
                                         accum_out=fst[:, 2:3]).then_inc(f_exp, 1)
                    act.wait_ge(ft_mm, 1)
                    nc.scalar.activation(f1[:, :, :], ps[2][:, 0:NB * H].rearrange("p (n h) -> p n h", h=H),
                                         ACT.Copy).then_inc(f1_ready, 1)
                    act.wait_ge(oc_mm, 1)
                    nc.scalar.activation(ata[:, 0:1], ps[3][:, 0:1], ACT.Copy)
                    nc.scalar.activation(atb[0:DHI, 0:1], ps[3][0:DHI, 8:9], ACT.Copy).then_inc(oc_copied, 1)
                    sg.meet()
                    for kind, i in SEQ_C:
                        if kind == "tr":
                            k = i // NB
                            norm_out(i, k, (xa[:, blk(i % NB)], xb[0:DHI, blk(i % NB)]),
                                     ((lna[:, 2 * k:2 * k + 1], lna[:, 2 * k + 1:2 * k + 2]),
                                      (lnb[0:DHI, 2 * k:2 * k + 1], lnb[0:DHI, 2 * k + 1:2 * k + 2])))
                        if kind == "hid":
                            act.wait_ge(h_mm, i + 1)
                            c, m = divmod(i, FF // P)
                            if c:
                                act.wait_ge(y_mm, NB + BPC)
                            nc.scalar.activation(hid[:, m, :], ps[6 + i % 2][:, :], ACT.Relu).then_inc(h_relu, 1)
                    sg.meet()
                    end_round(act, b * ROUNDS + 1 + l)

                sg.restart()
                for j in range(NB):
                    norm_out(j, 0, (xa[:, blk(j)], xb[0:DHI, blk(j)]),
                             ((lfa[:, 0:1], lfa[:, 1:2]), (lfb[0:DHI, 0:1], lfb[0:DHI, 1:2])))
                nc.scalar.activation(dcol[:, 1:2], dcol[:, 0:1], ACT.Exp, scale=-1.0).then_inc(act_own, 1)
                sg.meet()
                for n in range(NB):
                    act.wait_ge(y_mm, NB + n + 1)
                    nc.scalar.activation(h0[:, blk(n)], ps[n % 4][:, 0:DM], ACT.Copy).then_inc(h0_kept, 1)
                    if n >= 2:
                        norm_out_d(n - 2)
                norm_out_d(NB - 2)
                norm_out_d(NB - 1)
                sg.meet()
                for n in range(NB):
                    act.wait_ge(z_mm, 2 * NB + n + 1)
                    nc.scalar.activation(ht[:, blk(n)], ps[4 + n % 2][:, 0:P], ACT.Identity, bias=l12[:, 3:4],
                                         scale=l12[:, 2:3]).then_inc(ln_out, 1)
                sg.meet()
                for i in range(NC * 2):
                    c, m = divmod(i, 2)
                    act.wait_ge(g_mm, i + 1)
                    nc.scalar.activation(gl[:, m * T + c * CH:m * T + (c + 1) * CH], ps[6 + i % 2][:, :], ACT.Gelu,
                                         bias=ab1s[:, m:m + 1]).then_inc(g_ready, 1)
                for n in range(NB):
                    act.wait_ge(z_mm, 3 * NB + n + 1)
                    nc.scalar.activation(xm[:, blk(n)], ps[4 + n % 2][:, 0:P], ACT.Copy).then_inc(ln_out, 1)
                sg.meet()
                act.wait_ge(lg_sub, 1)
                nc.scalar.activation(gt[:, 2, :, :], gt[:, 1, :, :], ACT.Exp).then_inc(lg_exp, 1)
                act.wait_ge(st_mm, 1)
                nc.scalar.activation(selt[:, 0:CH], ps[1][0:E, :], ACT.Copy)
                nc.scalar.activation(selt[:, CH:T], ps[2][0:E, :], ACT.Copy).then_inc(st_copied, 1)
                for e in range(E):
                    for c in range(NC):
                        for m in range(EH // P):
                            i = (e * NC + c) * (EH // P) + m
                            act.wait_ge(e_mm, i + 1)
                            if i >= EH // P:
                                act.wait_ge(ey_mm, BPC * (i // (EH // P)))
                            nc.scalar.activation(eh[:, m * CH:(m + 1) * CH], ps[4 + i % 4][:, :], ACT.Relu,
                                                 bias=mb1s[:, e, m:m + 1]).then_inc(e_relu, 1)
                sg.meet()
                end_round(act, b * ROUNDS + 1 + L)

        @block.vector
        def _(dve):
            ch = Link(dve, dve_own)
            sg = Stages(dve)
            dve.wait_ge(const_in, 16 * 21)
            for k in range(KC):
                nc.vector.tensor_scalar(diag[:, k, :], idf[:, :], cw[:, k:k + 1], None, ALU.mult)
            dve.drain().then_inc(setup, 1)
            dve.wait_ge(setup, 5)

            def stats(j, src, wait=True):
                if wait:
                    dve.wait_ge(y_mm, j + 1)
                ch.link(nc.vector.bn_stats(stt_[:, j % 4, :], src))
                nc.vector.bn_aggr(mv[:, j % 4, :], stt_[:, j % 4, :]).then_inc(y_stats, 1)

            def normed(j, src, dst):
                dve.wait_ge(y_rstd, j + 1)
                return nc.vector.tensor_scalar(dst, src, mv[:, j % 4, 0:1], rstd[:, j % 4:j % 4 + 1],
                                               ALU.subtract, ALU.mult)

            def heads(t):
                return t.rearrange("p (h d) -> p h d", d=DH)

            with dve.Fori(0, B) as b:
                ch.restart()
                dve.wait_ge(ids_in, 16)
                nc.vector.tensor_scalar(oneh, idsi, colc[:, 0:1], None, ALU.is_equal).then_inc(onehot_ready, 1)
                dve.wait_ge(pad_in, 16)
                ch.link(nc.vector.tensor_copy(padw[0], padu[:, :].bitcast(U8)))
                ch.link(nc.vector.tensor_copy(padw[1], padw[0]))
                ch.link(nc.vector.memset(padw[0][:, 0:1], 1.0))
                for i in range(4):
                    ins = nc.vector.tensor_scalar(kbrow[:, i, :], padw[i // 2], (KB_HI, KB_LO)[i % 2], None, ALU.mult)
                ch.link(ins)
                dve.drain().then_inc(padf_ready, 1)
                end_round(dve, b * ROUNDS)

                with dve.Fori(0, L) as l:
                    ch.restart()
                    sg.restart()
                    nc.vector.tensor_scalar(wqa[:, 0:D], wqa[:, 0:D], 0.25, None, ALU.mult)
                    nc.vector.tensor_scalar(wqb[0:DHI + 1, 0:D], wqb[0:DHI + 1, 0:D], 0.25, None,
                                            ALU.mult).then_inc(glob_ready, 1)
                    for n in range(NB):
                        r = heads(res[:, n % 2, :])
                        rv = heads(resv[:, n % 2, :])
                        dve.wait_ge(qk_p1, n + 1)
                        nc.vector.tensor_tensor(r, heads(ps[n % 2][:, 0:2 * D]), nat[:, n, :, 0:DH],
                                                ALU.subtract).then_inc(qk_res, 1)
                        dve.wait_ge(v_p1, n + 1)
                        nc.vector.tensor_tensor(rv, heads(ps[2 + n % 2][:, 0:D]), vst[:, n, :, 0:DH],
                                                ALU.subtract).then_inc(v_res, 1)
                        q, k = nat[:, n, 0:H, :], nat[:, n, H:2 * H, :]
                        for t, at in ((q, Q_ROWS[0][1]), (q, Q_ROWS[0][2]), (k, K_ROWS[0][1]), (k, K_ROWS[0][2])):
                            nc.vector.tensor_copy(t[:, :, at:at + DH], t[:, :, 0:DH])
                        dve.wait_ge(qk_p2, n + 1)
                        for t, rows, rr in ((q, Q_ROWS, r[:, 0:H, :]), (k, K_ROWS, r[:, H:2 * H, :])):
                            a, c, d = rows[1][0], rows[1][1], rows[2][0]
                            nc.vector.tensor_copy(t[:, :, c:c + DH], t[:, :, a:a + DH])
                            ins = nc.vector.tensor_tensor(t[:, :, d:d + DH], rr, t[:, :, a:a + DH], ALU.subtract)
                        ins.then_inc(nat_ready, 1)
                        dve.wait_ge(v_p2, n + 1)
                        nc.vector.tensor_tensor(vst[:, n, :, 2 * DH:3 * DH], rv, vst[:, n, :, DH:2 * DH], ALU.subtract)
                    for k in range(1, 2 * H, 2):
                        dve.wait_ge(tr_mm, k + 1)
                        nc.vector.tensor_copy(stack[0:NPIECE, k, :], psb[4 + k % 4][0:NPIECE, :]).then_inc(ev_dve, 1)
                    sg.meet()
                    nc.vector.tensor_scalar(k0s[0:K_NAT, :], stack[0:K_NAT, H:2 * H, 0], colc[0:K_NAT, 1:2], None, ALU.mult)
                    nc.vector.tensor_scalar(q0s[0:K_NAT, :, :].rearrange("p a b -> p (a b)")[:, 0:H * H:H + 1],
                                            stack[0:K_NAT, 0:H, 0], colc[0:K_NAT, 1:2], colc[0:K_NAT, 2:3],
                                            ALU.mult, ALU.add).then_inc(glob_ready, 1)
                    dve.wait_ge(v0_mm, 1)
                    for g in range(2):
                        v = ps[6 + g][:, 0:HH * VW].rearrange("p (h w) -> p h w", w=VW)
                        ch.link(nc.vector.tensor_copy(v0t[:, 0, half(g), :], v[:, :, 2 * DH:3 * DH]))
                        ch.link(nc.vector.tensor_tensor(v0t[:, 1, half(g), :], v[:, :, DH:2 * DH],
                                                        v0t[:, 0, half(g), :], ALU.add))
                        ins = nc.vector.tensor_tensor(v0b[:, half(g), :], v[:, :, 0:DH], v0t[:, 1, half(g), :], ALU.add)
                    ins.then_inc(v0_ready, 1)
                    for s in range(-LEAD, U + 14):
                        v = s + LEAD
                        if v < U:
                            n, h = divmod(v, H)
                            w = len(window(n)) * P
                            dve.wait_ge(nat_mm, v + 1)
                            nc.vector.tensor_reduce(nmx[:, n % 3, h:h + 1], ps[v % 2][:, 0:w], AX.X, ALU.max,
                                                    negate=True).then_inc(max_done, 1)
                            if h == H - 1:
                                dve.wait_ge(max_done, v + 1)
                                dve.wait_ge(sg_mm, n + 1)
                                ch.link(nc.vector.scalar_tensor_tensor(nm[:, :], ps[5][:, 0:H], -1.0, nmx[:, n % 3, :],
                                                                       ALU.mult, ALU.min))
                                if n >= 1:
                                    dve.wait_ge(mt_mm, n)
                                ch.link(nc.vector.tensor_copy(mcat[:, 0, :], nm[:, :]))
                                ch.link(nc.vector.tensor_tensor(nmr[:, :], nm[:, :], mcat[:, 0, :], ALU.subtract))
                                ch.link(nc.vector.tensor_copy(mcat[:, 1, :], nmr[:, :]))
                                nc.vector.tensor_tensor(mcat[:, 2, :], nmr[:, :], mcat[:, 1, :], ALU.subtract)
                                nc.vector.tensor_tensor(dg0[:, n % 4, :], ps[5][:, 0:H], nm[:, :],
                                                        ALU.add).then_inc(dg_ready, 1)
                        u = s - 1
                        if 0 <= u < U and u % 4 == 3:
                            dve.wait_ge(p1_ready, u + 1)
                            if u >= 4:
                                dve.wait_ge(pv_mm, u - 3)
                            w = len(window(u // H)) * P
                            nc.vector.tensor_tensor(p2[:, u % 4, 0:w], p32[:, u % 3, 0:w], p1[:, u % 4, 0:w],
                                                    ALU.subtract).then_inc(p2_dve, 1)
                        for g in range(2):
                            n, r = divmod(s - (8 if g == 0 else 14), H)
                            if r == 0 and 0 <= n < NB:
                                k = 2 * n + g
                                pv = ps[6 + g][:, 0:HH * VW].rearrange("p (h w) -> p h w", w=VW)
                                t = pvt[:, g, :, :, :]
                                dve.wait_ge(pv_mm, H * n + HH * (g + 1))
                                dve.wait_ge(pvg_ready, k + 1)
                                nc.vector.tensor_tensor(den[:, g, 0, :], pv[:, :, 3 * DH], eg[:, n % 4, half(g)], ALU.add)
                                ch.link(nc.vector.tensor_tensor(t[:, 1, :, :], pv[:, :, 2 * DH:3 * DH], t[:, 0, :, :], ALU.add))
                                nc.vector.reciprocal(den[:, g, 1, :], den[:, g, 0, :])
                                ch.link(nc.vector.tensor_tensor(t[:, 2, :, :], pv[:, :, DH:2 * DH], t[:, 1, :, :], ALU.add))
                                ch.link(nc.vector.tensor_tensor(t[:, 3, :, :], pv[:, :, 0:DH], t[:, 2, :, :], ALU.add))
                                if n >= 2 and g == 0:
                                    dve.wait_ge(at_mm, n - 1)
                                nc.vector.tensor_tensor(
                                    heads(att[:, n % 2, :])[:, half(g), :], t[:, 3, :, :],
                                    den[:, g, 1, :].unsqueeze(2).to_broadcast([P, HH, DH]), ALU.mult).then_inc(comb, 1)
                    dve.wait_ge(f_mm, 2)
                    nc.vector.tensor_reduce(fst[:, 2:3], ps[0][0:H, :], AX.X, ALU.max, negate=True)
                    ch.link(nc.vector.tensor_reduce(fst[:, 3:4], ps[1][0:H, :], AX.X, ALU.max, negate=True))
                    nc.vector.tensor_tensor(fst[:, 0:1], fst[:, 2:3], fst[:, 3:4], ALU.min).then_inc(f_max, 1)
                    dve.wait_ge(f_exp, 2)
                    ch.link(nc.vector.tensor_tensor(fst[:, 3:4], fst[:, 1:2], fst[:, 2:3], ALU.add))
                    ch.link(nc.vector.reciprocal(fst[:, 3:4], fst[:, 3:4]))
                    nc.vector.tensor_scalar(pfull[:, 1, :], pfull[:, 0, :], fst[:, 3:4], None, ALU.mult).then_inc(f_norm, 1)
                    dve.wait_ge(f1_ready, 1)
                    nc.vector.tensor_tensor(f2[:, :, :], ps[2][:, 0:NB * H].rearrange("p (n h) -> p n h", h=H),
                                            f1[:, :, :], ALU.subtract).then_inc(f2_ready, 1)
                    dve.wait_ge(og_mm, 1)
                    for g in range(2):
                        v = ps[6 + g][0:H, 0:HH * VW].rearrange("p (h w) -> p h w", w=VW)
                        for i in range(3):
                            ins = nc.vector.tensor_tensor(heads(og[:, i, :])[:, half(g), :], v[:, :, i * DH:(i + 1) * DH],
                                                          heads(bm[0:H, :])[:, half(g), :], ALU.mult)
                    ins.then_inc(og_ready, 1)
                    sg.meet()
                    pend = []
                    for kind, i in SEQ_C:
                        if kind == "y":
                            stats(i, ps[i % 4][:, 0:D])
                            pend.append(i)
                        if kind == "z":
                            if i >= 2:
                                dve.wait_ge(z_mm, i - 1)
                            normed(i, ps[i % 4][:, 0:D], zt[:, i % 2, :]).then_inc(z_ready, 1)
                    sg.meet()
                    end_round(dve, b * ROUNDS + 1 + l)

                ch.restart()
                sg.restart()
                for j in range(NB + 1):
                    if j < NB:
                        stats(j, ps[j % 4][:, 0:D])
                    if j >= 1:
                        i = j - 1
                        if i >= 2:
                            dve.wait_ge(z_mm, i - 1)
                        normed(i, ps[i % 4][:, 0:D], zt[:, i % 2, :]).then_inc(z_ready, 1)
                sg.meet()
                ch.link(nc.vector.tensor_scalar(dcol[:, 2:3], dcol[:, 1:2], 1.0, None, ALU.add))
                ch.link(nc.vector.reciprocal(dcol[:, 3:4], dcol[:, 2:3]))
                ch.link(nc.vector.tensor_scalar(dcol[:, 2:3], dcol[:, 3:4], -1.0, 1.0, ALU.mult, ALU.add))
                for n in range(NB):
                    j = NB + 2 * n
                    dve.wait_ge(h0_kept, n + 1)
                    stats(j, ps[n % 4][:, 0:DM], False)
                    ch.link(normed(j, ps[n % 4][:, 0:DM], x1[:, blk(n)]))
                    stats(j + 1, x1[:, blk(n)], False)
                    if n >= 2:
                        dve.wait_ge(z_mm, NB + n - 1)
                    normed(j + 1, x1[:, blk(n)], zt[:, n % 2, 0:DM]).then_inc(z_ready, 1)
                sg.meet()
                ch.link(nc.vector.tensor_scalar(d1, xn[:, 2:2 + T], dcol[:, 2:3], None, ALU.mult))
                nc.vector.tensor_tensor_scan(st, dcol[:, 3:4].to_broadcast([P, T]), d1, 0.0, ALU.mult,
                                             ALU.add).then_inc(s_ready, 1)
                for n in range(NB):
                    j = 3 * NB + n
                    dve.wait_ge(y_mm, 2 * NB + n + 1)
                    ch.link(nc.vector.tensor_tensor(x1[:, blk(n)], ps[n % 4][:, 0:DM], x1[:, blk(n)], ALU.add))
                    stats(j, x1[:, blk(n)], False)
                    if n >= 2:
                        dve.wait_ge(z_mm, 2 * NB + n - 1)
                    normed(j, x1[:, blk(n)], zt[:, n % 2, 0:DM]).then_inc(z_ready, 1)
                sg.meet()
                for n in range(NB):
                    j = 4 * NB + n
                    dve.wait_ge(y_mm, 3 * NB + n + 1)
                    ch.link(nc.vector.tensor_tensor(x1[:, blk(n)], ps[n % 4][:, 0:DM], x1[:, blk(n)], ALU.add))
                    ch.link(nc.vector.tensor_tensor(h0[:, blk(n)], h0[:, blk(n)], x1[:, blk(n)], ALU.add))
                    stats(j, h0[:, blk(n)], False)
                    if n >= 2:
                        dve.wait_ge(z_mm, 3 * NB + n - 1)
                    normed(j, h0[:, blk(n)], zt[:, n % 2, 0:DM]).then_inc(z_ready, 1)
                sg.meet()
                dve.wait_ge(lg_mm, 1)
                ch.link(nc.vector.tensor_copy(gt[:, 0, :, :], ps[0][:, 0:NB * E].rearrange("p (n e) -> p n e", e=E)))
                ch.link(nc.vector.tensor_reduce(gs[:, 0, :], gt[:, 0, :, :], AX.X, ALU.max))
                top = gs[:, 0, :].unsqueeze(2).to_broadcast([P, NB, E])
                nc.vector.tensor_tensor(gt[:, 1, :, :], gt[:, 0, :, :], top, ALU.subtract).then_inc(lg_sub, 1)
                ch.link(nc.vector.tensor_tensor(gt[:, 3, :, :], gt[:, 0, :, :], top, ALU.is_equal))
                for e in range(E):
                    ins = nc.vector.tensor_scalar(gt[:, 4, :, e], gt[:, 3, :, e], float(E - e), None, ALU.mult)
                ch.link(ins)
                ch.link(nc.vector.tensor_reduce(gs[:, 1, :], gt[:, 4, :, :], AX.X, ALU.max))
                nc.vector.tensor_tensor(gt[:, 5, :, :], gt[:, 4, :, :],
                                        gs[:, 1, :].unsqueeze(2).to_broadcast([P, NB, E]), ALU.is_equal).then_inc(sel_ready, 1)
                dve.wait_ge(lg_exp, 1)
                ch.link(nc.vector.tensor_reduce(gs[:, 2, :], gt[:, 2, :, :], AX.X, ALU.add))
                nc.vector.reciprocal(gs[:, 3, :], gs[:, 2, :])
                dve.wait_ge(a0_mm, 1)
                for c in range(NC):
                    nc.vector.tensor_copy(acc[:, c * CH:(c + 1) * CH], ps[1 + c][:, :])
                ch.link(nc.vector.memset(fst[0:1, 0:1], 0.0))
                nc.vector.memset(fst[0:1, 1:2], 0.0).then_inc(acc_done, 1)
                for i in range(E * NB):
                    e, n = divmod(i, NB)
                    dve.wait_ge(ey_mm, i + 1)
                    if e:
                        dve.wait_ge(acc_done, i - NB + 2)
                    nc.vector.scalar_tensor_tensor(acc[:, blk(n)], ps[i % 4][:, 0:DM], gt[:, 5, n, e:e + 1],
                                                   acc[:, blk(n)], ALU.mult, ALU.add).then_inc(acc_done, 1)
                for n in range(NB):
                    dve.wait_ge(acc_done, E * NB - NB + n + 2)
                    nc.vector.scalar_tensor_tensor(acc[:, blk(n)], acc[:, blk(n)], gs[:, 3, n:n + 1], h0[:, blk(n)],
                                                   ALU.mult, ALU.add).then_inc(o_ready, 1)
                sg.meet()
                end_round(dve, b * ROUNDS + 1 + L)

        @block.tensor
        def _(pe):
            sg = Stages(pe)
            mm = nc.tensor.matmul
            pe.wait_ge(const_in, 16 * 21)
            pe.drain().then_inc(setup, 1)
            pe.wait_ge(setup, 5)

            def ln_transpose(j, zc, width):
                pe.wait_ge(z_ready, zc + 1)
                if zc >= 2:
                    pe.wait_ge(ln_out, zc - 1)
                bank = ps[4 + zc % 2]
                ins = nc.tensor.transpose(bank[:, 0:P], zt[:, zc % 2, 0:P], idf[:, :])
                if width > P:
                    ins = nc.tensor.transpose(bank[0:width - P, P:2 * P], zt[:, zc % 2, P:width], idf[:, :])
                ins.then_inc(z_mm, 1)

            with pe.Fori(0, B) as b:
                pe.wait_ge(onehot_ready, 1)
                for c in range(NC):
                    mm(ps[2 * c][:, :], embs[:, 0:DLO], oneh[:, c * CH:(c + 1) * CH], start=True, stop=True)
                    mm(ps[2 * c + 1][0:DHI, :], embs[:, DLO:D], oneh[:, c * CH:(c + 1) * CH], start=True,
                       stop=True).then_inc(emb_mm, 1)
                end_round(pe, b * ROUNDS)

                with pe.Fori(0, L) as l:
                    sg.restart()
                    pe.wait_ge(glob_ready, 1)
                    for n in range(NB):
                        if n >= 2:
                            pe.wait_ge(qk_res, n - 1)
                            pe.wait_ge(v_res, n - 1)
                        mm(ps[n % 2][:, 0:2 * D], xa[:, blk(n)], wqa[:, 0:2 * D], start=True, stop=False)
                        mm(ps[n % 2][:, 0:2 * D], xb[0:DHI + 1, blk(n)], wqb[0:DHI + 1, 0:2 * D], start=False,
                           stop=True).then_inc(qk_mm, 1)
                        mm(ps[2 + n % 2][:, 0:D], xa[:, blk(n)], wqa[:, 2 * D:3 * D], start=True, stop=False)
                        mm(ps[2 + n % 2][:, 0:D], xb[0:DHI + 1, blk(n)], wqb[0:DHI + 1, 2 * D:3 * D], start=False,
                           stop=True).then_inc(v_mm, 1)
                    pe.wait_ge(nat_ready, NB)
                    for k in range(2 * H):
                        if k >= 4:
                            pe.wait_ge(ev_dve if k % 2 else ev_act, (k - 4) // 2 + 1)
                        for n in range(NB):
                            ins = nc.tensor.transpose(psb[4 + k % 4][0:NPIECE, blk(n)], nat[:, n, k, :], idb[:, :])
                        ins.then_inc(tr_mm, 1)
                    sg.meet()
                    for g in range(2):
                        ins = mm(ps[6 + g][:, 0:HH * VW], onesb[0:1, :], vst[0:1, 0, half(g), :], start=True, stop=True)
                    ins.then_inc(v0_mm, 1)
                    pe.wait_ge(glob_ready, 2)
                    for s in range(-LEAD, U + 14):
                        v = s + LEAD
                        if v < U:
                            n, h = divmod(v, H)
                            win = window(n)
                            if v >= 2:
                                pe.wait_ge(max_done, v - 1)
                            s_ps = ps[v % 2]
                            q = stack[0:K_NAT, h, blk(n)]
                            edges = [(i, m) for i, m in enumerate(win) if m != n]
                            mm(s_ps[:, 0:len(win) * P], q, stack[0:K_NAT, H + h, blk(win[0], len(win))], start=True,
                               stop=False)
                            for i, m in edges:
                                ins = mm(s_ps[:, blk(i)], idb[:, :], bandb[:, 0 if m < n else 1, :], start=False,
                                         stop=(i, m) == edges[-1])
                            ins.then_inc(nat_mm, 1)
                            if h == H - 1:
                                if n >= 3:
                                    pe.wait_ge(at_copied, n - 2)
                                elif n >= 1:
                                    pe.wait_ge(mt_copied, n)
                                for g in range(H):
                                    ins = mm(ps[5][:, g:g + 1], stack[0:K_NAT, g, blk(n)], k0s[0:K_NAT, g:g + 1],
                                             start=True, stop=True)
                                ins.then_inc(sg_mm, 1)
                        for n in range(NB):
                            if s == H * n - 6:
                                pe.wait_ge(dg_ready, n + 1)
                                nc.tensor.transpose(psb[5][0:3 * H, 64:64 + P],
                                                    mcat[:, :, :].rearrange("p i h -> p (i h)"), idb[:, :]).then_inc(mt_mm, 1)
                            if s == H * (n + 1) + 8:
                                if n + 2 < NB:
                                    pe.wait_ge(mt_copied, n + 3)
                                elif n >= 1:
                                    pe.wait_ge(at_copied, n)
                                pe.wait_ge(comb, 2 * n + 2)
                                nc.tensor.transpose(ps[5][:, P:2 * P], att[:, n % 2, 0:DLO], idf[:, :])
                                nc.tensor.transpose(ps[5][0:DHI, 2 * P:3 * P], att[:, n % 2, DLO:D],
                                                    idf[:, :]).then_inc(at_mm, 1)
                        if 0 <= s < U:
                            n, h = divmod(s, H)
                            if h == 0:
                                pe.wait_ge(m_in[n % 2], 48 * (n // 2 + 1))
                            if s >= 3:
                                pe.wait_ge(p1_ready, s - 2)
                            win = window(n)
                            for i, m in enumerate(win):
                                ins = mm(ps[2 + s % 3][:, blk(i)], stack[0:K_ALL, H + h, blk(m)],
                                         stack[0:K_ALL, h, blk(n)], start=True, stop=m == n)
                                if m != n:
                                    ins = mm(ps[2 + s % 3][:, blk(i)], idb[:, :], bandb[:, 1 if m < n else 0, :],
                                             start=False, stop=True)
                            ins.then_inc(t_mm, 1)
                        w = s - PV_LAG
                        if 0 <= w < U:
                            n, h = divmod(w, H)
                            g, i = divmod(h, HH)
                            if w == 0:
                                pe.wait_ge(v0_ready, 1)
                            if i == 0 and n >= 1:
                                pe.wait_ge(comb, 2 * (n - 1) + g + 1)
                            if w % 4 == 3:
                                pe.wait_ge(p2_dve, w // 4 + 1)
                            else:
                                pe.wait_ge(p2_pool, w - w // 4 + (0 if w % 4 == 3 else 1))
                            win = window(n)
                            out_ps = ps[6 + g][:, i * VW:(i + 1) * VW]
                            for a, m in enumerate(win):
                                for pt in (p1, p2):
                                    ins = mm(out_ps, pt[:, w % 4, blk(a)], vst[:, m, h, :],
                                             start=a == 0 and pt is p1, stop=a == len(win) - 1 and pt is p2)
                            ins.then_inc(pv_mm, 1)
                    for c in range(NC):
                        for h in range(H):
                            ins = mm(ps[c][0:H, :], q0s[0:K_NAT, h, :], stack[0:K_NAT, H + h, c * CH:(c + 1) * CH],
                                     start=h == 0, stop=h == H - 1)
                        ins.then_inc(f_mm, 1)
                    pe.wait_ge(f_norm, 1)
                    for n in range(NB):
                        ins = nc.tensor.transpose(ps[2][:, n * H:(n + 1) * H], pfull[:, 1, blk(n)], idf[0:H, 0:H])
                    ins.then_inc(ft_mm, 1)
                    pe.wait_ge(f2_ready, 1)
                    for g in range(2):
                        for n in range(NB):
                            for ft in (f1, f2):
                                ins = mm(ps[6 + g][0:H, 0:HH * VW], ft[:, n, :], vst[:, n, half(g), :],
                                         start=n == 0 and ft is f1, stop=n == NB - 1 and ft is f2)
                    ins.then_inc(og_mm, 1)
                    pe.wait_ge(og_ready, 1)
                    for i in range(3):
                        mm(ps[3][:, 0:1], og[:, i, 0:DLO], ones[0:H, 0:1], start=i == 0, stop=i == 2)
                    for i in range(3):
                        ins = mm(ps[3][0:DHI, 8:9], og[:, i, DLO:D], ones[0:H, 0:1], start=i == 0, stop=i == 2)
                    ins.then_inc(oc_mm, 1)
                    sg.meet()
                    for kind, i in SEQ_C:
                        if kind == "y":
                            n = i % NB
                            if i >= 4:
                                pe.wait_ge(z_ready, i - 3)
                            y = ps[i % 4][:, 0:D]
                            if i < NB:
                                mm(y, ata[:, blk(n)], woa[:, :], start=True, stop=False)
                                mm(y, atb[0:DHI + 1, blk(n)], wob[0:DHI + 1, :], start=False, stop=False)
                                mm(ps[i % 4][:, 0:P], xa[:, blk(n)], idf[:, :], start=False, stop=False)
                                mm(ps[i % 4][:, P:D], xb[0:DHI, blk(n)], idf[0:DHI, 0:DHI], start=False,
                                   stop=True).then_inc(y_mm, 1)
                            else:
                                c = n // BPC
                                pe.wait_ge(h_relu, (c + 1) * (FF // P))
                                mm(y, xb[0:DHI + 1, blk(n)], rwb[0:DHI + 1, :], start=True, stop=False)
                                mm(ps[i % 4][:, 0:P], xa[:, blk(n)], idf[:, :], start=False, stop=False)
                                for m in range(FF // P):
                                    ins = mm(y, hid[:, m, blk(n % BPC)], w2s[:, m, :], start=False, stop=m == FF // P - 1)
                                ins.then_inc(y_mm, 1)
                        if kind == "tr":
                            ln_transpose(i, i, D)
                        if kind == "hid":
                            c, m = divmod(i, FF // P)
                            pe.wait_ge(ln_out, (c + 1) * BPC)
                            if i >= 2:
                                pe.wait_ge(h_relu, i - 1)
                            cs = slice(c * CH, (c + 1) * CH)
                            mm(ps[6 + i % 2][:, :], w1a[:, m * P:(m + 1) * P], xa[:, cs], start=True, stop=False)
                            mm(ps[6 + i % 2][:, :], w1b[0:DHI + 1, m * P:(m + 1) * P], xb[0:DHI + 1, cs], start=False,
                               stop=True).then_inc(h_mm, 1)
                    sg.meet()
                    end_round(pe, b * ROUNDS + 1 + l)

                sg.restart()
                for n in range(NB + 2):
                    if n < NB:
                        if n >= 4:
                            pe.wait_ge(z_ready, n - 3)
                        mm(ps[n % 4][:, 0:P], xa[:, blk(n)], idf[:, :], start=True, stop=True)
                        mm(ps[n % 4][:, P:D], xb[0:DHI, blk(n)], idf[0:DHI, 0:DHI], start=True, stop=True).then_inc(y_mm, 1)
                    if n >= 2:
                        ln_transpose(n - 2, n - 2, D)
                sg.meet()
                for n in range(NB + 2):
                    if n < NB:
                        if n >= 4:
                            pe.wait_ge(z_ready, NB + n - 3)
                            pe.wait_ge(h0_kept, n - 3)
                        mm(ps[n % 4][:, 0:DM], xa[:, blk(n)], wca[:, :], start=True, stop=False)
                        mm(ps[n % 4][:, 0:DM], xb[0:DHI + 1, blk(n)], wcb[0:DHI + 1, :], start=False,
                           stop=True).then_inc(y_mm, 1)
                    if n >= 2:
                        ln_transpose(0, NB + n - 2, DM)
                sg.meet()
                pe.wait_ge(s_ready, 1)
                for n in range(NB + 2):
                    if n < NB:
                        if n >= 4:
                            pe.wait_ge(z_ready, 2 * NB + n - 3)
                        y = ps[n % 4][:, 0:DM]
                        for k in range(KC):
                            mm(y, xn[:, n * P + k:(n + 1) * P + k], diag[:, k, :], start=k == 0, stop=False)
                        mm(y, st[:, blk(n)], wos[:, :], start=False, stop=False)
                        mm(y, ones[0:2, :], bo2s[:, :], start=False, stop=True).then_inc(y_mm, 1)
                    if n >= 2:
                        ln_transpose(0, 2 * NB + n - 2, DM)
                sg.meet()
                for i in range(NC * 2):
                    c, m = divmod(i, 2)
                    if i >= 2:
                        pe.wait_ge(g_ready, i - 1)
                    mm(ps[6 + i % 2][:, :], aw1s[:, m * P:(m + 1) * P], ht[:, c * CH:(c + 1) * CH], start=True,
                       stop=True).then_inc(g_mm, 1)
                pe.wait_ge(g_ready, 2 * NC)
                for n in range(NB + 2):
                    if n < NB:
                        if n >= 4:
                            pe.wait_ge(z_ready, 3 * NB + n - 3)
                        y = ps[n % 4][:, 0:DM]
                        for m in range(2):
                            mm(y, gl[:, m * T + n * P:m * T + (n + 1) * P], aw2s[:, m, :], start=m == 0, stop=False)
                        mm(y, ones[0:1, :], ab2s[:, :], start=False, stop=True).then_inc(y_mm, 1)
                    if n >= 2:
                        ln_transpose(0, 3 * NB + n - 2, DM)
                sg.meet()
                for n in range(NB):
                    mm(ps[0][:, n * E:(n + 1) * E], xm[:, blk(n)], wgs[:, :], start=True, stop=False)
                    ins = mm(ps[0][:, n * E:(n + 1) * E], ones[0:1, :], bgs[:, :], start=False, stop=True)
                ins.then_inc(lg_mm, 1)
                pe.wait_ge(sel_ready, 1)
                for n in range(NB):
                    ins = nc.tensor.transpose(ps[1 + n // BPC][0:E, blk(n % BPC)], gt[:, 5, n, :], idf[:, :])
                ins.then_inc(st_mm, 1)
                pe.wait_ge(st_copied, 1)
                for n in range(NB):
                    ins = mm(ps[1 + n // BPC][:, blk(n % BPC)], selt[:, blk(n)], mb2s[:, :], start=True, stop=True)
                ins.then_inc(a0_mm, 1)
                pe.wait_ge(mw_in, 32)
                for e in range(E):
                    for c in range(NC):
                        for m in range(EH // P):
                            i = (e * NC + c) * (EH // P) + m
                            if i >= 4:
                                pe.wait_ge(e_relu, i - 3)
                            mm(ps[4 + i % 4][:, :], mw1s[:, e, m * P:(m + 1) * P], xm[:, c * CH:(c + 1) * CH],
                               start=True, stop=True).then_inc(e_mm, 1)
                        pe.wait_ge(e_relu, (e * NC + c + 1) * (EH // P))
                        for n in range(BPC):
                            i = e * NB + c * BPC + n
                            pe.wait_ge(acc_done, max(1, i - 2))
                            for m in range(EH // P):
                                ins = mm(ps[i % 4][:, 0:DM], eh[:, m * CH + n * P:m * CH + (n + 1) * P],
                                         mw2s[:, e, m, :], start=m == 0, stop=m == EH // P - 1)
                            ins.then_inc(ey_mm, 1)
                sg.meet()
                end_round(pe, b * ROUNDS + 1 + L)


def _seq_c():
    seq = []

    def y(i):
        seq.append(("y", i))
        if i >= 1:
            seq.append(("z", i - 1))

    for i in range(4):
        y(i)
    for i in range(4):
        seq.append(("tr", i) if i < 3 else ("z", 3))
        if i < 3:
            y(4 + i)
    seq = [s for k, s in enumerate(seq) if s not in seq[:k]]
    seq.append(("tr", 3))
    y(7)
    seq.append(("z", 7))
    seq += [("hid", m) for m in range(3)] + [("tr", 4), ("tr", 5)] + [("hid", m) for m in range(3, 6)]
    seq += [("tr", 6), ("tr", 7)]
    seq += [("y", 8), ("y", 9), ("z", 8), ("y", 10), ("z", 9), ("y", 11), ("z", 10), ("z", 11)]
    seq += [("hid", m) for m in range(6, 9)] + [("tr", 8), ("tr", 9)] + [("hid", m) for m in range(9, 12)]
    seq += [("tr", 10), ("tr", 11)]
    seq += [("y", 12), ("y", 13), ("z", 12), ("y", 14), ("z", 13), ("tr", 12), ("y", 15), ("z", 14), ("tr", 13),
            ("z", 15), ("tr", 14), ("tr", 15)]
    return seq


SEQ_C = _seq_c()


_OUTS = [((2, 1024, 128), 'float32')]


def kernel(**inputs):
    import numpy as _np
    import concourse.bacc as _bacc
    from concourse import mybir as _mybir
    from concourse.bass_utils import run_bass_kernel_spmd as _run

    g = {k: _np.asarray(v) for k, v in inputs.items()}
    t = "L0_tok_"
    a = "L0_attn_"
    f = "L0_ffn_"

    def cat(ws, bs):
        w = _np.concatenate([_np.transpose(g[t + n], (0, 2, 1)) for n in ws], axis=2)
        r = _np.concatenate([g[t + n][:, None, :] for n in bs], axis=2)
        return _np.concatenate([w, r], axis=1)

    def row(v):
        return v.reshape(1, -1)

    def columns(*vs):
        return _np.stack(vs, axis=-1)

    p, q = _np.arange(P)[:, None], _np.arange(P)[None, :]
    low = _np.where(q < p, BAND_OUT, 0.0).astype(_np.float32)
    high = _np.where(q > p, BAND_OUT, 0.0).astype(_np.float32)
    cols = _np.zeros((P, 4), _np.float32)
    cols[:, 0] = _np.arange(P)
    cols[0:NPIECE, 1] = 1.0
    cols[R_FULL:R_MAX, 2] = 1.0
    cols[:, 3] = -0.5
    eye = _np.eye(D, dtype=_np.float32)
    arrays = {
        "x": g["x"], "pad": g["mask_BS_b0_1"].view(_np.int32), "emb": g[t + "emb"],
        "wqkv": cat(["Wq", "Wk", "Wv"], ["bq", "bk", "bv"]), "wo": cat(["Wo"], ["bo"]), "w1": cat(["W1"], ["b1"]),
        "w2": _np.transpose(g[t + "W2"], (0, 2, 1)),
        "rw": _np.stack([_np.concatenate([eye, g[t + "b2"][l][None, :]]) for l in range(L)]),
        "lnl": columns(*(g[t + n] for n in ("g1", "beta1", "g2", "beta2"))),
        "lnf": columns(g[t + "gf"], g[t + "betaf"]),
        "wc": _np.concatenate([g[t + "Wc"].T, row(g[t + "bc"])]),
        "ident": _np.eye(P, dtype=_np.float32), "band": _np.stack([low, high], axis=1), "cols": cols,
        "decay": g[a + "decay_logit"].reshape(-1, 1), "convw": g[a + "conv_w"].reshape(DM, KC),
        "wout": g[a + "W_out"].T, "bo2": _np.stack([g[a + "b_out"], g[a + "conv_b"]]),
        "ln12": columns(*(g[a + n] for n in ("ln1_g", "ln1_b", "ln2_g", "ln2_b"))),
        "aw1": g[a + "W1"].T, "ab1": g[a + "b1"].reshape(2, P).T,
        "aw2": g[a + "W2"].T.reshape(2, P, DM).transpose(1, 0, 2), "ab2": row(g[a + "b2"]),
        "wg": g[f + "Wg"], "bg": row(g[f + "bg"]),
        "mw1": g[f + "W1"].transpose(1, 0, 2), "mb1": g[f + "b1"].reshape(E, EH // P, P).transpose(2, 0, 1),
        "mw2": g[f + "W2"].reshape(E, EH // P, P, DM).transpose(2, 0, 1, 3), "mb2": g[f + "b2"],
    }
    nc = _bacc.Bacc("TRN2", target_bir_lowering=False, num_devices=1)
    held, args = {}, []
    for name, v in arrays.items():
        v = _np.ascontiguousarray(v)
        held[f"in_{name}"] = v
        args.append(nc.dram_tensor(f"in_{name}", v.shape, _mybir.dt.from_np(v.dtype), kind="ExternalInput").ap())
    for i, (shape, dtype) in enumerate(_OUTS):
        args.append(nc.dram_tensor(f"out_{i}", shape, _mybir.dt.from_np(_np.dtype(dtype)), kind="ExternalOutput").ap())
    program(nc, *args)
    r = _run(nc, [held], core_ids=[0])
    return r.results[0]["out_0"]
```

```python
from contextlib import ExitStack

import numpy as np

import concourse.bass as bass
from concourse import mybir

ALU = mybir.AluOpType
ACT = mybir.ActivationFunctionType
AX = mybir.AxisListType
F32 = mybir.dt.float32
BF16 = mybir.dt.bfloat16
F16 = mybir.dt.float16
F32R = mybir.dt.float32r
I32 = mybir.dt.int32
U8 = mybir.dt.uint8

P = 128
B, T = 2, 1024
NB = T // P
CH = 512
NC = T // CH
BPC = CH // P
L, D, H, FF = 2, 192, 12, 768
DH = D // H
DLO, DHI = P, D - P
DM = 128
HID = 256
KC = 5
E, EH = 8, 512
EPS = 1e-5
BAND_OUT = -1e9
KB_HI, KB_LO = -9984.0, -16.0

Q_ROWS = ((0, 16, 32), (48, 64), (80,))
K_ROWS = ((0, 48, 80), (16, 64), (32,))
NPIECE = 96
R_BIAS = 96
R_FULL = 98
R_MAX = 100
K_NAT = 100
K_ALL = 103
VW = 3 * DH + 1
HH = H // 2
LEAD = 20
PV_LAG = 4
PARTS = ((0, 0), (0, 1), (1, 0))
RING = 6
U = NB * H


def window(n):
    return [m for m in (n - 1, n, n + 1) if 0 <= m < NB]


def program(nc, x, pad, emb, wqkv, wo, w1, w2, rw, lnl, lnf, wc, ident, band, cols, decay, convw, wout, bo2,
            ln12, aw1, ab1, aw2, ab2, wg, bg, mw1, mb1, mw2, mb2, qrows, krows, out):
    with ExitStack() as ctx:
        def sb(name, shape, dt):
            return ctx.enter_context(nc.sbuf_tensor(name, shape, dt))

        work_sems = []

        def sem(name, work=True):
            s = ctx.enter_context(nc.semaphore(name))
            if work:
                work_sems.append(s)
            return s

        ps = [ctx.enter_context(nc.psum_tensor(f"bank{i}", [P, CH], F32)) for i in range(8)]
        psb = [p[:, :].bitcast(BF16) for p in ps]

        vst = sb("vst", [P, NB, H, VW], BF16)
        xa = sb("xa", [P, T], F32)
        xb = sb("xb", [P, T], F32)
        ata = sb("ata", [P, T], F32)
        atb = sb("atb", [P, T], F32)
        wqa = sb("wqa", [P, 3 * D], F32)
        wqb = sb("wqb", [P, 3 * D], F32)
        woa = sb("woa", [P, D], F32)
        wob = sb("wob", [P, D], F32)
        w1a = sb("w1a", [P, FF], F32)
        w1b = sb("w1b", [P, FF], F32)
        w2s = sb("w2s", [P, FF // P, D], F32)
        rwb = sb("rwb", [P, D], F32)
        lna = sb("lna", [P, 4], F32)
        lnb = sb("lnb", [P, 4], F32)
        lfa = sb("lfa", [P, 2], F32)
        lfb = sb("lfb", [P, 2], F32)
        wca = sb("wca", [P, DM], F32)
        wcb = sb("wcb", [P, DM], F32)
        embs = sb("embs", [P, D], F32)
        idf = sb("idf", [P, P], F32)
        idb = sb("idb", [P, P], BF16)
        bandf = sb("bandf", [P, 2, P], F32)
        bandb = sb("bandb", [P, 2, P], BF16)
        colc = sb("colc", [P, 4], F32)
        bm = sb("bm", [P, D], F32)
        ones = sb("ones", [P, P], F32)
        onesb = sb("onesb", [P, P], BF16)
        epst = sb("epst", [P, 1], F32)
        kbrow = sb("kbrow", [1, 4, T], BF16)
        padu = sb("padu", [1, T // 4], I32)
        res = sb("res", [P, 2, 2 * D], F32)
        resv = sb("resv", [P, 2, D], F32)
        k0s = sb("k0s", [P, H], BF16)
        q0s = sb("q0s", [P, H, H], BF16)
        v0b = sb("v0b", [P, H, DH], F32)
        v0t = sb("v0t", [P, 2, H, DH], F32)
        nmx = sb("nmx", [P, 3, H], F32)
        nm = sb("nm", [P, H], F32)
        nmr = sb("nmr", [P, H], F32)
        mcat = sb("mcat", [P, 3, H], BF16)
        mtr = sb("mtr", [3 * H, 2, P], BF16)
        dg0 = sb("dg0", [P, 4, H], F32)
        eg = sb("eg", [P, 4, H], F32)
        pvt = sb("pvt", [P, 2, 4, HH, DH], F32)
        den = sb("den", [P, 2, 2, HH], F32)
        att = sb("att", [P, 2, D], F32)
        fst = sb("fst", [H, 4], F32)
        f1 = sb("f1", [P, NB, H], F16)
        f2 = sb("f2", [P, NB, H], F16)
        og = sb("og", [H, 3, D], F32)
        stt_ = sb("bnst", [P, 4, 6], F32)
        mv = sb("mv", [P, 4, 2], F32)
        ve = sb("ve", [P, 4], F32)
        rstd = sb("rstd", [P, 4], F32)
        zt = sb("zt", [P, 2, D], F32)
        dcol = sb("dcol", [P, 4], F32)
        cw = sb("cw", [P, KC], F32)
        diag = sb("diag", [P, KC, DM], F32)
        wos = sb("wos", [P, DM], F32)
        bo2s = sb("bo2s", [2, DM], F32)
        l12 = sb("l12", [P, 4], F32)
        aw1s = sb("aw1s", [P, HID], F32)
        ab1s = sb("ab1s", [P, 2], F32)
        aw2s = sb("aw2s", [P, 2, DM], F32)
        ab2s = sb("ab2s", [1, DM], F32)
        wgs = sb("wgs", [P, E], F32)
        bgs = sb("bgs", [1, E], F32)
        mb1s = sb("mb1s", [P, E, EH // P], F32)
        mb2s = sb("mb2s", [P, E], F32)
        rowe = sb("rowe", [E, E, P], BF16)
        gt = sb("gt", [P, 6, NB, E], F32)
        gs = sb("gs", [P, 4, NB], F32)
        selt = sb("selt", [E, T], BF16)

        xn = sb("xn", [P, T + KC - 1], F32)

        with ExitStack() as layers:
            def lsb(name, shape, dt):
                return layers.enter_context(nc.sbuf_tensor(name, shape, dt))

            stack = lsb("stack", [P, 2 * H, T], BF16)
            nat = lsb("nat", [P, NB, 2 * H, NPIECE], BF16)
            p32 = lsb("p32", [P, RING, 3 * P], F32)
            p1 = lsb("p1", [P, RING, 3 * P], F16)
            p2 = lsb("p2", [P, RING, 3 * P], F16)
            hid = lsb("hid", [P, FF // P, CH], F32)
        h0 = sb("h0", [P, T], F32)
        xm = sb("xm", [P, T], F32)
        acc = sb("acc", [P, T], F32)
        mw1s = sb("mw1s", [P, E, EH], F32)
        mw2s = sb("mw2s", [P, E, EH // P, DM], F32)
        w1r = sb("w1r", [P, 2, 2, EH], F32R)
        w2r = sb("w2r", [P, 2, 2, EH // P, DM], F32R)
        with ExitStack() as retention:
            def rsb(name, width):
                return retention.enter_context(nc.sbuf_tensor(name, [P, width], F32))[:, :]

            x1 = rsb("x1", T)
            st = rsb("st", T)
            d1 = rsb("d1", T)
            gl = rsb("gl", 2 * T)
            ht = rsb("ht", T)
        ehr = sb("ehr", [P, 2, 2, EH // P, CH], F32R)
        xmr = sb("xmr", [P, 2, T], F32R)
        eh32 = sb("eh32", [P, 4, CH], F32)
        ey = sb("ey", [P, 2, CH], F32)
        mask = sb("mask", [P, 2, CH], BF16)
        idsi = hid[:, 0:2, :].rearrange("p a b -> p (a b)").bitcast(I32)
        oneh = hid[:, 2:4, :].rearrange("p a b -> p (a b)")
        pfull = hid[0:H, 0:4, :].rearrange("p (i a) b -> p i (a b)", i=2)
        padw = (ata[0:1, :], atb[0:1, :])

        arrive = sem("arrive", False)
        go = sem("go", False)
        spare = sem("spare", False)
        const_in = sem("const_in", False)
        setup = sem("setup", False)
        stage = sem("stage")
        ids_in = sem("ids_in")
        pad_in = sem("pad_in")
        kb_out = sem("kb_out")
        rows_in = sem("rows_in")
        onehot_ready = sem("onehot_ready")
        padf_ready = sem("padf_ready")
        emb_mm = sem("emb_mm")
        emb_cp = sem("emb_cp")
        dve_own = sem("dve_own")
        act_own = sem("act_own")
        pool_own = sem("pool_own")
        wqkv_in = sem("wqkv_in")
        wrest_in = sem("wrest_in")
        qk_mm = sem("qk_mm")
        v_mm = sem("v_mm")
        qk_p1 = sem("qk_p1")
        qk_res = sem("qk_res")
        qk_p2 = sem("qk_p2")
        v_p1 = sem("v_p1")
        v_res = sem("v_res")
        v_p2 = sem("v_p2")
        nat_ready = sem("nat_ready")
        tr_mm = sem("tr_mm")
        ev_act = sem("ev_act")
        ev_dve = sem("ev_dve")
        glob_ready = sem("glob_ready")
        v0_mm = sem("v0_mm")
        v0_ready = sem("v0_ready")
        nat_mm = sem("nat_mm")
        max_done = sem("max_done")
        sg_mm = sem("sg_mm")
        m_ready = sem("m_ready")
        mt_mm = sem("mt_mm")
        mt_copied = sem("mt_copied")
        m_in = [sem(f"m_in{i}") for i in range(2)]
        dg_ready = sem("dg_ready")
        eg_ready = sem("eg_ready")
        t_mm = sem("t_mm")
        p32_ready = sem("p32_ready")
        p1_ready = sem("p1_ready")
        p2_pool = sem("p2_pool")
        p2_dve = sem("p2_dve")
        pv_mm = sem("pv_mm")
        pvg_ready = sem("pvg_ready")
        comb = sem("comb")
        at_mm = sem("at_mm")
        at_copied = sem("at_copied")
        f_mm = sem("f_mm")
        f_max = sem("f_max")
        f_exp = sem("f_exp")
        f_norm = sem("f_norm")
        ft_mm = sem("ft_mm")
        f1_ready = sem("f1_ready")
        f2_ready = sem("f2_ready")
        og_mm = sem("og_mm")
        og_ready = sem("og_ready")
        oc_mm = sem("oc_mm")
        oc_copied = sem("oc_copied")
        y_mm = sem("y_mm")
        y_stats = sem("y_stats")
        y_rstd = sem("y_rstd")
        z_ready = sem("z_ready")
        z_mm = sem("z_mm")
        ln_out = sem("ln_out")
        h_mm = sem("h_mm")
        h_relu = sem("h_relu")
        h0_kept = sem("h0_kept")
        s_ready = sem("s_ready")
        g_mm = sem("g_mm")
        g_ready = sem("g_ready")
        lg_mm = sem("lg_mm")
        lg_sub = sem("lg_sub")
        lg_exp = sem("lg_exp")
        sel_ready = sem("sel_ready")
        st_mm = sem("st_mm")
        st_copied = sem("st_copied")
        ey_masked = sem("ey_masked")
        mask_mm = sem("mask_mm")
        mask_copied = sem("mask_copied")
        o_mm = sem("o_mm")
        e_mm = sem("e_mm")
        e_relu = sem("e_relu")
        e_split = sem("e_split")
        w_split = sem("w_split")
        x_hi = sem("x_hi")
        x_lo = sem("x_lo")
        ey_mm = sem("ey_mm")
        acc_done = sem("acc_done")
        o_ready = sem("o_ready")
        o_out = sem("o_out")
        mw_in = sem("mw_in")

        first, last = min(s.num for s in work_sems), max(s.num for s in work_sems)
        assert last - first + 1 == len(work_sems)
        ROUNDS = 1 + L + 1

        class Link:

            def __init__(self, eng, own):
                self.eng, self.own, self.count = eng, own, 0

            def link(self, ins):
                self.count += 1
                ins.then_inc(self.own, 1)
                self.eng.wait_ge(self.own, self.count)

            def restart(self):
                self.count = 0

        class Stages:

            def __init__(self, eng):
                self.eng, self.count = eng, 0

            def meet(self):
                self.arrive()
                self.pass_()

            def arrive(self):
                self.count += 1
                self.eng.drain().then_inc(stage, 1)

            def pass_(self):
                self.eng.wait_ge(stage, 4 * self.count)

            def restart(self):
                self.count = 0

        def end_round(eng, r, clears=False):
            eng.drain().then_inc(arrive, 1)
            eng.wait_ge(arrive, 5 * r + 5)
            eng.sem_inc(spare, 1)
            if clears:
                eng.sem_clear(range(first, last + 1))
            eng.drain().then_inc(go, 1)
            eng.wait_ge(go, 5 * r + 5)
            eng.sem_inc(spare, 1)

        def blk(n, k=1):
            return slice(n * P, (n + k) * P)

        def half(b):
            return slice(b * HH, (b + 1) * HH)

        block = ctx.enter_context(nc.Block())

        @block.sync
        def _(sp):
            def load_qkv(l):
                w = wqkv[bass.ds(l, 1), :, :].rearrange("o k n -> (o k) n")
                sp.dma_start(wqa[:, :], w[0:DLO, :]).then_inc(wqkv_in, 16)
                sp.dma_start(wqb[0:DHI + 1, :], w[DLO:D + 1, :]).then_inc(wqkv_in, 16)

            def load_rest(l):
                o = wo[bass.ds(l, 1), :, :].rearrange("o k n -> (o k) n")
                a = w1[bass.ds(l, 1), :, :].rearrange("o k n -> (o k) n")
                b = w2[bass.ds(l, 1), :, :].rearrange("o k n -> (o k) n")
                r = rw[bass.ds(l, 1), :, :].rearrange("o k n -> (o k) n")
                g = lnl[bass.ds(l, 1), :, :].rearrange("o k n -> (o k) n")
                for dst, src in ((woa[:, :], o[0:DLO, :]), (wob[0:DHI + 1, :], o[DLO:D + 1, :]),
                                 (w1a[:, :], a[0:DLO, :]), (w1b[0:DHI + 1, :], a[DLO:D + 1, :]),
                                 (w2s[:, :, :], b.rearrange("(j p) n -> p j n", p=P)),
                                 (rwb[0:DHI + 1, :], r[DLO:D + 1, :]),
                                 (lna[:, :], g[0:DLO, :]), (lnb[0:DHI, :], g[DLO:D, :])):
                    sp.dma_start(dst, src).then_inc(wrest_in, 16)

            consts = [
                (idf[:, :], ident), (bandf[:, :, :], band), (colc[:, :], cols), (embs[:, :], emb),
                (lfa[:, :], lnf[0:DLO, :]), (lfb[0:DHI, :], lnf[DLO:D, :]),
                (wca[:, :], wc[0:DLO, :]), (wcb[0:DHI + 1, :], wc[DLO:D + 1, :]),
                (dcol[:, 0:1], decay), (cw[:, :], convw), (wos[:, :], wout), (bo2s[:, :], bo2),
                (l12[:, :], ln12), (aw1s[:, :], aw1), (ab1s[:, :], ab1), (aw2s[:, :, :], aw2), (ab2s[:, :], ab2),
                (wgs[:, :], wg), (bgs[:, :], bg), (mb1s[:, :, :], mb1), (mb2s[:, :], mb2),
            ]
            for dst, src in consts:
                sp.dma_start(dst, src).then_inc(const_in, 16)
            sp.wait_ge(const_in, 16 * len(consts))
            sp.sem_inc(setup, 1)
            sp.wait_ge(setup, 5)

            with sp.Fori(0, B) as b:
                sp.dma_start(idsi, x[bass.ds(b, 1), :].to_broadcast([P, T])).then_inc(ids_in, 16)
                sp.dma_start(padu[:, :], pad[bass.ds(b, 1), :]).then_inc(pad_in, 16)
                load_qkv(0)
                sp.dma_start(stack[R_BIAS:R_MAX, 0:H, :].rearrange("p h t -> p (h t)"), qrows).then_inc(rows_in, 16)
                sp.dma_start(stack[R_MAX:K_ALL, H:2 * H, :].rearrange("p h t -> p (h t)"), krows).then_inc(rows_in, 16)
                sp.wait_ge(padf_ready, 1)
                for h in range(H):
                    sp.dma_start(stack[R_BIAS:R_MAX, H + h, :], kbrow[0:1, :, :]).then_inc(kb_out, 16)
                sp.wait_ge(kb_out, 16 * H)
                sp.wait_ge(rows_in, 32)
                sp.wait_ge(ids_in, 16)
                sp.wait_ge(wqkv_in, 32)
                end_round(sp, b * ROUNDS)

                with sp.Fori(0, L) as l:
                    load_rest(l)
                    for n in range(NB):
                        sp.wait_ge(mt_copied, n + 1)
                        for i in range(3):
                            sp.dma_start(stack[R_MAX + i:R_MAX + i + 1, 0:H, blk(n)],
                                         mtr[i * H:(i + 1) * H, n % 2, :]).then_inc(m_in[n % 2], 16)
                    sp.wait_ge(m_in[0], 48 * NB // 2)
                    sp.wait_ge(m_in[1], 48 * NB // 2)
                    load_qkv(1 - l)
                    sp.wait_ge(wqkv_in, 32)
                    sp.wait_ge(wrest_in, 128)
                    end_round(sp, b * ROUNDS + 1 + l)

                sp.dma_start(mw1s[:, :, :], mw1).then_inc(mw_in, 16)
                sp.dma_start(mw2s[:, :, :, :], mw2).then_inc(mw_in, 16)
                for n in range(NB):
                    sp.wait_ge(o_ready, n + 1)
                    sp.dma_start(out[bass.ds(b, 1), blk(n), :].rearrange("o p m -> (o p) m"),
                                 h0[:, blk(n)]).then_inc(o_out, 16)
                sp.wait_ge(o_out, 16 * NB)
                sp.wait_ge(mw_in, 32)
                end_round(sp, b * ROUNDS + 1 + L)

        @block.gpsimd
        def _(pool):
            ch = Link(pool, pool_own)
            sg = Stages(pool)
            pool.wait_ge(const_in, 16 * 21)
            for t, value in ((xb[DHI:DHI + 1, :], 1.0), (atb[DHI:DHI + 1, :], 1.0), (ones[:, :], 1.0), (onesb[:, :], 1.0),
                             (q0s[:, :, :], 0.0), (epst[:, :], EPS), (xn[:, :], 0.0), (bm[:, :], 1.0),
                             (vst[:, :, :, 3 * DH:VW], 1.0)):
                ch.link(nc.gpsimd.memset(t, value))
            ch.link(nc.gpsimd.affine_select(out=bm[:, :], in_=bm[:, :], compare_op=ALU.is_ge, fill=0.0, base=0,
                                            pattern=[[1, D]], channel_multiplier=-DH))
            ch.link(nc.gpsimd.affine_select(out=bm[:, :], in_=bm[:, :], compare_op=ALU.is_ge, fill=0.0, base=DH - 1,
                                            pattern=[[-1, D]], channel_multiplier=DH))
            pool.sem_clear(pool_own)
            pool.drain().then_inc(setup, 1)
            pool.wait_ge(setup, 5)

            def rstd_of(j):
                pool.wait_ge(y_stats, j + 1)
                ch.link(nc.gpsimd.tensor_tensor(ve[:, j % 4:j % 4 + 1], mv[:, j % 4, 1:2], epst[:, :], ALU.add))
                nc.gpsimd.tensor_tensor(rstd[:, j % 4:j % 4 + 1], ve[:, j % 4:j % 4 + 1], colc[:, 3:4],
                                        ALU.pow).then_inc(y_rstd, 1)

            def split_weights(e):
                nc.gpsimd.tensor_copy(w1r[:, e % 2, 0, :], mw1s[:, e, :])
                ch.link(nc.gpsimd.tensor_copy(w2r[:, e % 2, 0, :, :], mw2s[:, e, :, :]))
                nc.gpsimd.tensor_tensor(w1r[:, e % 2, 1, :], mw1s[:, e, :], w1r[:, e % 2, 0, :].bitcast(F32),
                                        ALU.subtract)
                nc.gpsimd.tensor_tensor(w2r[:, e % 2, 1, :, :], mw2s[:, e, :, :], w2r[:, e % 2, 0, :, :].bitcast(F32),
                                        ALU.subtract).then_inc(w_split, 1)

            with pool.Fori(0, B) as b:
                end_round(pool, b * ROUNDS, True)

                with pool.Fori(0, L) as l:
                    ch.restart()
                    sg.restart()
                    sg.meet()
                    for s in range(U + 18):
                        u = s - 1
                        if 0 <= u < U and u % 4 != 3:
                            pool.wait_ge(p1_ready, u + 1)
                            if u >= RING:
                                pool.wait_ge(pv_mm, u - RING + 1)
                            w = len(window(u // H)) * P
                            nc.gpsimd.tensor_tensor(p2[:, u % RING, 0:w], p32[:, u % RING, 0:w], p1[:, u % RING, 0:w],
                                                    ALU.subtract).then_inc(p2_pool, 1)
                        n, r = divmod(s, H)
                        for g, at in ((0, 0), (1, 6)):
                            if r == at and n < NB:
                                k = 2 * n + g
                                if g == 0:
                                    pool.wait_ge(eg_ready, n + 1)
                                if k == 0:
                                    pool.wait_ge(v0_ready, 1)
                                if k >= 2:
                                    pool.wait_ge(comb, k - 1)
                                nc.gpsimd.tensor_tensor(
                                    pvt[:, g, 0, :, :], v0b[:, half(g), :],
                                    eg[:, n % 4, half(g)].unsqueeze(2).to_broadcast([P, HH, DH]),
                                    ALU.mult).then_inc(pvg_ready, 1)
                    sg.meet()
                    for j in range(2 * NB):
                        rstd_of(j)
                    sg.meet()
                    end_round(pool, b * ROUNDS + 1 + l, True)

                ch.restart()
                sg.restart()
                for j in range(NB):
                    rstd_of(j)
                sg.meet()
                for j in range(NB, 3 * NB):
                    rstd_of(j)
                sg.arrive()
                pool.wait_ge(mw_in, 32)
                split_weights(0)
                sg.pass_()
                for j in range(3 * NB, 4 * NB):
                    rstd_of(j)
                sg.arrive()
                split_weights(1)
                sg.pass_()
                for j in range(4 * NB, 5 * NB):
                    rstd_of(j)
                sg.meet()
                for e in range(2, E):
                    pool.wait_ge(ey_mm, NC * (e - 1))
                    split_weights(e)
                sg.meet()
                end_round(pool, b * ROUNDS + 1 + L, True)

        @block.scalar
        def _(act):
            sg = Stages(act)
            act.wait_ge(const_in, 16 * 21)
            nc.scalar.activation(idb[:, :], idf[:, :], ACT.Copy)
            nc.scalar.activation(bandb[:, :, :], bandf[:, :, :], ACT.Copy)
            nc.scalar.activation(rowe[:, :, :], idf[0:E, 0:E].unsqueeze(2).to_broadcast([E, E, P]), ACT.Copy)
            act.drain().then_inc(setup, 1)
            act.wait_ge(setup, 5)

            def norm_out(j, k, dst, gb):
                act.wait_ge(z_mm, j + 1)
                bank = ps[4 + j % 2]
                for i, (d, (g, o)) in enumerate(zip(dst, gb)):
                    ins = nc.scalar.activation(d, bank[0:d.shape[0], i * P:(i + 1) * P], ACT.Identity, bias=o, scale=g)
                ins.then_inc(ln_out, 1)

            def norm_out_d(n):
                act.wait_ge(z_mm, NB + n + 1)
                nc.scalar.activation(xn[:, 2 + n * P:2 + (n + 1) * P], ps[4 + n % 2][:, 0:P], ACT.Identity,
                                     bias=l12[:, 1:2], scale=l12[:, 0:1]).then_inc(ln_out, 1)

            with act.Fori(0, B) as b:
                for c in range(NC):
                    act.wait_ge(emb_mm, c + 1)
                    nc.scalar.activation(xa[:, c * CH:(c + 1) * CH], ps[2 * c][:, :], ACT.Copy)
                    nc.scalar.activation(xb[0:DHI, c * CH:(c + 1) * CH], ps[2 * c + 1][0:DHI, :], ACT.Copy)
                end_round(act, b * ROUNDS)

                with act.Fori(0, L) as l:
                    sg.restart()
                    for n in range(NB):
                        act.wait_ge(qk_mm, n + 1)
                        nc.scalar.activation(nat[:, n, :, 0:DH],
                                             ps[n % 2][:, 0:2 * D].rearrange("p (h d) -> p h d", d=DH),
                                             ACT.Copy).then_inc(qk_p1, 1)
                        act.wait_ge(v_mm, n + 1)
                        nc.scalar.activation(vst[:, n, :, 0:DH],
                                             ps[2 + n % 2][:, 0:D].rearrange("p (h d) -> p h d", d=DH),
                                             ACT.Copy).then_inc(v_p1, 1)
                        act.wait_ge(qk_res, n + 1)
                        r = res[:, n % 2, :].rearrange("p (h d) -> p h d", d=DH)
                        nc.scalar.activation(nat[:, n, 0:H, Q_ROWS[1][0]:Q_ROWS[1][0] + DH], r[:, 0:H, :], ACT.Copy)
                        nc.scalar.activation(nat[:, n, H:2 * H, K_ROWS[1][0]:K_ROWS[1][0] + DH], r[:, H:2 * H, :],
                                             ACT.Copy).then_inc(qk_p2, 1)
                        act.wait_ge(v_res, n + 1)
                        nc.scalar.activation(vst[:, n, :, DH:2 * DH],
                                             resv[:, n % 2, :].rearrange("p (h d) -> p h d", d=DH),
                                             ACT.Copy).then_inc(v_p2, 1)
                    for k in range(0, 2 * H, 2):
                        act.wait_ge(tr_mm, k + 1)
                        nc.scalar.activation(stack[0:NPIECE, k, :], psb[4 + k % 4][0:NPIECE, :],
                                             ACT.Copy).then_inc(ev_act, 1)
                    sg.meet()
                    for s in range(-LEAD, U + 18):
                        if s == -LEAD + 4:
                            act.wait_ge(f_max, 1)
                            nc.scalar.activation(pfull[:, 0, 0:CH], ps[2][0:H, :], ACT.Exp, bias=fst[:, 0:1],
                                                 accum_out=fst[:, 1:2]).then_inc(f_exp, 1)
                            nc.scalar.activation(pfull[:, 0, CH:T], ps[3][0:H, :], ACT.Exp, bias=fst[:, 0:1],
                                                 accum_out=fst[:, 2:3]).then_inc(f_exp, 1)
                        if s == -LEAD + 10:
                            act.wait_ge(ft_mm, 1)
                            nc.scalar.activation(f1[:, :, :], ps[4][:, 0:NB * H].rearrange("p (n h) -> p n h", h=H),
                                                 ACT.Copy).then_inc(f1_ready, 1)
                        if s == -1:
                            act.wait_ge(oc_mm, 1)
                            nc.scalar.activation(ata[:, 0:1], ps[4][:, 0:1], ACT.Copy)
                            nc.scalar.activation(atb[0:DHI, 0:1], ps[4][0:DHI, 8:9], ACT.Copy).then_inc(oc_copied, 1)
                        for n in range(NB):
                            if s == H * n - 5:
                                act.wait_ge(mt_mm, n + 1)
                                if n >= 2:
                                    act.wait_ge(m_in[n % 2], 48 * (n // 2))
                                nc.scalar.activation(mtr[:, n % 2, :], psb[5][0:3 * H, 64:64 + P],
                                                     ACT.Copy).then_inc(mt_copied, 1)
                                act.wait_ge(dg_ready, n + 1)
                                nc.scalar.activation(eg[:, n % 4, :], dg0[:, n % 4, :], ACT.Exp).then_inc(eg_ready, 1)
                        if 0 <= s < U:
                            w = len(window(s // H)) * P
                            act.wait_ge(t_mm, s + 1)
                            if s >= RING:
                                act.wait_ge(pv_mm, s - RING + 1)
                            nc.scalar.activation(p32[:, s % RING, 0:w], ps[2 + s % 3][:, 0:w], ACT.Exp).then_inc(p32_ready, 1)
                            nc.scalar.activation(p1[:, s % RING, 0:w], ps[2 + s % 3][:, 0:w], ACT.Exp).then_inc(p1_ready, 1)
                        for n in range(NB):
                            if s == H * (n + 1) + 9 + 1:
                                act.wait_ge(at_mm, n + 1)
                                t0 = n == 0
                                nc.scalar.activation(ata[:, n * P + t0:(n + 1) * P], ps[5][:, P + t0:2 * P], ACT.Copy)
                                nc.scalar.activation(atb[0:DHI, n * P + t0:(n + 1) * P],
                                                     ps[5][0:DHI, 2 * P + t0:3 * P], ACT.Copy).then_inc(at_copied, 1)
                    sg.meet()
                    act.wait_ge(wrest_in, 128)
                    for kind, i in SEQ_C:
                        if kind == "tr":
                            k = i // NB
                            norm_out(i, k, (xa[:, blk(i % NB)], xb[0:DHI, blk(i % NB)]),
                                     ((lna[:, 2 * k:2 * k + 1], lna[:, 2 * k + 1:2 * k + 2]),
                                      (lnb[0:DHI, 2 * k:2 * k + 1], lnb[0:DHI, 2 * k + 1:2 * k + 2])))
                        if kind == "hid":
                            act.wait_ge(h_mm, i + 1)
                            c, m = divmod(i, FF // P)
                            if c:
                                act.wait_ge(y_mm, NB + BPC)
                            nc.scalar.activation(hid[:, m, :], ps[6 + i % 2][:, :], ACT.Relu).then_inc(h_relu, 1)
                    sg.meet()
                    end_round(act, b * ROUNDS + 1 + l)

                sg.restart()
                for j in range(NB):
                    norm_out(j, 0, (xa[:, blk(j)], xb[0:DHI, blk(j)]),
                             ((lfa[:, 0:1], lfa[:, 1:2]), (lfb[0:DHI, 0:1], lfb[0:DHI, 1:2])))
                nc.scalar.activation(dcol[:, 1:2], dcol[:, 0:1], ACT.Exp, scale=-1.0).then_inc(act_own, 1)
                sg.meet()
                for n in range(NB):
                    act.wait_ge(y_mm, NB + n + 1)
                    nc.scalar.activation(h0[:, blk(n)], ps[n % 4][:, 0:DM], ACT.Copy).then_inc(h0_kept, 1)
                    if n >= 2:
                        norm_out_d(n - 2)
                norm_out_d(NB - 2)
                norm_out_d(NB - 1)
                sg.meet()
                for n in range(NB):
                    act.wait_ge(z_mm, 2 * NB + n + 1)
                    nc.scalar.activation(ht[:, blk(n)], ps[4 + n % 2][:, 0:P], ACT.Identity, bias=l12[:, 3:4],
                                         scale=l12[:, 2:3]).then_inc(ln_out, 1)
                sg.meet()
                for i in range(NC * 2):
                    c, m = divmod(i, 2)
                    act.wait_ge(g_mm, i + 1)
                    nc.scalar.activation(gl[:, m * T + c * CH:m * T + (c + 1) * CH], ps[6 + i % 2][:, :], ACT.Gelu,
                                         bias=ab1s[:, m:m + 1]).then_inc(g_ready, 1)
                for n in range(NB):
                    act.wait_ge(z_mm, 3 * NB + n + 1)
                    nc.scalar.activation(xm[:, blk(n)], ps[4 + n % 2][:, 0:P], ACT.Copy).then_inc(ln_out, 1)
                sg.meet()
                nc.scalar.activation(xmr[:, 0, :], xm[:, :], ACT.Copy).then_inc(x_hi, 1)
                for k in range(E * NC):
                    if k == 1:
                        act.wait_ge(lg_sub, 1)
                        nc.scalar.activation(gt[:, 2, :, :], gt[:, 1, :, :], ACT.Exp).then_inc(lg_exp, 1)
                        act.wait_ge(st_mm, 1)
                        nc.scalar.activation(selt[:, 0:CH], ps[2][0:E, :], ACT.Copy)
                        nc.scalar.activation(selt[:, CH:T], ps[3][0:E, :], ACT.Copy).then_inc(st_copied, 1)
                    if k >= 2:
                        act.wait_ge(ey_mm, k - 1)
                    for m in range(EH // P):
                        i = k * (EH // P) + m
                        act.wait_ge(e_mm, i + 1)
                        if i >= 4:
                            act.wait_ge(e_split, i - 3)
                        bias = mb1s[:, k // NC, m:m + 1]
                        nc.scalar.activation(eh32[:, i % 4, :], ps[4 + i % 4][:, :], ACT.Relu, bias=bias)
                        nc.scalar.activation(ehr[:, k % 2, 0, m, :], ps[4 + i % 4][:, :], ACT.Relu,
                                             bias=bias).then_inc(e_relu, 1)
                sg.meet()
                end_round(act, b * ROUNDS + 1 + L)

        @block.vector
        def _(dve):
            ch = Link(dve, dve_own)
            sg = Stages(dve)
            dve.wait_ge(const_in, 16 * 21)
            for k in range(KC):
                nc.vector.tensor_scalar(diag[:, k, :], idf[:, :], cw[:, k:k + 1], None, ALU.mult)
            dve.drain().then_inc(setup, 1)
            dve.wait_ge(setup, 5)

            def stats(j, src, wait=True):
                if wait:
                    dve.wait_ge(y_mm, j + 1)
                ch.link(nc.vector.bn_stats(stt_[:, j % 4, :], src))
                nc.vector.bn_aggr(mv[:, j % 4, :], stt_[:, j % 4, :]).then_inc(y_stats, 1)

            def normed(j, src, dst):
                dve.wait_ge(y_rstd, j + 1)
                return nc.vector.tensor_scalar(dst, src, mv[:, j % 4, 0:1], rstd[:, j % 4:j % 4 + 1],
                                               ALU.subtract, ALU.mult)

            def chunk(t, j):
                return t[:, (j % NC) * CH:(j % NC + 1) * CH]

            def heads(t):
                return t.rearrange("p (h d) -> p h d", d=DH)

            with dve.Fori(0, B) as b:
                ch.restart()
                dve.wait_ge(ids_in, 16)
                nc.vector.tensor_scalar(oneh, idsi, colc[:, 0:1], None, ALU.is_equal).then_inc(onehot_ready, 1)
                dve.wait_ge(pad_in, 16)
                ch.link(nc.vector.tensor_copy(padw[0], padu[:, :].bitcast(U8)))
                ch.link(nc.vector.tensor_copy(padw[1], padw[0]))
                ch.link(nc.vector.memset(padw[0][:, 0:1], 1.0))
                for i in range(4):
                    ins = nc.vector.tensor_scalar(kbrow[:, i, :], padw[i // 2], (KB_HI, KB_LO)[i % 2], None, ALU.mult)
                ch.link(ins)
                dve.drain().then_inc(padf_ready, 1)
                end_round(dve, b * ROUNDS)

                with dve.Fori(0, L) as l:
                    ch.restart()
                    sg.restart()
                    nc.vector.tensor_scalar(wqa[:, 0:D], wqa[:, 0:D], 0.25, None, ALU.mult)
                    nc.vector.tensor_scalar(wqb[0:DHI + 1, 0:D], wqb[0:DHI + 1, 0:D], 0.25, None,
                                            ALU.mult).then_inc(glob_ready, 1)
                    for n in range(NB):
                        r = heads(res[:, n % 2, :])
                        rv = heads(resv[:, n % 2, :])
                        dve.wait_ge(qk_p1, n + 1)
                        nc.vector.tensor_tensor(r, heads(ps[n % 2][:, 0:2 * D]), nat[:, n, :, 0:DH],
                                                ALU.subtract).then_inc(qk_res, 1)
                        dve.wait_ge(v_p1, n + 1)
                        nc.vector.tensor_tensor(rv, heads(ps[2 + n % 2][:, 0:D]), vst[:, n, :, 0:DH],
                                                ALU.subtract).then_inc(v_res, 1)
                        q, k = nat[:, n, 0:H, :], nat[:, n, H:2 * H, :]
                        for t, at in ((q, Q_ROWS[0][1]), (q, Q_ROWS[0][2]), (k, K_ROWS[0][1]), (k, K_ROWS[0][2])):
                            nc.vector.tensor_copy(t[:, :, at:at + DH], t[:, :, 0:DH])
                        dve.wait_ge(qk_p2, n + 1)
                        for t, rows, rr in ((q, Q_ROWS, r[:, 0:H, :]), (k, K_ROWS, r[:, H:2 * H, :])):
                            a, c, d = rows[1][0], rows[1][1], rows[2][0]
                            nc.vector.tensor_copy(t[:, :, c:c + DH], t[:, :, a:a + DH])
                            ins = nc.vector.tensor_tensor(t[:, :, d:d + DH], rr, t[:, :, a:a + DH], ALU.subtract)
                        ins.then_inc(nat_ready, 1)
                        dve.wait_ge(v_p2, n + 1)
                        nc.vector.tensor_tensor(vst[:, n, :, 2 * DH:3 * DH], rv, vst[:, n, :, DH:2 * DH], ALU.subtract)
                    for k in range(1, 2 * H, 2):
                        dve.wait_ge(tr_mm, k + 1)
                        nc.vector.tensor_copy(stack[0:NPIECE, k, :], psb[4 + k % 4][0:NPIECE, :]).then_inc(ev_dve, 1)
                    sg.meet()
                    nc.vector.tensor_scalar(k0s[0:K_NAT, :], stack[0:K_NAT, H:2 * H, 0], colc[0:K_NAT, 1:2], None, ALU.mult)
                    nc.vector.tensor_scalar(q0s[0:K_NAT, :, :].rearrange("p a b -> p (a b)")[:, 0:H * H:H + 1],
                                            stack[0:K_NAT, 0:H, 0], colc[0:K_NAT, 1:2], colc[0:K_NAT, 2:3],
                                            ALU.mult, ALU.add).then_inc(glob_ready, 1)
                    dve.wait_ge(v0_mm, 1)
                    for g in range(2):
                        v = ps[6 + g][:, 0:HH * VW].rearrange("p (h w) -> p h w", w=VW)
                        ch.link(nc.vector.tensor_copy(v0t[:, 0, half(g), :], v[:, :, 2 * DH:3 * DH]))
                        ch.link(nc.vector.tensor_tensor(v0t[:, 1, half(g), :], v[:, :, DH:2 * DH],
                                                        v0t[:, 0, half(g), :], ALU.add))
                        ins = nc.vector.tensor_tensor(v0b[:, half(g), :], v[:, :, 0:DH], v0t[:, 1, half(g), :], ALU.add)
                    ins.then_inc(v0_ready, 1)
                    for s in range(-LEAD, U + 18):
                        if s == -LEAD + 3:
                            dve.wait_ge(f_mm, 2)
                            nc.vector.tensor_reduce(fst[:, 2:3], ps[2][0:H, :], AX.X, ALU.max, negate=True)
                            ch.link(nc.vector.tensor_reduce(fst[:, 3:4], ps[3][0:H, :], AX.X, ALU.max, negate=True))
                            nc.vector.tensor_tensor(fst[:, 0:1], fst[:, 2:3], fst[:, 3:4], ALU.min).then_inc(f_max, 1)
                        if s == -LEAD + 7:
                            dve.wait_ge(f_exp, 2)
                            ch.link(nc.vector.tensor_tensor(fst[:, 3:4], fst[:, 1:2], fst[:, 2:3], ALU.add))
                            ch.link(nc.vector.reciprocal(fst[:, 3:4], fst[:, 3:4]))
                            nc.vector.tensor_scalar(pfull[:, 1, :], pfull[:, 0, :], fst[:, 3:4], None,
                                                    ALU.mult).then_inc(f_norm, 1)
                        if s == -LEAD + 12:
                            dve.wait_ge(f1_ready, 1)
                            nc.vector.tensor_tensor(f2[:, :, :], ps[4][:, 0:NB * H].rearrange("p (n h) -> p n h", h=H),
                                                    f1[:, :, :], ALU.subtract).then_inc(f2_ready, 1)
                        if s == -3:
                            dve.wait_ge(og_mm, 1)
                            for g in range(2):
                                v = ps[6 + g][0:H, 0:HH * VW].rearrange("p (h w) -> p h w", w=VW)
                                for i in range(3):
                                    ins = nc.vector.tensor_tensor(
                                        heads(og[:, i, :])[:, half(g), :], v[:, :, i * DH:(i + 1) * DH],
                                        heads(bm[0:H, :])[:, half(g), :], ALU.mult)
                            ins.then_inc(og_ready, 1)
                        v = s + LEAD
                        if v < U:
                            n, h = divmod(v, H)
                            w = len(window(n)) * P
                            dve.wait_ge(nat_mm, v + 1)
                            nc.vector.tensor_reduce(nmx[:, n % 3, h:h + 1], ps[v % 2][:, 0:w], AX.X, ALU.max,
                                                    negate=True).then_inc(max_done, 1)
                            if h == H - 1:
                                dve.wait_ge(max_done, v + 1)
                                dve.wait_ge(sg_mm, n + 1)
                                ch.link(nc.vector.scalar_tensor_tensor(nm[:, :], ps[5][:, 0:H], -1.0, nmx[:, n % 3, :],
                                                                       ALU.mult, ALU.min))
                                if n >= 1:
                                    dve.wait_ge(mt_mm, n)
                                ch.link(nc.vector.tensor_copy(mcat[:, 0, :], nm[:, :]))
                                ch.link(nc.vector.tensor_tensor(nmr[:, :], nm[:, :], mcat[:, 0, :], ALU.subtract))
                                ch.link(nc.vector.tensor_copy(mcat[:, 1, :], nmr[:, :]))
                                nc.vector.tensor_tensor(mcat[:, 2, :], nmr[:, :], mcat[:, 1, :], ALU.subtract)
                                nc.vector.tensor_tensor(dg0[:, n % 4, :], ps[5][:, 0:H], nm[:, :],
                                                        ALU.add).then_inc(dg_ready, 1)
                        u = s - 1
                        if 0 <= u < U and u % 4 == 3:
                            dve.wait_ge(p1_ready, u + 1)
                            if u >= RING:
                                dve.wait_ge(pv_mm, u - RING + 1)
                            w = len(window(u // H)) * P
                            nc.vector.tensor_tensor(p2[:, u % RING, 0:w], p32[:, u % RING, 0:w], p1[:, u % RING, 0:w],
                                                    ALU.subtract).then_inc(p2_dve, 1)
                        for g in range(2):
                            n, r = divmod(s - (10 if g == 0 else 16), H)
                            if r == 0 and 0 <= n < NB:
                                k = 2 * n + g
                                pv = ps[6 + g][:, 0:HH * VW].rearrange("p (h w) -> p h w", w=VW)
                                t = pvt[:, g, :, :, :]
                                dve.wait_ge(pv_mm, H * n + HH * (g + 1))
                                dve.wait_ge(pvg_ready, k + 1)
                                nc.vector.tensor_tensor(den[:, g, 0, :], pv[:, :, 3 * DH], eg[:, n % 4, half(g)], ALU.add)
                                ch.link(nc.vector.tensor_tensor(t[:, 1, :, :], pv[:, :, 2 * DH:3 * DH], t[:, 0, :, :], ALU.add))
                                nc.vector.reciprocal(den[:, g, 1, :], den[:, g, 0, :])
                                ch.link(nc.vector.tensor_tensor(t[:, 2, :, :], pv[:, :, DH:2 * DH], t[:, 1, :, :], ALU.add))
                                ch.link(nc.vector.tensor_tensor(t[:, 3, :, :], pv[:, :, 0:DH], t[:, 2, :, :], ALU.add))
                                if n >= 2 and g == 0:
                                    dve.wait_ge(at_mm, n - 1)
                                nc.vector.tensor_tensor(
                                    heads(att[:, n % 2, :])[:, half(g), :], t[:, 3, :, :],
                                    den[:, g, 1, :].unsqueeze(2).to_broadcast([P, HH, DH]), ALU.mult).then_inc(comb, 1)
                    sg.meet()
                    pend = []
                    for kind, i in SEQ_C:
                        if kind == "y":
                            stats(i, ps[i % 4][:, 0:D])
                            pend.append(i)
                        if kind == "z":
                            if i >= 2:
                                dve.wait_ge(z_mm, i - 1)
                            normed(i, ps[i % 4][:, 0:D], zt[:, i % 2, :]).then_inc(z_ready, 1)
                    sg.meet()
                    end_round(dve, b * ROUNDS + 1 + l)

                ch.restart()
                sg.restart()
                for j in range(NB + 1):
                    if j < NB:
                        stats(j, ps[j % 4][:, 0:D])
                    if j >= 1:
                        i = j - 1
                        if i >= 2:
                            dve.wait_ge(z_mm, i - 1)
                        normed(i, ps[i % 4][:, 0:D], zt[:, i % 2, :]).then_inc(z_ready, 1)
                sg.meet()
                ch.link(nc.vector.tensor_scalar(dcol[:, 2:3], dcol[:, 1:2], 1.0, None, ALU.add))
                ch.link(nc.vector.reciprocal(dcol[:, 3:4], dcol[:, 2:3]))
                ch.link(nc.vector.tensor_scalar(dcol[:, 2:3], dcol[:, 3:4], -1.0, 1.0, ALU.mult, ALU.add))
                for k in range(NB + 2):
                    if k < NB:
                        dve.wait_ge(h0_kept, k + 1)
                        stats(UNIT_H[k], ps[k % 4][:, 0:DM], False)
                    if 1 <= k <= NB:
                        n = k - 1
                        ch.link(normed(UNIT_H[n], ps[n % 4][:, 0:DM], x1[:, blk(n)]))
                        stats(UNIT_X[n], x1[:, blk(n)], False)
                    if k >= 2:
                        n = k - 2
                        if n >= 2:
                            dve.wait_ge(z_mm, NB + n - 1)
                        normed(UNIT_X[n], x1[:, blk(n)], zt[:, n % 2, 0:DM]).then_inc(z_ready, 1)
                sg.meet()
                ch.link(nc.vector.tensor_scalar(d1, xn[:, 2:2 + T], dcol[:, 2:3], None, ALU.mult))
                nc.vector.tensor_tensor_scan(st, dcol[:, 3:4].to_broadcast([P, T]), d1, 0.0, ALU.mult,
                                             ALU.add).then_inc(s_ready, 1)
                for k in range(NB + 1):
                    if k < NB:
                        dve.wait_ge(y_mm, 2 * NB + k + 1)
                        ch.link(nc.vector.tensor_tensor(x1[:, blk(k)], ps[k % 4][:, 0:DM], x1[:, blk(k)], ALU.add))
                        stats(3 * NB + k, x1[:, blk(k)], False)
                    if k >= 1:
                        n = k - 1
                        if n >= 2:
                            dve.wait_ge(z_mm, 2 * NB + n - 1)
                        normed(3 * NB + n, x1[:, blk(n)], zt[:, n % 2, 0:DM]).then_inc(z_ready, 1)
                sg.meet()
                for k in range(NB + 1):
                    if k < NB:
                        dve.wait_ge(y_mm, 3 * NB + k + 1)
                        ch.link(nc.vector.tensor_tensor(x1[:, blk(k)], ps[k % 4][:, 0:DM], x1[:, blk(k)], ALU.add))
                        ch.link(nc.vector.tensor_tensor(h0[:, blk(k)], h0[:, blk(k)], x1[:, blk(k)], ALU.add))
                        stats(4 * NB + k, h0[:, blk(k)], False)
                    if k >= 1:
                        n = k - 1
                        if n >= 2:
                            dve.wait_ge(z_mm, 3 * NB + n - 1)
                        normed(4 * NB + n, h0[:, blk(n)], zt[:, n % 2, 0:DM]).then_inc(z_ready, 1)
                sg.meet()
                dve.wait_ge(x_hi, 1)
                nc.vector.tensor_tensor(xmr[:, 1, :], xm[:, :], xmr[:, 0, :].bitcast(F32), ALU.subtract).then_inc(x_lo, 1)
                dve.wait_ge(lg_mm, 1)
                ch.link(nc.vector.tensor_copy(gt[:, 0, :, :], ps[0][:, 0:NB * E].rearrange("p (n e) -> p n e", e=E)))
                ch.link(nc.vector.tensor_reduce(gs[:, 0, :], gt[:, 0, :, :], AX.X, ALU.max))
                top = gs[:, 0, :].unsqueeze(2).to_broadcast([P, NB, E])
                nc.vector.tensor_tensor(gt[:, 1, :, :], gt[:, 0, :, :], top, ALU.subtract).then_inc(lg_sub, 1)
                ch.link(nc.vector.tensor_tensor(gt[:, 3, :, :], gt[:, 0, :, :], top, ALU.is_equal))
                for e in range(E):
                    ins = nc.vector.tensor_scalar(gt[:, 4, :, e], gt[:, 3, :, e], float(E - e), None, ALU.mult)
                ch.link(ins)
                ch.link(nc.vector.tensor_reduce(gs[:, 1, :], gt[:, 4, :, :], AX.X, ALU.max))
                nc.vector.tensor_tensor(gt[:, 5, :, :], gt[:, 4, :, :],
                                        gs[:, 1, :].unsqueeze(2).to_broadcast([P, NB, E]), ALU.is_equal).then_inc(sel_ready, 1)
                for k in range(E * NC + 2):
                    for m in range(EH // P):
                        if k < E * NC:
                            i = k * (EH // P) + m
                            dve.wait_ge(e_relu, i + 1)
                            nc.vector.tensor_tensor(ehr[:, k % 2, 1, m, :], eh32[:, i % 4, :],
                                                    ehr[:, k % 2, 0, m, :].bitcast(F32), ALU.subtract).then_inc(e_split, 1)
                        if m == 0 and k >= 2 + NC:
                            j = k - 2
                            dve.wait_ge(ey_masked, j + 1)
                            if j >= 2 * NC:
                                dve.wait_ge(acc_done, j - 2 * NC + 1)
                            nc.vector.tensor_tensor(chunk(acc, j), ey[:, j % 2, :], chunk(acc, j), ALU.add).then_inc(acc_done, 1)
                    if k == 0:
                        dve.wait_ge(lg_exp, 1)
                        ch.link(nc.vector.tensor_reduce(gs[:, 2, :], gt[:, 2, :, :], AX.X, ALU.add))
                        ch.link(nc.vector.reciprocal(gs[:, 3, :], gs[:, 2, :]))
                    if 1 <= k <= E * NC:
                        j = k - 1
                        dve.wait_ge(mask_mm, j + 1)
                        if j >= 2:
                            dve.wait_ge(ey_masked, j - 1)
                        if j >= 2 + NC:
                            dve.wait_ge(acc_done, j - 2 - NC + 1)
                        nc.vector.tensor_copy(mask[:, j % 2, :], ps[2 + j % 2][:, :]).then_inc(mask_copied, 1)
                        dve.wait_ge(mask_copied, j + 1)
                        dve.wait_ge(ey_mm, j + 1)
                        nc.vector.scalar_tensor_tensor(ey[:, j % 2, :] if j >= NC else chunk(acc, j), ps[j % 2][:, :],
                                                       mb2s[:, j // NC:j // NC + 1], mask[:, j % 2, :],
                                                       ALU.add, ALU.mult).then_inc(ey_masked, 1)
                for n in range(NB):
                    dve.wait_ge(o_mm, n // BPC + 1)
                    nc.vector.scalar_tensor_tensor(h0[:, blk(n)], ps[4 + n // BPC][:, blk(n % BPC)], gs[:, 3, n:n + 1],
                                                   h0[:, blk(n)], ALU.mult, ALU.add).then_inc(o_ready, 1)
                sg.meet()
                end_round(dve, b * ROUNDS + 1 + L)

        @block.tensor
        def _(pe):
            sg = Stages(pe)
            mm = nc.tensor.matmul
            pe.wait_ge(const_in, 16 * 21)
            pe.drain().then_inc(setup, 1)
            pe.wait_ge(setup, 5)

            def ln_transpose(j, zc, width):
                pe.wait_ge(z_ready, zc + 1)
                if zc >= 2:
                    pe.wait_ge(ln_out, zc - 1)
                bank = ps[4 + zc % 2]
                ins = nc.tensor.transpose(bank[:, 0:P], zt[:, zc % 2, 0:P], idf[:, :])
                if width > P:
                    ins = nc.tensor.transpose(bank[0:width - P, P:2 * P], zt[:, zc % 2, P:width], idf[:, :])
                ins.then_inc(z_mm, 1)

            with pe.Fori(0, B) as b:
                pe.wait_ge(onehot_ready, 1)
                for c in range(NC):
                    mm(ps[2 * c][:, :], embs[:, 0:DLO], oneh[:, c * CH:(c + 1) * CH], start=True, stop=True)
                    mm(ps[2 * c + 1][0:DHI, :], embs[:, DLO:D], oneh[:, c * CH:(c + 1) * CH], start=True,
                       stop=True).then_inc(emb_mm, 1)
                end_round(pe, b * ROUNDS)

                with pe.Fori(0, L) as l:
                    sg.restart()
                    pe.wait_ge(glob_ready, 1)
                    for n in range(NB):
                        if n >= 2:
                            pe.wait_ge(qk_res, n - 1)
                            pe.wait_ge(v_res, n - 1)
                        mm(ps[n % 2][:, 0:2 * D], xa[:, blk(n)], wqa[:, 0:2 * D], start=True, stop=False)
                        mm(ps[n % 2][:, 0:2 * D], xb[0:DHI + 1, blk(n)], wqb[0:DHI + 1, 0:2 * D], start=False,
                           stop=True).then_inc(qk_mm, 1)
                        mm(ps[2 + n % 2][:, 0:D], xa[:, blk(n)], wqa[:, 2 * D:3 * D], start=True, stop=False)
                        mm(ps[2 + n % 2][:, 0:D], xb[0:DHI + 1, blk(n)], wqb[0:DHI + 1, 2 * D:3 * D], start=False,
                           stop=True).then_inc(v_mm, 1)
                    pe.wait_ge(nat_ready, NB)
                    for k in range(2 * H):
                        if k >= 4:
                            pe.wait_ge(ev_dve if k % 2 else ev_act, (k - 4) // 2 + 1)
                        for n in range(NB):
                            ins = nc.tensor.transpose(psb[4 + k % 4][0:NPIECE, blk(n)], nat[:, n, k, :], idb[:, :])
                        ins.then_inc(tr_mm, 1)
                    sg.meet()
                    for g in range(2):
                        ins = mm(ps[6 + g][:, 0:HH * VW], onesb[0:1, :], vst[0:1, 0, half(g), :], start=True, stop=True)
                    ins.then_inc(v0_mm, 1)
                    pe.wait_ge(glob_ready, 2)
                    for s in range(-LEAD, U + 18):
                        if s in (-LEAD + 1, -LEAD + 2):
                            c = s + LEAD - 1
                            for h in range(H):
                                ins = mm(ps[2 + c][0:H, :], q0s[0:K_NAT, h, :], stack[0:K_NAT, H + h, c * CH:(c + 1) * CH],
                                         start=h == 0, stop=h == H - 1)
                            ins.then_inc(f_mm, 1)
                        if s == -LEAD + 9:
                            pe.wait_ge(f_norm, 1)
                            for n in range(NB):
                                ins = nc.tensor.transpose(ps[4][:, n * H:(n + 1) * H], pfull[:, 1, blk(n)], idf[0:H, 0:H])
                            ins.then_inc(ft_mm, 1)
                        if s == -LEAD + 15:
                            pe.wait_ge(f2_ready, 1)
                            pe.wait_ge(v0_ready, 1)
                            for g in range(2):
                                for n in range(NB):
                                    for ft in (f1, f2):
                                        ins = mm(ps[6 + g][0:H, 0:HH * VW], ft[:, n, :], vst[:, n, half(g), :],
                                                 start=n == 0 and ft is f1, stop=n == NB - 1 and ft is f2)
                            ins.then_inc(og_mm, 1)
                        if s == -1:
                            pe.wait_ge(og_ready, 1)
                            for i in range(3):
                                mm(ps[4][:, 0:1], og[:, i, 0:DLO], ones[0:H, 0:1], start=i == 0, stop=i == 2)
                            for i in range(3):
                                ins = mm(ps[4][0:DHI, 8:9], og[:, i, DLO:D], ones[0:H, 0:1], start=i == 0, stop=i == 2)
                            ins.then_inc(oc_mm, 1)
                        v = s + LEAD
                        if v < U:
                            n, h = divmod(v, H)
                            win = window(n)
                            if v >= 2:
                                pe.wait_ge(max_done, v - 1)
                            s_ps = ps[v % 2]
                            q = stack[0:K_NAT, h, blk(n)]
                            edges = [(i, m) for i, m in enumerate(win) if m != n]
                            mm(s_ps[:, 0:len(win) * P], q, stack[0:K_NAT, H + h, blk(win[0], len(win))], start=True,
                               stop=False)
                            for i, m in edges:
                                ins = mm(s_ps[:, blk(i)], idb[:, :], bandb[:, 0 if m < n else 1, :], start=False,
                                         stop=(i, m) == edges[-1])
                            ins.then_inc(nat_mm, 1)
                            if h == H - 1:
                                if n >= 3:
                                    pe.wait_ge(at_copied, n - 2)
                                elif n >= 1:
                                    pe.wait_ge(mt_copied, n)
                                for g in range(H):
                                    ins = mm(ps[5][:, g:g + 1], stack[0:K_NAT, g, blk(n)], k0s[0:K_NAT, g:g + 1],
                                             start=True, stop=True)
                                ins.then_inc(sg_mm, 1)
                        for n in range(NB):
                            if s == H * n - 6:
                                pe.wait_ge(dg_ready, n + 1)
                                nc.tensor.transpose(psb[5][0:3 * H, 64:64 + P],
                                                    mcat[:, :, :].rearrange("p i h -> p (i h)"), idb[:, :]).then_inc(mt_mm, 1)
                            if s == H * (n + 1) + 9:
                                if n + 2 < NB:
                                    pe.wait_ge(mt_copied, n + 3)
                                elif n >= 1:
                                    pe.wait_ge(at_copied, n)
                                pe.wait_ge(comb, 2 * n + 2)
                                nc.tensor.transpose(ps[5][:, P:2 * P], att[:, n % 2, 0:DLO], idf[:, :])
                                nc.tensor.transpose(ps[5][0:DHI, 2 * P:3 * P], att[:, n % 2, DLO:D],
                                                    idf[:, :]).then_inc(at_mm, 1)
                        if 0 <= s < U:
                            n, h = divmod(s, H)
                            if h == 0:
                                pe.wait_ge(m_in[n % 2], 48 * (n // 2 + 1))
                            if s >= 3:
                                pe.wait_ge(p1_ready, s - 2)
                            elif s == 2:
                                pe.wait_ge(oc_copied, 1)
                            win = window(n)
                            for i, m in enumerate(win):
                                ins = mm(ps[2 + s % 3][:, blk(i)], stack[0:K_ALL, H + h, blk(m)],
                                         stack[0:K_ALL, h, blk(n)], start=True, stop=m == n)
                                if m != n:
                                    ins = mm(ps[2 + s % 3][:, blk(i)], idb[:, :], bandb[:, 1 if m < n else 0, :],
                                             start=False, stop=True)
                            ins.then_inc(t_mm, 1)
                        w = s - PV_LAG
                        if 0 <= w < U:
                            n, h = divmod(w, H)
                            g, i = divmod(h, HH)
                            if i == 0 and n >= 1:
                                pe.wait_ge(comb, 2 * (n - 1) + g + 1)
                            if w % 4 == 3:
                                pe.wait_ge(p2_dve, w // 4 + 1)
                            else:
                                pe.wait_ge(p2_pool, w - w // 4 + (0 if w % 4 == 3 else 1))
                            win = window(n)
                            out_ps = ps[6 + g][:, i * VW:(i + 1) * VW]
                            for a, m in enumerate(win):
                                for pt in (p1, p2):
                                    ins = mm(out_ps, pt[:, w % RING, blk(a)], vst[:, m, h, :],
                                             start=a == 0 and pt is p1, stop=a == len(win) - 1 and pt is p2)
                            ins.then_inc(pv_mm, 1)
                    sg.meet()
                    pe.wait_ge(wrest_in, 128)
                    for kind, i in SEQ_C:
                        if kind == "y":
                            n = i % NB
                            if i >= 4:
                                pe.wait_ge(z_ready, i - 3)
                            y = ps[i % 4][:, 0:D]
                            if i < NB:
                                mm(y, ata[:, blk(n)], woa[:, :], start=True, stop=False)
                                mm(y, atb[0:DHI + 1, blk(n)], wob[0:DHI + 1, :], start=False, stop=False)
                                mm(ps[i % 4][:, 0:P], xa[:, blk(n)], idf[:, :], start=False, stop=False)
                                mm(ps[i % 4][:, P:D], xb[0:DHI, blk(n)], idf[0:DHI, 0:DHI], start=False,
                                   stop=True).then_inc(y_mm, 1)
                            else:
                                c = n // BPC
                                pe.wait_ge(h_relu, (c + 1) * (FF // P))
                                mm(y, xb[0:DHI + 1, blk(n)], rwb[0:DHI + 1, :], start=True, stop=False)
                                mm(ps[i % 4][:, 0:P], xa[:, blk(n)], idf[:, :], start=False, stop=False)
                                for m in range(FF // P):
                                    ins = mm(y, hid[:, m, blk(n % BPC)], w2s[:, m, :], start=False, stop=m == FF // P - 1)
                                ins.then_inc(y_mm, 1)
                        if kind == "tr":
                            ln_transpose(i, i, D)
                        if kind == "hid":
                            c, m = divmod(i, FF // P)
                            pe.wait_ge(ln_out, (c + 1) * BPC)
                            if i >= 2:
                                pe.wait_ge(h_relu, i - 1)
                            cs = slice(c * CH, (c + 1) * CH)
                            mm(ps[6 + i % 2][:, :], w1a[:, m * P:(m + 1) * P], xa[:, cs], start=True, stop=False)
                            mm(ps[6 + i % 2][:, :], w1b[0:DHI + 1, m * P:(m + 1) * P], xb[0:DHI + 1, cs], start=False,
                               stop=True).then_inc(h_mm, 1)
                    sg.meet()
                    end_round(pe, b * ROUNDS + 1 + l)

                sg.restart()
                for n in range(NB + 2):
                    if n < NB:
                        if n >= 4:
                            pe.wait_ge(z_ready, n - 3)
                        mm(ps[n % 4][:, 0:P], xa[:, blk(n)], idf[:, :], start=True, stop=True)
                        mm(ps[n % 4][:, P:D], xb[0:DHI, blk(n)], idf[0:DHI, 0:DHI], start=True, stop=True).then_inc(y_mm, 1)
                    if n >= 2:
                        ln_transpose(n - 2, n - 2, D)
                sg.meet()
                for n in range(NB + 2):
                    if n < NB:
                        if n >= 4:
                            pe.wait_ge(y_stats, UNIT_X[n - 4] + 1)
                        mm(ps[n % 4][:, 0:DM], xa[:, blk(n)], wca[:, :], start=True, stop=False)
                        mm(ps[n % 4][:, 0:DM], xb[0:DHI + 1, blk(n)], wcb[0:DHI + 1, :], start=False,
                           stop=True).then_inc(y_mm, 1)
                    if n >= 2:
                        ln_transpose(0, NB + n - 2, DM)
                sg.meet()
                pe.wait_ge(s_ready, 1)
                for n in range(NB + 2):
                    if n < NB:
                        if n >= 4:
                            pe.wait_ge(z_ready, 2 * NB + n - 3)
                        y = ps[n % 4][:, 0:DM]
                        for k in range(KC):
                            mm(y, xn[:, n * P + k:(n + 1) * P + k], diag[:, k, :], start=k == 0, stop=False)
                        mm(y, st[:, blk(n)], wos[:, :], start=False, stop=False)
                        mm(y, ones[0:2, :], bo2s[:, :], start=False, stop=True).then_inc(y_mm, 1)
                    if n >= 2:
                        ln_transpose(0, 2 * NB + n - 2, DM)
                sg.meet()
                for i in range(NC * 2):
                    c, m = divmod(i, 2)
                    if i >= 2:
                        pe.wait_ge(g_ready, i - 1)
                    mm(ps[6 + i % 2][:, :], aw1s[:, m * P:(m + 1) * P], ht[:, c * CH:(c + 1) * CH], start=True,
                       stop=True).then_inc(g_mm, 1)
                pe.wait_ge(g_ready, 2 * NC)
                for n in range(NB + 2):
                    if n < NB:
                        if n >= 4:
                            pe.wait_ge(z_ready, 3 * NB + n - 3)
                        y = ps[n % 4][:, 0:DM]
                        for m in range(2):
                            mm(y, gl[:, m * T + n * P:m * T + (n + 1) * P], aw2s[:, m, :], start=m == 0, stop=False)
                        mm(y, ones[0:1, :], ab2s[:, :], start=False, stop=True).then_inc(y_mm, 1)
                    if n >= 2:
                        ln_transpose(0, 3 * NB + n - 2, DM)
                sg.meet()
                for n in range(NB):
                    mm(ps[0][:, n * E:(n + 1) * E], xm[:, blk(n)], wgs[:, :], start=True, stop=False)
                    ins = mm(ps[0][:, n * E:(n + 1) * E], ones[0:1, :], bgs[:, :], start=False, stop=True)
                ins.then_inc(lg_mm, 1)
                pe.wait_ge(x_lo, 1)
                for k in range(E * NC + 1):
                    if k < E * NC:
                        e, c = divmod(k, NC)
                        pe.wait_ge(w_split, e + 1)
                        for m in range(EH // P):
                            i = k * (EH // P) + m
                            if i >= 4:
                                pe.wait_ge(e_relu, i - 3)
                            for a, b_ in PARTS:
                                ins = mm(ps[4 + i % 4][:, :], w1r[:, e % 2, a, m * P:(m + 1) * P],
                                         xmr[:, b_, c * CH:(c + 1) * CH], start=(a, b_) == PARTS[0], stop=(a, b_) == PARTS[-1])
                            ins.then_inc(e_mm, 1)
                    if k == 0:
                        pe.wait_ge(sel_ready, 1)
                        for n in range(NB):
                            ins = nc.tensor.transpose(ps[2 + n // BPC][0:E, blk(n % BPC)], gt[:, 5, n, :], idf[:, :])
                        ins.then_inc(st_mm, 1)
                    if k >= 1:
                        j = k - 1
                        e, c = divmod(j, NC)
                        if j == 0:
                            pe.wait_ge(st_copied, 1)
                        else:
                            pe.wait_ge(e_split, k * (EH // P))
                        if j >= 2:
                            pe.wait_ge(ey_masked, j - 1)
                            pe.wait_ge(mask_copied, j - 1)
                        mm(ps[2 + j % 2][:, :], rowe[:, e, :], selt[:, c * CH:(c + 1) * CH], start=True,
                           stop=True).then_inc(mask_mm, 1)
                        if j == 0:
                            pe.wait_ge(e_split, k * (EH // P))
                        for m in range(EH // P):
                            for a, b_ in PARTS:
                                ins = mm(ps[j % 2][:, :], w2r[:, e % 2, a, m, :], ehr[:, j % 2, b_, m, :],
                                         start=m == 0 and (a, b_) == PARTS[0],
                                         stop=m == EH // P - 1 and (a, b_) == PARTS[-1])
                        ins.then_inc(ey_mm, 1)
                for c in range(NC):
                    pe.wait_ge(acc_done, NC * (E - 2) + 1 + c)
                    for n in range(BPC):
                        ins = nc.tensor.transpose(ps[4 + c][:, blk(n)], acc[:, blk(c * BPC + n)], idf[:, :])
                    ins.then_inc(o_mm, 1)
                sg.meet()
                end_round(pe, b * ROUNDS + 1 + L)


def _seq_c():
    seq = []

    def y(i):
        seq.append(("y", i))
        if i >= 1:
            seq.append(("z", i - 1))

    for i in range(4):
        y(i)
    for i in range(4):
        seq.append(("tr", i) if i < 3 else ("z", 3))
        if i < 3:
            y(4 + i)
    seq = [s for k, s in enumerate(seq) if s not in seq[:k]]
    seq.append(("tr", 3))
    y(7)
    seq.append(("z", 7))
    seq += [("hid", m) for m in range(3)] + [("tr", 4), ("tr", 5)] + [("hid", m) for m in range(3, 6)]
    seq += [("tr", 6), ("tr", 7)]
    seq += [("y", 8), ("y", 9), ("z", 8), ("y", 10), ("z", 9), ("y", 11), ("z", 10), ("z", 11)]
    seq += [("hid", m) for m in range(6, 9)] + [("tr", 8), ("tr", 9)] + [("hid", m) for m in range(9, 12)]
    seq += [("tr", 10), ("tr", 11)]
    seq += [("y", 12), ("y", 13), ("z", 12), ("y", 14), ("z", 13), ("tr", 12), ("y", 15), ("z", 14), ("tr", 13),
            ("z", 15), ("tr", 14), ("tr", 15)]
    return seq


SEQ_C = _seq_c()


def _units():
    order = [u for k in range(NB + 1) for u in ([("h", k)] if k < NB else []) + ([("x", k - 1)] if k else [])]
    return ([NB + order.index((kind, n)) for n in range(NB)] for kind in "hx")


UNIT_H, UNIT_X = _units()


_OUTS = [((2, 1024, 128), 'float32')]


def kernel(**inputs):
    import numpy as _np
    import concourse.bacc as _bacc
    from concourse import mybir as _mybir
    from concourse.bass_utils import run_bass_kernel_spmd as _run

    g = {k: _np.asarray(v) for k, v in inputs.items()}
    t = "L0_tok_"
    a = "L0_attn_"
    f = "L0_ffn_"

    def cat(ws, bs):
        w = _np.concatenate([_np.transpose(g[t + n], (0, 2, 1)) for n in ws], axis=2)
        r = _np.concatenate([g[t + n][:, None, :] for n in bs], axis=2)
        return _np.concatenate([w, r], axis=1)

    def row(v):
        return v.reshape(1, -1)

    def columns(*vs):
        return _np.stack(vs, axis=-1)

    p, q = _np.arange(P)[:, None], _np.arange(P)[None, :]
    low = _np.where(q < p, BAND_OUT, 0.0).astype(_np.float32)
    high = _np.where(q > p, BAND_OUT, 0.0).astype(_np.float32)
    cols = _np.zeros((P, 4), _np.float32)
    cols[:, 0] = _np.arange(P)
    cols[0:NPIECE, 1] = 1.0
    cols[R_FULL:R_MAX, 2] = 1.0
    cols[:, 3] = -0.5
    eye = _np.eye(D, dtype=_np.float32)
    arrays = {
        "x": g["x"], "pad": g["mask_BS_b0_1"].view(_np.int32), "emb": g[t + "emb"],
        "wqkv": cat(["Wq", "Wk", "Wv"], ["bq", "bk", "bv"]), "wo": cat(["Wo"], ["bo"]), "w1": cat(["W1"], ["b1"]),
        "w2": _np.transpose(g[t + "W2"], (0, 2, 1)),
        "rw": _np.stack([_np.concatenate([eye, g[t + "b2"][l][None, :]]) for l in range(L)]),
        "lnl": columns(*(g[t + n] for n in ("g1", "beta1", "g2", "beta2"))),
        "lnf": columns(g[t + "gf"], g[t + "betaf"]),
        "wc": _np.concatenate([g[t + "Wc"].T, row(g[t + "bc"])]),
        "ident": _np.eye(P, dtype=_np.float32), "band": _np.stack([low, high], axis=1), "cols": cols,
        "decay": g[a + "decay_logit"].reshape(-1, 1), "convw": g[a + "conv_w"].reshape(DM, KC),
        "wout": g[a + "W_out"].T, "bo2": _np.stack([g[a + "b_out"], g[a + "conv_b"]]),
        "ln12": columns(*(g[a + n] for n in ("ln1_g", "ln1_b", "ln2_g", "ln2_b"))),
        "aw1": g[a + "W1"].T, "ab1": g[a + "b1"].reshape(2, P).T,
        "aw2": g[a + "W2"].T.reshape(2, P, DM).transpose(1, 0, 2), "ab2": row(g[a + "b2"]),
        "wg": g[f + "Wg"], "bg": row(g[f + "bg"]),
        "mw1": g[f + "W1"].transpose(1, 0, 2), "mb1": g[f + "b1"].reshape(E, EH // P, P).transpose(2, 0, 1),
        "mw2": g[f + "W2"].reshape(E, EH // P, P, DM).transpose(2, 0, 1, 3), "mb2": g[f + "b2"].T,
        "qrows": _np.repeat([[1], [1], [0], [0]], H * T, axis=1).astype(_mybir.dt.np(_mybir.dt.bfloat16)),
        "krows": _np.ones((3, H * T), _mybir.dt.np(_mybir.dt.bfloat16)),
    }
    nc = _bacc.Bacc("TRN2", target_bir_lowering=False, num_devices=1)
    held, args = {}, []
    for name, v in arrays.items():
        v = _np.ascontiguousarray(v)
        held[f"in_{name}"] = v
        args.append(nc.dram_tensor(f"in_{name}", v.shape, _mybir.dt.from_np(v.dtype), kind="ExternalInput").ap())
    for i, (shape, dtype) in enumerate(_OUTS):
        args.append(nc.dram_tensor(f"out_{i}", shape, _mybir.dt.from_np(_np.dtype(dtype)), kind="ExternalOutput").ap())
    program(nc, *args)
    r = _run(nc, [held], core_ids=[0])
    return r.results[0]["out_0"]
```

```python
from contextlib import ExitStack

import numpy as np

import concourse.bass as bass
from concourse import mybir

ALU = mybir.AluOpType
ACT = mybir.ActivationFunctionType
AX = mybir.AxisListType
F32 = mybir.dt.float32
BF16 = mybir.dt.bfloat16
F16 = mybir.dt.float16
F32R = mybir.dt.float32r
I32 = mybir.dt.int32
U8 = mybir.dt.uint8

P = 128
B, T = 2, 1024
NB = T // P
CH = 512
NC = T // CH
BPC = CH // P
L, D, H, FF = 2, 192, 12, 768
DH = D // H
DLO, DHI = P, D - P
DM = 128
HID = 256
KC = 5
E, EH = 8, 512
EPS = 1e-5
BAND_OUT = -1e9
KB_HI, KB_LO = -9984.0, -16.0

Q_ROWS = ((0, 16, 32), (48, 64), (80,))
K_ROWS = ((0, 48, 80), (16, 64), (32,))
NPIECE = 96
R_BIAS = 96
R_FULL = 98
R_MAX = 100
K_NAT = 100
K_ALL = 103
VW = 3 * DH + 1
HH = H // 2
LEAD = 24
PV_LAG = 4
PARTS = ((0, 0), (0, 1), (1, 0))
SHARE = 6
RING = 6
U = NB * H
ROW = U - LEAD


def window(n):
    return [m for m in (n - 1, n, n + 1) if 0 <= m < NB]


def program(nc, x, pad, emb, wqkv, wo, w1, w2, rw, lnl, lnf, wc, ident, band, cols, decay, convw, wout, bo2,
            ln12, aw1, ab1, aw2, ab2, wg, bg, mw1, mb1, mw2, mb2, qrows, krows, out):
    with ExitStack() as ctx:
        def sb(name, shape, dt):
            return ctx.enter_context(nc.sbuf_tensor(name, shape, dt))

        work_sems = []

        def sem(name, work=True):
            s = ctx.enter_context(nc.semaphore(name))
            if work:
                work_sems.append(s)
            return s

        ps = [ctx.enter_context(nc.psum_tensor(f"bank{i}", [P, CH], F32)) for i in range(8)]
        psb = [p[:, :].bitcast(BF16) for p in ps]

        vst = sb("vst", [P, NB, H, VW], BF16)
        xa = sb("xa", [P, T], F32)
        xb = sb("xb", [P, T], F32)
        ata = sb("ata", [P, T], F32)
        atb = sb("atb", [P, T], F32)
        wqa = sb("wqa", [P, 3 * D], F32)
        wqb = sb("wqb", [P, 3 * D], F32)
        woa = sb("woa", [P, D], F32)
        wob = sb("wob", [P, D], F32)
        w1a = sb("w1a", [P, FF], F32)
        w1b = sb("w1b", [P, FF], F32)
        w2s = sb("w2s", [P, FF // P, D], F32)
        rwb = sb("rwb", [P, D], F32)
        lna = sb("lna", [P, 4], F32)
        lnb = sb("lnb", [P, 4], F32)
        lfa = sb("lfa", [P, 2], F32)
        lfb = sb("lfb", [P, 2], F32)
        wca = sb("wca", [P, DM], F32)
        wcb = sb("wcb", [P, DM], F32)
        embs = sb("embs", [P, D], F32)
        idf = sb("idf", [P, P], F32)
        idb = sb("idb", [P, P], BF16)
        bandf = sb("bandf", [P, 2, P], F32)
        bandb = sb("bandb", [P, 2, P], BF16)
        colc = sb("colc", [P, 4], F32)
        bm = sb("bm", [P, D], F32)
        ones = sb("ones", [P, P], F32)
        onesb = sb("onesb", [P, P], BF16)
        epst = sb("epst", [P, 1], F32)
        kbrow = sb("kbrow", [1, 4, T], BF16)
        padu = sb("padu", [1, T // 4], I32)
        res = sb("res", [P, 2, 2 * D], F32)
        resv = sb("resv", [P, 2, D], F32)
        k0s = sb("k0s", [P, H], BF16)
        q0s = sb("q0s", [P, H, H], BF16)
        v0b = sb("v0b", [P, H, DH], F32)
        v0t = sb("v0t", [P, 2, H, DH], F32)
        nmx = sb("nmx", [P, 3, H], F32)
        nm = sb("nm", [P, H], F32)
        nmr = sb("nmr", [P, H], F32)
        mcat = sb("mcat", [P, 3, H], BF16)
        mtr = sb("mtr", [3 * H, 2, P], BF16)
        dg0 = sb("dg0", [P, 4, H], F32)
        eg = sb("eg", [P, 4, H], F32)
        pvt = sb("pvt", [P, 2, 4, HH, DH], F32)
        den = sb("den", [P, 2, 2, HH], F32)
        att = sb("att", [P, 2, D], F32)
        fst = sb("fst", [H, 4], F32)
        f1 = sb("f1", [P, NB, H], F16)
        f2 = sb("f2", [P, NB, H], F16)
        og = sb("og", [H, 3, D], F32)
        stt_ = sb("bnst", [P, 4, 6], F32)
        mv = sb("mv", [P, 4, 2], F32)
        ve = sb("ve", [P, 4], F32)
        rstd = sb("rstd", [P, 4], F32)
        cst = sb("cst", [P, NB, 6], F32)
        cmv = sb("cmv", [P, 2, NB, 2], F32)
        cve = sb("cve", [P, 2, NB], F32)
        crs = sb("crs", [P, 2, NB], F32)
        zt = sb("zt", [P, 2, D], F32)
        dcol = sb("dcol", [P, 4], F32)
        cw = sb("cw", [P, KC], F32)
        diag = sb("diag", [P, KC, DM], F32)
        wos = sb("wos", [P, DM], F32)
        bo2s = sb("bo2s", [2, DM], F32)
        l12 = sb("l12", [P, 4], F32)
        aw1s = sb("aw1s", [P, HID], F32)
        ab1s = sb("ab1s", [P, 2], F32)
        aw2s = sb("aw2s", [P, 2, DM], F32)
        ab2s = sb("ab2s", [1, DM], F32)
        wgs = sb("wgs", [P, E], F32)
        bgs = sb("bgs", [1, E], F32)
        mb1s = sb("mb1s", [P, E, EH // P], F32)
        mb2s = sb("mb2s", [P, E], F32)
        rowe = sb("rowe", [E, E, P], BF16)
        gt = sb("gt", [P, 6, NB, E], F32)
        gs = sb("gs", [P, 4, NB], F32)
        selt = sb("selt", [E, T], BF16)

        xn = sb("xn", [P, T + KC - 1], F32)

        with ExitStack() as layers:
            def lsb(name, shape, dt):
                return layers.enter_context(nc.sbuf_tensor(name, shape, dt))

            stack = lsb("stack", [P, 2 * H, T], BF16)
            nat = lsb("nat", [P, NB, 2 * H, NPIECE], BF16)
            p32 = lsb("p32", [P, RING, 3 * P], F32)
            p1 = lsb("p1", [P, RING, 3 * P], F16)
            p2 = lsb("p2", [P, RING, 3 * P], F16)
            hid = lsb("hid", [P, FF // P, CH], F32)
        h0 = sb("h0", [P, T], F32)
        xm = sb("xm", [P, T], F32)
        acc = sb("acc", [P, T], F32)
        mw1s = sb("mw1s", [P, E, EH], F32)
        mw2s = sb("mw2s", [P, E, EH // P, DM], F32)
        w1r = sb("w1r", [P, 2, 2, EH], F32R)
        w2r = sb("w2r", [P, 2, 2, EH // P, DM], F32R)
        with ExitStack() as retention:
            def rsb(name, width):
                return retention.enter_context(nc.sbuf_tensor(name, [P, width], F32))[:, :]

            x1 = rsb("x1", T)
            st = rsb("st", T)
            d1 = rsb("d1", T)
            gl = rsb("gl", 2 * T)
            ht = rsb("ht", T)
        ehr = sb("ehr", [P, 2, 2, EH // P, CH], F32R)
        xmr = sb("xmr", [P, 2, T], F32R)
        eh32 = sb("eh32", [P, 4, CH], F32)
        ey = sb("ey", [P, 2, CH], F32)
        mask = sb("mask", [P, 2, CH], BF16)
        idsi = hid[:, 0:2, :].rearrange("p a b -> p (a b)").bitcast(I32)
        oneh = hid[:, 2:4, :].rearrange("p a b -> p (a b)")
        pfull = hid[0:H, 0:4, :].rearrange("p (i a) b -> p i (a b)", i=2)
        padw = (ata[0:1, :], atb[0:1, :])

        arrive = sem("arrive", False)
        go = sem("go", False)
        spare = sem("spare", False)
        const_in = sem("const_in", False)
        setup = sem("setup", False)
        stage = sem("stage")
        ids_in = sem("ids_in")
        pad_in = sem("pad_in")
        kb_out = sem("kb_out")
        rows_in = sem("rows_in")
        onehot_ready = sem("onehot_ready")
        emb_mm = sem("emb_mm")
        emb_cp = sem("emb_cp")
        dve_own = sem("dve_own")
        act_own = sem("act_own")
        pool_own = sem("pool_own")
        wqkv_in = sem("wqkv_in")
        wrest_in = sem("wrest_in")
        qk_mm = sem("qk_mm")
        v_mm = sem("v_mm")
        qk_p1 = sem("qk_p1")
        qk_res = sem("qk_res")
        qk_p2 = sem("qk_p2")
        v_p1 = sem("v_p1")
        v_res = sem("v_res")
        v_p2 = sem("v_p2")
        nat_ready = sem("nat_ready")
        tr_mm = sem("tr_mm")
        ev_act = sem("ev_act")
        ev_dve = sem("ev_dve")
        glob_ready = sem("glob_ready")
        v0_mm = sem("v0_mm")
        v0_ready = sem("v0_ready")
        nat_mm = sem("nat_mm")
        max_done = sem("max_done")
        sg_mm = sem("sg_mm")
        m_ready = sem("m_ready")
        mt_mm = sem("mt_mm")
        mt_copied = sem("mt_copied")
        m_in = [sem(f"m_in{i}") for i in range(2)]
        dg_ready = sem("dg_ready")
        eg_ready = sem("eg_ready")
        t_mm = sem("t_mm")
        p32_ready = sem("p32_ready")
        p1_ready = sem("p1_ready")
        p2_pool = sem("p2_pool")
        p2_dve = sem("p2_dve")
        pv_mm = sem("pv_mm")
        pvg_ready = sem("pvg_ready")
        comb = sem("comb")
        at_mm = sem("at_mm")
        at_copied = sem("at_copied")
        f_mm = sem("f_mm")
        f_max = sem("f_max")
        f_exp = sem("f_exp")
        f_norm = sem("f_norm")
        ft_mm = sem("ft_mm")
        f1_ready = sem("f1_ready")
        f2_ready = sem("f2_ready")
        og_mm = sem("og_mm")
        og_ready = sem("og_ready")
        oc_mm = sem("oc_mm")
        oc_copied = sem("oc_copied")
        y_mm = sem("y_mm")
        y_stats = sem("y_stats")
        y_rstd = sem("y_rstd")
        z_ready = sem("z_ready")
        z_mm = sem("z_mm")
        ln_out = sem("ln_out")
        h_mm = sem("h_mm")
        h_relu = sem("h_relu")
        h0_kept = sem("h0_kept")
        h_sums = sem("h_sums")
        mlp_mm = sem("mlp_mm")
        c_stats = sem("c_stats")
        c_rstd = sem("c_rstd")
        s_ready = sem("s_ready")
        g_mm = sem("g_mm")
        g_ready = sem("g_ready")
        lg_mm = sem("lg_mm")
        lg_sub = sem("lg_sub")
        lg_exp = sem("lg_exp")
        sel_ready = sem("sel_ready")
        st_mm = sem("st_mm")
        st_copied = sem("st_copied")
        ey_masked = sem("ey_masked")
        mask_mm = sem("mask_mm")
        mask_copied = sem("mask_copied")
        o_mm = sem("o_mm")
        e_mm = sem("e_mm")
        e_relu = sem("e_relu")
        e_split = sem("e_split")
        w1_split = sem("w1_split")
        w2_split = sem("w2_split")
        x_hi = sem("x_hi")
        x_lo = sem("x_lo")
        ey_mm = sem("ey_mm")
        acc_done = sem("acc_done")
        o_ready = sem("o_ready")
        o_out = sem("o_out")
        mw_in = sem("mw_in")

        first, last = min(s.num for s in work_sems), max(s.num for s in work_sems)
        assert last - first + 1 == len(work_sems)
        ROUNDS = 1 + L + 1

        class Link:

            def __init__(self, eng, own):
                self.eng, self.own, self.count = eng, own, 0

            def link(self, ins):
                self.count += 1
                ins.then_inc(self.own, 1)
                self.eng.wait_ge(self.own, self.count)

            def mark(self, ins):
                self.count += 1
                ins.then_inc(self.own, 1)
                return self.count

            def restart(self):
                self.count = 0

        class Stages:

            def __init__(self, eng):
                self.eng, self.count = eng, 0

            def meet(self):
                self.arrive()
                self.pass_()

            def arrive(self):
                self.count += 1
                self.eng.drain().then_inc(stage, 1)

            def pass_(self):
                self.eng.wait_ge(stage, 4 * self.count)

            def restart(self):
                self.count = 0

        def end_round(eng, r, clears=False):
            eng.drain().then_inc(arrive, 1)
            eng.wait_ge(arrive, 5 * r + 5)
            eng.sem_inc(spare, 1)
            if clears:
                eng.sem_clear(range(first, last + 1))
            eng.drain().then_inc(go, 1)
            eng.wait_ge(go, 5 * r + 5)
            eng.sem_inc(spare, 1)

        def blk(n, k=1):
            return slice(n * P, (n + k) * P)

        def nat_bank(v):
            return ps[v % 4] if v < LEAD else ps[v % 2]

        def half(b):
            return slice(b * HH, (b + 1) * HH)

        consts = [
            (idf[:, :], ident), (bandf[:, :, :], band), (colc[:, :], cols), (embs[:, :], emb),
            (lfa[:, :], lnf[0:DLO, :]), (lfb[0:DHI, :], lnf[DLO:D, :]),
            (wca[:, :], wc[0:DLO, :]), (wcb[0:DHI + 1, :], wc[DLO:D + 1, :]),
            (dcol[:, 0:1], decay), (cw[:, :], convw), (wos[:, :], wout), (bo2s[:, :], bo2),
            (l12[:, :], ln12), (aw1s[:, :], aw1), (ab1s[:, :], ab1), (aw2s[:, :, :], aw2), (ab2s[:, :], ab2),
            (wgs[:, :], wg), (bgs[:, :], bg), (mb1s[:, :, :], mb1), (mb2s[:, :], mb2),
        ]
        early = 10

        block = ctx.enter_context(nc.Block())

        @block.sync
        def _(sp):
            def load_qkv(l):
                w = wqkv[bass.ds(l, 1), :, :].rearrange("o k n -> (o k) n")
                sp.dma_start(wqa[:, :], w[0:DLO, :]).then_inc(wqkv_in, 16)
                sp.dma_start(wqb[0:DHI + 1, :], w[DLO:D + 1, :]).then_inc(wqkv_in, 16)

            def load_rest(l):
                o = wo[bass.ds(l, 1), :, :].rearrange("o k n -> (o k) n")
                a = w1[bass.ds(l, 1), :, :].rearrange("o k n -> (o k) n")
                b = w2[bass.ds(l, 1), :, :].rearrange("o k n -> (o k) n")
                r = rw[bass.ds(l, 1), :, :].rearrange("o k n -> (o k) n")
                g = lnl[bass.ds(l, 1), :, :].rearrange("o k n -> (o k) n")
                for dst, src in ((woa[:, :], o[0:DLO, :]), (wob[0:DHI + 1, :], o[DLO:D + 1, :]),
                                 (w1a[:, :], a[0:DLO, :]), (w1b[0:DHI + 1, :], a[DLO:D + 1, :]),
                                 (w2s[:, :, :], b.rearrange("(j p) n -> p j n", p=P)),
                                 (rwb[0:DHI + 1, :], r[DLO:D + 1, :]),
                                 (lna[:, :], g[0:DLO, :]), (lnb[0:DHI, :], g[DLO:D, :])):
                    sp.dma_start(dst, src).then_inc(wrest_in, 16)

            for dst, src in consts[:early]:
                sp.dma_start(dst, src).then_inc(const_in, 16)
            sp.wait_ge(const_in, 16 * len(consts))
            sp.sem_inc(setup, 1)
            sp.wait_ge(setup, 5)

            with sp.Fori(0, B) as b:
                sp.dma_start(idsi, x[bass.ds(b, 1), :].to_broadcast([P, T])).then_inc(ids_in, 16)
                sp.dma_start(padu[:, :], pad[bass.ds(b, 1), :]).then_inc(pad_in, 16)
                load_qkv(0)
                sp.wait_ge(ids_in, 16)
                sp.wait_ge(wqkv_in, 32)
                end_round(sp, b * ROUNDS)

                with sp.Fori(0, L) as l:
                    sp.dma_start(stack[R_BIAS:R_MAX, 0:H, :].rearrange("p h t -> p (h t)"), qrows).then_inc(rows_in, 16)
                    sp.dma_start(stack[R_MAX:K_ALL, H:2 * H, :].rearrange("p h t -> p (h t)"), krows).then_inc(rows_in, 16)
                    for h in range(H):
                        sp.dma_start(stack[R_BIAS:R_MAX, H + h, :], kbrow[0:1, :, :]).then_inc(kb_out, 16)
                    load_rest(l)
                    for n in range(NB):
                        sp.wait_ge(mt_copied, n + 1)
                        for i in range(3):
                            sp.dma_start(stack[R_MAX + i:R_MAX + i + 1, 0:H, blk(n)],
                                         mtr[i * H:(i + 1) * H, n % 2, :]).then_inc(m_in[n % 2], 16)
                    sp.wait_ge(m_in[0], 48 * NB // 2)
                    sp.wait_ge(m_in[1], 48 * NB // 2)
                    load_qkv(1 - l)
                    sp.wait_ge(wqkv_in, 32)
                    sp.wait_ge(wrest_in, 128)
                    end_round(sp, b * ROUNDS + 1 + l)

                sp.dma_start(mw1s[:, :, :], mw1).then_inc(mw_in, 16)
                sp.dma_start(mw2s[:, :, :, :], mw2).then_inc(mw_in, 16)
                for n in range(NB):
                    sp.wait_ge(o_ready, n + 1)
                    sp.dma_start(out[bass.ds(b, 1), blk(n), :].rearrange("o p m -> (o p) m"),
                                 h0[:, blk(n)]).then_inc(o_out, 16)
                sp.wait_ge(o_out, 16 * NB)
                sp.wait_ge(mw_in, 32)
                end_round(sp, b * ROUNDS + 1 + L)

        @block.gpsimd
        def _(pool):
            ch = Link(pool, pool_own)
            sg = Stages(pool)
            for t, value in ((xb[DHI:DHI + 1, :], 1.0), (atb[DHI:DHI + 1, :], 1.0), (ones[:, :], 1.0), (onesb[:, :], 1.0),
                             (q0s[:, :, :], 0.0), (epst[:, :], EPS), (xn[:, :], 0.0), (bm[:, :], 1.0),
                             (vst[:, :, :, 3 * DH:VW], 1.0)):
                ch.link(nc.gpsimd.memset(t, value))
            ch.link(nc.gpsimd.affine_select(out=bm[:, :], in_=bm[:, :], compare_op=ALU.is_ge, fill=0.0, base=0,
                                            pattern=[[1, D]], channel_multiplier=-DH))
            ch.link(nc.gpsimd.affine_select(out=bm[:, :], in_=bm[:, :], compare_op=ALU.is_ge, fill=0.0, base=DH - 1,
                                            pattern=[[-1, D]], channel_multiplier=DH))
            pool.sem_clear(pool_own)
            pool.wait_ge(const_in, 16 * len(consts))
            pool.drain().then_inc(setup, 1)
            pool.wait_ge(setup, 5)

            def rstd_of(j):
                pool.wait_ge(y_stats, j + 1)
                ch.link(nc.gpsimd.tensor_tensor(ve[:, j % 4:j % 4 + 1], mv[:, j % 4, 1:2], epst[:, :], ALU.add))
                nc.gpsimd.tensor_tensor(rstd[:, j % 4:j % 4 + 1], ve[:, j % 4:j % 4 + 1], colc[:, 3:4],
                                        ALU.pow).then_inc(y_rstd, 1)

            def rstd_of_half(j, w, c):
                cb = slice(c * BPC, (c + 1) * BPC)
                pool.wait_ge(c_stats, j + 1)
                ch.link(nc.gpsimd.tensor_tensor(cve[:, w, cb], cmv[:, w, cb, 1], epst[:, :].to_broadcast([P, BPC]), ALU.add))
                nc.gpsimd.tensor_tensor(crs[:, w, cb], cve[:, w, cb], colc[:, 3:4].to_broadcast([P, BPC]),
                                        ALU.pow).then_inc(c_rstd, 1)

            def split_weights(e):
                for w, wr, used, count, ready in (
                        (mw1s[:, e, :], w1r[:, e % 2, :, :], e_mm, NC * (EH // P) * (e - 1), w1_split),
                        (mw2s[:, e, :, :].rearrange("p j m -> p (j m)"),
                         w2r[:, e % 2, :, :, :].rearrange("p a j m -> p a (j m)"), ey_mm, NC * (e - 1), w2_split)):
                    if e >= 2:
                        pool.wait_ge(used, count)
                    ch.link(nc.gpsimd.tensor_copy(wr[:, 0, :], w))
                    nc.gpsimd.tensor_tensor(wr[:, 1, :], w, wr[:, 0, :].bitcast(F32), ALU.subtract).then_inc(ready, 1)

            with pool.Fori(0, B) as b:
                end_round(pool, b * ROUNDS, True)

                with pool.Fori(0, L) as l:
                    ch.restart()
                    sg.restart()
                    sg.meet()
                    for s in range(U + 18):
                        u = s - 1
                        if 0 <= u < U and u % SHARE != SHARE - 1:
                            pool.wait_ge(p1_ready, u + 1)
                            if u >= RING:
                                pool.wait_ge(pv_mm, u - RING + 1)
                            w = len(window(u // H)) * P
                            nc.gpsimd.tensor_tensor(p2[:, u % RING, 0:w], p32[:, u % RING, 0:w], p1[:, u % RING, 0:w],
                                                    ALU.subtract).then_inc(p2_pool, 1)
                        n, r = divmod(s, H)
                        for g, at in ((0, 4), (1, 10)):
                            if r == at and n < NB:
                                k = 2 * n + g
                                if g == 0:
                                    pool.wait_ge(eg_ready, n + 1)
                                if k == 0:
                                    pool.wait_ge(v0_ready, 1)
                                if k >= 2:
                                    pool.wait_ge(comb, k - 1)
                                nc.gpsimd.tensor_tensor(
                                    pvt[:, g, 0, :, :], v0b[:, half(g), :],
                                    eg[:, n % 4, half(g)].unsqueeze(2).to_broadcast([P, HH, DH]),
                                    ALU.mult).then_inc(pvg_ready, 1)
                    sg.meet()
                    for j in range(2 * NB):
                        rstd_of(j)
                    sg.meet()
                    end_round(pool, b * ROUNDS + 1 + l, True)

                ch.restart()
                sg.restart()
                for j in range(NB):
                    rstd_of(j)
                sg.meet()
                for j in range(2 * NC):
                    rstd_of_half(j, *divmod(j, NC))
                sg.arrive()
                pool.wait_ge(mw_in, 32)
                split_weights(0)
                sg.pass_()
                for j in range(NB, 2 * NB):
                    rstd_of(j)
                sg.arrive()
                split_weights(1)
                sg.pass_()
                for c in range(NC):
                    rstd_of_half(2 * NC + c, 0, c)
                sg.meet()
                for e in range(2, E):
                    split_weights(e)
                sg.meet()
                end_round(pool, b * ROUNDS + 1 + L, True)

        @block.scalar
        def _(act):
            sg = Stages(act)
            for dst, src in consts[early:]:
                act.dma_start(dst, src).then_inc(const_in, 16)
            act.wait_ge(const_in, 16 * len(consts))
            nc.scalar.activation(idb[:, :], idf[:, :], ACT.Copy)
            nc.scalar.activation(bandb[:, :, :], bandf[:, :, :], ACT.Copy)
            nc.scalar.activation(rowe[:, :, :], idf[0:E, 0:E].unsqueeze(2).to_broadcast([E, E, P]), ACT.Copy)
            act.drain().then_inc(setup, 1)
            act.wait_ge(setup, 5)

            def norm_out(j, k, dst, gb):
                act.wait_ge(z_mm, j + 1)
                bank = ps[4 + j % 2]
                for i, (d, (g, o)) in enumerate(zip(dst, gb)):
                    ins = nc.scalar.activation(d, bank[0:d.shape[0], i * P:(i + 1) * P], ACT.Identity, bias=o, scale=g)
                ins.then_inc(ln_out, 1)

            def norm_out_d(n):
                act.wait_ge(z_mm, NB + n + 1)
                nc.scalar.activation(xn[:, 2 + n * P:2 + (n + 1) * P], ps[4 + n % 2][:, 0:P], ACT.Identity,
                                     bias=l12[:, 1:2], scale=l12[:, 0:1]).then_inc(ln_out, 1)

            with act.Fori(0, B) as b:
                for c in range(NC):
                    act.wait_ge(emb_mm, c + 1)
                    nc.scalar.activation(xa[:, c * CH:(c + 1) * CH], ps[2 * c][:, :], ACT.Copy)
                    nc.scalar.activation(xb[0:DHI, c * CH:(c + 1) * CH], ps[2 * c + 1][0:DHI, :], ACT.Copy)
                end_round(act, b * ROUNDS)

                with act.Fori(0, L) as l:
                    sg.restart()
                    for n in range(NB):
                        act.wait_ge(qk_mm, n + 1)
                        nc.scalar.activation(nat[:, n, :, 0:DH],
                                             ps[n % 2][:, 0:2 * D].rearrange("p (h d) -> p h d", d=DH),
                                             ACT.Copy).then_inc(qk_p1, 1)
                        act.wait_ge(v_mm, n + 1)
                        nc.scalar.activation(vst[:, n, :, 0:DH],
                                             ps[2 + n % 2][:, 0:D].rearrange("p (h d) -> p h d", d=DH),
                                             ACT.Copy).then_inc(v_p1, 1)
                        act.wait_ge(qk_res, n + 1)
                        r = res[:, n % 2, :].rearrange("p (h d) -> p h d", d=DH)
                        nc.scalar.activation(nat[:, n, 0:H, Q_ROWS[1][0]:Q_ROWS[1][0] + DH], r[:, 0:H, :], ACT.Copy)
                        nc.scalar.activation(nat[:, n, H:2 * H, K_ROWS[1][0]:K_ROWS[1][0] + DH], r[:, H:2 * H, :],
                                             ACT.Copy).then_inc(qk_p2, 1)
                        act.wait_ge(v_res, n + 1)
                        nc.scalar.activation(vst[:, n, :, DH:2 * DH],
                                             resv[:, n % 2, :].rearrange("p (h d) -> p h d", d=DH),
                                             ACT.Copy).then_inc(v_p2, 1)
                    for k in range(0, 2 * H, 2):
                        act.wait_ge(tr_mm, k + 1)
                        nc.scalar.activation(stack[0:NPIECE, k, :], psb[4 + k % 4][0:NPIECE, :],
                                             ACT.Copy).then_inc(ev_act, 1)
                    sg.meet()
                    for s in range(-LEAD, U + 18):
                        if s == ROW + 14:
                            act.wait_ge(f_max, 1)
                            nc.scalar.activation(pfull[:, 0, 0:CH], ps[0][0:H, :], ACT.Exp, bias=fst[:, 0:1],
                                                 accum_out=fst[:, 1:2]).then_inc(f_exp, 1)
                            nc.scalar.activation(pfull[:, 0, CH:T], ps[1][0:H, :], ACT.Exp, bias=fst[:, 0:1],
                                                 accum_out=fst[:, 2:3]).then_inc(f_exp, 1)
                        if s == ROW + 19:
                            act.wait_ge(ft_mm, 1)
                            nc.scalar.activation(f1[:, :, :], ps[0][:, 0:NB * H].rearrange("p (n h) -> p n h", h=H),
                                                 ACT.Copy).then_inc(f1_ready, 1)
                        if s == U + 7:
                            act.wait_ge(oc_mm, 1)
                            nc.scalar.activation(ata[:, 0:1], ps[2][:, 0:1], ACT.Copy)
                            nc.scalar.activation(atb[0:DHI, 0:1], ps[2][0:DHI, 8:9], ACT.Copy).then_inc(oc_copied, 1)
                        for n in range(NB):
                            if s == H * n - 5:
                                act.wait_ge(mt_mm, n + 1)
                                if n >= 2:
                                    act.wait_ge(m_in[n % 2], 48 * (n // 2))
                                nc.scalar.activation(mtr[:, n % 2, :], psb[5][0:3 * H, 64:64 + P],
                                                     ACT.Copy).then_inc(mt_copied, 1)
                                act.wait_ge(dg_ready, n + 1)
                                nc.scalar.activation(eg[:, n % 4, :], dg0[:, n % 4, :], ACT.Exp).then_inc(eg_ready, 1)
                        if 0 <= s < U:
                            w = len(window(s // H)) * P
                            act.wait_ge(t_mm, s + 1)
                            if s >= RING:
                                act.wait_ge(pv_mm, s - RING + 1)
                            nc.scalar.activation(p32[:, s % RING, 0:w], ps[2 + s % 3][:, 0:w], ACT.Exp).then_inc(p32_ready, 1)
                            nc.scalar.activation(p1[:, s % RING, 0:w], ps[2 + s % 3][:, 0:w], ACT.Exp).then_inc(p1_ready, 1)
                        for n in range(NB):
                            if s == H * (n + 1) + 9 + 1:
                                act.wait_ge(at_mm, n + 1)
                                t0 = n == 0
                                nc.scalar.activation(ata[:, n * P + t0:(n + 1) * P], ps[5][:, P + t0:2 * P], ACT.Copy)
                                nc.scalar.activation(atb[0:DHI, n * P + t0:(n + 1) * P],
                                                     ps[5][0:DHI, 2 * P + t0:3 * P], ACT.Copy).then_inc(at_copied, 1)
                    sg.meet()
                    act.wait_ge(wrest_in, 128)
                    for kind, i in SEQ_C:
                        if kind == "tr":
                            k = i // NB
                            norm_out(i, k, (xa[:, blk(i % NB)], xb[0:DHI, blk(i % NB)]),
                                     ((lna[:, 2 * k:2 * k + 1], lna[:, 2 * k + 1:2 * k + 2]),
                                      (lnb[0:DHI, 2 * k:2 * k + 1], lnb[0:DHI, 2 * k + 1:2 * k + 2])))
                        if kind == "hid":
                            act.wait_ge(h_mm, i + 1)
                            c, m = divmod(i, FF // P)
                            if c:
                                act.wait_ge(y_mm, NB + BPC)
                            nc.scalar.activation(hid[:, m, :], ps[6 + i % 2][:, :], ACT.Relu).then_inc(h_relu, 1)
                    sg.meet()
                    end_round(act, b * ROUNDS + 1 + l)

                sg.restart()
                for j in range(NB):
                    norm_out(j, 0, (xa[:, blk(j)], xb[0:DHI, blk(j)]),
                             ((lfa[:, 0:1], lfa[:, 1:2]), (lfb[0:DHI, 0:1], lfb[0:DHI, 1:2])))
                nc.scalar.activation(dcol[:, 1:2], dcol[:, 0:1], ACT.Exp, scale=-1.0).then_inc(act_own, 1)
                sg.meet()
                for c in range(NC):
                    act.wait_ge(h_sums, c + 1)
                    nc.scalar.activation(h0[:, c * CH:(c + 1) * CH], ps[c][:, :], ACT.Copy).then_inc(h0_kept, 1)
                for n in range(NB):
                    norm_out_d(n)
                sg.meet()
                for n in range(NB):
                    act.wait_ge(z_mm, 2 * NB + n + 1)
                    nc.scalar.activation(ht[:, blk(n)], ps[4 + n % 2][:, 0:P], ACT.Identity, bias=l12[:, 3:4],
                                         scale=l12[:, 2:3]).then_inc(ln_out, 1)
                sg.meet()
                for i in range(NC * 2):
                    c, m = divmod(i, 2)
                    act.wait_ge(g_mm, i + 1)
                    nc.scalar.activation(gl[:, m * T + c * CH:m * T + (c + 1) * CH], ps[6 + i % 2][:, :], ACT.Gelu,
                                         bias=ab1s[:, m:m + 1]).then_inc(g_ready, 1)
                for n in range(NB):
                    act.wait_ge(z_mm, 3 * NB + n + 1)
                    nc.scalar.activation(xm[:, blk(n)], ps[4 + n % 2][:, 0:P], ACT.Copy).then_inc(ln_out, 1)
                sg.meet()
                nc.scalar.activation(xmr[:, 0, :], xm[:, :], ACT.Copy).then_inc(x_hi, 1)
                for k in range(E * NC):
                    if k == 1:
                        act.wait_ge(lg_sub, 1)
                        nc.scalar.activation(gt[:, 2, :, :], gt[:, 1, :, :], ACT.Exp).then_inc(lg_exp, 1)
                        act.wait_ge(st_mm, 1)
                        nc.scalar.activation(selt[:, 0:CH], ps[2][0:E, :], ACT.Copy)
                        nc.scalar.activation(selt[:, CH:T], ps[3][0:E, :], ACT.Copy).then_inc(st_copied, 1)
                    if k >= 2:
                        act.wait_ge(ey_mm, k - 1)
                    for m in range(EH // P):
                        i = k * (EH // P) + m
                        act.wait_ge(e_mm, i + 1)
                        if i >= 4:
                            act.wait_ge(e_split, i - 3)
                        bias = mb1s[:, k // NC, m:m + 1]
                        nc.scalar.activation(eh32[:, i % 4, :], ps[4 + i % 4][:, :], ACT.Relu, bias=bias)
                        nc.scalar.activation(ehr[:, k % 2, 0, m, :], ps[4 + i % 4][:, :], ACT.Relu,
                                             bias=bias).then_inc(e_relu, 1)
                sg.meet()
                end_round(act, b * ROUNDS + 1 + L)

        @block.vector
        def _(dve):
            ch = Link(dve, dve_own)
            sg = Stages(dve)
            dve.wait_ge(const_in, 16 * len(consts))
            for k in range(KC):
                nc.vector.tensor_scalar(diag[:, k, :], idf[:, :], cw[:, k:k + 1], None, ALU.mult)
            dve.drain().then_inc(setup, 1)
            dve.wait_ge(setup, 5)

            def stats(j, src, wait=True):
                if wait:
                    dve.wait_ge(y_mm, j + 1)
                ch.link(nc.vector.bn_stats(stt_[:, j % 4, :], src))
                nc.vector.bn_aggr(mv[:, j % 4, :], stt_[:, j % 4, :]).then_inc(y_stats, 1)

            def normed(j, src, dst):
                dve.wait_ge(y_rstd, j + 1)
                return nc.vector.tensor_scalar(dst, src, mv[:, j % 4, 0:1], rstd[:, j % 4:j % 4 + 1],
                                               ALU.subtract, ALU.mult)

            def chunk(t, j):
                return t[:, (j % NC) * CH:(j % NC + 1) * CH]

            def heads(t):
                return t.rearrange("p (h d) -> p h d", d=DH)

            with dve.Fori(0, B) as b:
                ch.restart()
                dve.wait_ge(ids_in, 16)
                nc.vector.tensor_scalar(oneh, idsi, colc[:, 0:1], None, ALU.is_equal).then_inc(onehot_ready, 1)
                dve.wait_ge(pad_in, 16)
                ch.link(nc.vector.tensor_copy(padw[0], padu[:, :].bitcast(U8)))
                ch.link(nc.vector.tensor_copy(padw[1], padw[0]))
                ch.link(nc.vector.memset(padw[0][:, 0:1], 1.0))
                for i in range(4):
                    ins = nc.vector.tensor_scalar(kbrow[:, i, :], padw[i // 2], (KB_HI, KB_LO)[i % 2], None, ALU.mult)
                ch.link(ins)
                end_round(dve, b * ROUNDS)

                with dve.Fori(0, L) as l:
                    ch.restart()
                    sg.restart()
                    nc.vector.tensor_scalar(wqa[:, 0:D], wqa[:, 0:D], 0.25, None, ALU.mult)
                    nc.vector.tensor_scalar(wqb[0:DHI + 1, 0:D], wqb[0:DHI + 1, 0:D], 0.25, None,
                                            ALU.mult).then_inc(glob_ready, 1)
                    for n in range(NB):
                        r = heads(res[:, n % 2, :])
                        rv = heads(resv[:, n % 2, :])
                        dve.wait_ge(qk_p1, n + 1)
                        nc.vector.tensor_tensor(r, heads(ps[n % 2][:, 0:2 * D]), nat[:, n, :, 0:DH],
                                                ALU.subtract).then_inc(qk_res, 1)
                        dve.wait_ge(v_p1, n + 1)
                        nc.vector.tensor_tensor(rv, heads(ps[2 + n % 2][:, 0:D]), vst[:, n, :, 0:DH],
                                                ALU.subtract).then_inc(v_res, 1)
                        q, k = nat[:, n, 0:H, :], nat[:, n, H:2 * H, :]
                        for t, at in ((q, Q_ROWS[0][1]), (q, Q_ROWS[0][2]), (k, K_ROWS[0][1]), (k, K_ROWS[0][2])):
                            nc.vector.tensor_copy(t[:, :, at:at + DH], t[:, :, 0:DH])
                        dve.wait_ge(qk_p2, n + 1)
                        for t, rows, rr in ((q, Q_ROWS, r[:, 0:H, :]), (k, K_ROWS, r[:, H:2 * H, :])):
                            a, c, d = rows[1][0], rows[1][1], rows[2][0]
                            nc.vector.tensor_copy(t[:, :, c:c + DH], t[:, :, a:a + DH])
                            ins = nc.vector.tensor_tensor(t[:, :, d:d + DH], rr, t[:, :, a:a + DH], ALU.subtract)
                        ins.then_inc(nat_ready, 1)
                        dve.wait_ge(v_p2, n + 1)
                        nc.vector.tensor_tensor(vst[:, n, :, 2 * DH:3 * DH], rv, vst[:, n, :, DH:2 * DH], ALU.subtract)
                    for k in range(1, 2 * H, 2):
                        dve.wait_ge(tr_mm, k + 1)
                        nc.vector.tensor_copy(stack[0:NPIECE, k, :], psb[4 + k % 4][0:NPIECE, :]).then_inc(ev_dve, 1)
                    sg.meet()
                    dve.wait_ge(kb_out, 16 * H)
                    dve.wait_ge(rows_in, 32)
                    nc.vector.tensor_scalar(k0s[0:K_NAT, :], stack[0:K_NAT, H:2 * H, 0], colc[0:K_NAT, 1:2], None, ALU.mult)
                    nc.vector.tensor_scalar(q0s[0:K_NAT, :, :].rearrange("p a b -> p (a b)")[:, 0:H * H:H + 1],
                                            stack[0:K_NAT, 0:H, 0], colc[0:K_NAT, 1:2], colc[0:K_NAT, 2:3],
                                            ALU.mult, ALU.add).then_inc(glob_ready, 1)
                    for s in range(-LEAD, U + 18):
                        v, u = s + LEAD, s - 1
                        if s == -LEAD + 2:
                            dve.wait_ge(v0_mm, 1)
                            for g in range(2):
                                pv = ps[6 + g][:, 0:HH * VW].rearrange("p (h w) -> p h w", w=VW)
                                ch.link(nc.vector.tensor_copy(v0t[:, 0, half(g), :], pv[:, :, 2 * DH:3 * DH]))
                                ch.link(nc.vector.tensor_tensor(v0t[:, 1, half(g), :], pv[:, :, DH:2 * DH],
                                                                v0t[:, 0, half(g), :], ALU.add))
                                ins = nc.vector.tensor_tensor(v0b[:, half(g), :], pv[:, :, 0:DH], v0t[:, 1, half(g), :],
                                                              ALU.add)
                            ins.then_inc(v0_ready, 1)
                        if s == ROW + 12:
                            dve.wait_ge(f_mm, 1)
                            nc.vector.tensor_reduce(fst[:, 2:3], ps[0][0:H, :], AX.X, ALU.max, negate=True)
                            ch.link(nc.vector.tensor_reduce(fst[:, 3:4], ps[1][0:H, :], AX.X, ALU.max, negate=True))
                            nc.vector.tensor_tensor(fst[:, 0:1], fst[:, 2:3], fst[:, 3:4], ALU.min).then_inc(f_max, 1)
                        if s == ROW + 16:
                            dve.wait_ge(f_exp, 2)
                            ch.link(nc.vector.tensor_tensor(fst[:, 3:4], fst[:, 1:2], fst[:, 2:3], ALU.add))
                            ch.link(nc.vector.reciprocal(fst[:, 3:4], fst[:, 3:4]))
                            nc.vector.tensor_scalar(pfull[:, 1, :], pfull[:, 0, :], fst[:, 3:4], None,
                                                    ALU.mult).then_inc(f_norm, 1)
                        if s == ROW + 20:
                            dve.wait_ge(f1_ready, 1)
                            nc.vector.tensor_tensor(f2[:, :, :], ps[0][:, 0:NB * H].rearrange("p (n h) -> p n h", h=H),
                                                    f1[:, :, :], ALU.subtract).then_inc(f2_ready, 1)
                        if s == U + 4:
                            dve.wait_ge(og_mm, 1)
                            for g in range(2):
                                v_ = ps[1 - g][0:H, 0:HH * VW].rearrange("p (h w) -> p h w", w=VW)
                                for i in range(3):
                                    ins = nc.vector.tensor_tensor(
                                        heads(og[:, i, :])[:, half(g), :], v_[:, :, i * DH:(i + 1) * DH],
                                        heads(bm[0:H, :])[:, half(g), :], ALU.mult)
                            ins.then_inc(og_ready, 1)

                        n, r = divmod(s + 10, H)
                        maximum = 0 <= n < NB and r <= 2
                        if maximum and r == 0:
                            dve.wait_ge(max_done, H * n + H)
                            dve.wait_ge(sg_mm, n + 1)
                            m_link = ch.mark(nc.vector.scalar_tensor_tensor(nm[:, :], ps[5][:, 0:H], -1.0, nmx[:, n % 3, :],
                                                                            ALU.mult, ALU.min))
                        if maximum and r == 1:
                            dve.wait_ge(dve_own, m_link)
                            m_link = ch.mark(nc.vector.tensor_tensor(nmr[:, :], nm[:, :], mcat[:, 0, :], ALU.subtract))
                        if maximum and r == 2:
                            dve.wait_ge(dve_own, m_link)
                            nc.vector.tensor_tensor(mcat[:, 2, :], nmr[:, :], mcat[:, 1, :], ALU.subtract)
                        cn, cr = divmod(s - 10, H)
                        g, cr = divmod(cr, 6)
                        combine = 0 <= cn < NB and cr <= 2
                        pv = ps[6 + g][:, 0:HH * VW].rearrange("p (h w) -> p h w", w=VW)
                        t = pvt[:, g, :, :, :]
                        if combine and cr == 0:
                            dve.wait_ge(pv_mm, H * cn + HH * (g + 1))
                            dve.wait_ge(pvg_ready, 2 * cn + g + 1)
                            nc.vector.tensor_tensor(den[:, g, 0, :], pv[:, :, 3 * DH], eg[:, cn % 4, half(g)], ALU.add)
                            c_link = ch.mark(nc.vector.tensor_tensor(t[:, 1, :, :], pv[:, :, 2 * DH:3 * DH], t[:, 0, :, :],
                                                                     ALU.add))
                        if combine and cr == 1:
                            dve.wait_ge(dve_own, c_link)
                            nc.vector.reciprocal(den[:, g, 1, :], den[:, g, 0, :])
                            c_link = ch.mark(nc.vector.tensor_tensor(t[:, 2, :, :], pv[:, :, DH:2 * DH], t[:, 1, :, :],
                                                                     ALU.add))
                        if combine and cr == 2:
                            dve.wait_ge(dve_own, c_link)
                            c_link = ch.mark(nc.vector.tensor_tensor(t[:, 3, :, :], pv[:, :, 0:DH], t[:, 2, :, :], ALU.add))
                        if v < U:
                            vn, h = divmod(v, H)
                            w = len(window(vn)) * P
                            dve.wait_ge(nat_mm, v + 1)
                            nc.vector.tensor_reduce(nmx[:, vn % 3, h:h + 1], nat_bank(v)[:, 0:w], AX.X, ALU.max,
                                                    negate=True).then_inc(max_done, 1)
                        if 0 <= u < U and u % SHARE == SHARE - 1:
                            dve.wait_ge(p1_ready, u + 1)
                            if u >= RING:
                                dve.wait_ge(pv_mm, u - RING + 1)
                            w = len(window(u // H)) * P
                            nc.vector.tensor_tensor(p2[:, u % RING, 0:w], p32[:, u % RING, 0:w], p1[:, u % RING, 0:w],
                                                    ALU.subtract).then_inc(p2_dve, 1)
                        if maximum and r == 0:
                            if n >= 1:
                                dve.wait_ge(mt_mm, n)
                            dve.wait_ge(dve_own, m_link)
                            m_link = ch.mark(nc.vector.tensor_copy(mcat[:, 0, :], nm[:, :]))
                        if maximum and r == 1:
                            dve.wait_ge(dve_own, m_link)
                            m_link = ch.mark(nc.vector.tensor_copy(mcat[:, 1, :], nmr[:, :]))
                        if maximum and r == 2:
                            nc.vector.tensor_tensor(dg0[:, n % 4, :], ps[5][:, 0:H], nm[:, :], ALU.add).then_inc(dg_ready, 1)
                        if combine and cr == 2:
                            dve.wait_ge(dve_own, c_link)
                            if cn >= 2 and g == 0:
                                dve.wait_ge(at_mm, cn - 1)
                            nc.vector.tensor_tensor(
                                heads(att[:, cn % 2, :])[:, half(g), :], t[:, 3, :, :],
                                den[:, g, 1, :].unsqueeze(2).to_broadcast([P, HH, DH]), ALU.mult).then_inc(comb, 1)
                    sg.meet()
                    pend = []
                    for kind, i in SEQ_C:
                        if kind == "y":
                            stats(i, ps[i % 4][:, 0:D])
                            pend.append(i)
                        if kind == "z":
                            if i >= 2:
                                dve.wait_ge(z_mm, i - 1)
                            normed(i, ps[i % 4][:, 0:D], zt[:, i % 2, :]).then_inc(z_ready, 1)
                    sg.meet()
                    end_round(dve, b * ROUNDS + 1 + l)

                ch.restart()
                sg.restart()
                for j in range(NB + 1):
                    if j < NB:
                        stats(j, ps[j % 4][:, 0:D])
                    if j >= 1:
                        i = j - 1
                        if i >= 2:
                            dve.wait_ge(z_mm, i - 1)
                        normed(i, ps[i % 4][:, 0:D], zt[:, i % 2, :]).then_inc(z_ready, 1)
                sg.meet()
                ch.link(nc.vector.tensor_scalar(dcol[:, 2:3], dcol[:, 1:2], 1.0, None, ALU.add))
                ch.link(nc.vector.reciprocal(dcol[:, 3:4], dcol[:, 2:3]))
                ch.link(nc.vector.tensor_scalar(dcol[:, 2:3], dcol[:, 3:4], -1.0, 1.0, ALU.mult, ALU.add))

                def half_stats(w, c, src):
                    for n in range(c * BPC, (c + 1) * BPC):
                        ins = nc.vector.bn_stats(cst[:, n, :], src[:, blk(n)])
                    ch.link(ins)
                    for n in range(c * BPC, (c + 1) * BPC):
                        ins = nc.vector.bn_aggr(cmv[:, w, n, :], cst[:, n, :])
                    ins.then_inc(c_stats, 1)

                def c_normed(w, n, src, dst):
                    return nc.vector.tensor_scalar(dst, src[:, blk(n)], cmv[:, w, n, 0:1], crs[:, w, n:n + 1],
                                                   ALU.subtract, ALU.mult)

                for c in range(NC):
                    dve.wait_ge(h0_kept, c + 1)
                    half_stats(0, c, h0)
                for c in range(NC):
                    dve.wait_ge(c_rstd, c + 1)
                    for n in range(c * BPC, (c + 1) * BPC):
                        ins = c_normed(0, n, h0, x1[:, blk(n)])
                    ch.link(ins)
                    half_stats(1, c, x1)
                for n in range(NB):
                    dve.wait_ge(c_rstd, NC + n // BPC + 1)
                    if n >= 2:
                        dve.wait_ge(z_mm, NB + n - 1)
                    c_normed(1, n, x1, zt[:, n % 2, 0:DM]).then_inc(z_ready, 1)
                sg.meet()
                ch.link(nc.vector.tensor_scalar(d1, xn[:, 2:2 + T], dcol[:, 2:3], None, ALU.mult))
                nc.vector.tensor_tensor_scan(st, dcol[:, 3:4].to_broadcast([P, T]), d1, 0.0, ALU.mult,
                                             ALU.add).then_inc(s_ready, 1)
                for k in range(NB + 1):
                    if k < NB:
                        dve.wait_ge(y_mm, NB + k + 1)
                        ch.link(nc.vector.tensor_tensor(x1[:, blk(k)], ps[k % 4][:, 0:DM], x1[:, blk(k)], ALU.add))
                        stats(NB + k, x1[:, blk(k)], False)
                    if k >= 1:
                        n = k - 1
                        if n >= 2:
                            dve.wait_ge(z_mm, 2 * NB + n - 1)
                        normed(NB + n, x1[:, blk(n)], zt[:, n % 2, 0:DM]).then_inc(z_ready, 1)
                sg.meet()
                for c in range(NC):
                    cs = slice(c * CH, (c + 1) * CH)
                    dve.wait_ge(mlp_mm, c + 1)
                    ch.link(nc.vector.tensor_tensor(x1[:, cs], ps[c][:, :], x1[:, cs], ALU.add))
                    ch.link(nc.vector.tensor_tensor(h0[:, cs], h0[:, cs], x1[:, cs], ALU.add))
                    half_stats(0, c, h0)
                for n in range(NB):
                    dve.wait_ge(c_rstd, 2 * NC + n // BPC + 1)
                    if n >= 2:
                        dve.wait_ge(z_mm, 3 * NB + n - 1)
                    c_normed(0, n, h0, zt[:, n % 2, 0:DM]).then_inc(z_ready, 1)
                sg.meet()
                dve.wait_ge(x_hi, 1)
                nc.vector.tensor_tensor(xmr[:, 1, :], xm[:, :], xmr[:, 0, :].bitcast(F32), ALU.subtract).then_inc(x_lo, 1)
                dve.wait_ge(lg_mm, 1)
                ch.link(nc.vector.tensor_copy(gt[:, 0, :, :], ps[0][:, 0:NB * E].rearrange("p (n e) -> p n e", e=E)))
                ch.link(nc.vector.tensor_reduce(gs[:, 0, :], gt[:, 0, :, :], AX.X, ALU.max))
                top = gs[:, 0, :].unsqueeze(2).to_broadcast([P, NB, E])
                nc.vector.tensor_tensor(gt[:, 1, :, :], gt[:, 0, :, :], top, ALU.subtract).then_inc(lg_sub, 1)
                ch.link(nc.vector.tensor_tensor(gt[:, 3, :, :], gt[:, 0, :, :], top, ALU.is_equal))
                for e in range(E):
                    ins = nc.vector.tensor_scalar(gt[:, 4, :, e], gt[:, 3, :, e], float(E - e), None, ALU.mult)
                ch.link(ins)
                ch.link(nc.vector.tensor_reduce(gs[:, 1, :], gt[:, 4, :, :], AX.X, ALU.max))
                nc.vector.tensor_tensor(gt[:, 5, :, :], gt[:, 4, :, :],
                                        gs[:, 1, :].unsqueeze(2).to_broadcast([P, NB, E]), ALU.is_equal).then_inc(sel_ready, 1)
                for k in range(E * NC + 2):
                    for m in range(EH // P):
                        if k < E * NC:
                            i = k * (EH // P) + m
                            dve.wait_ge(e_relu, i + 1)
                            nc.vector.tensor_tensor(ehr[:, k % 2, 1, m, :], eh32[:, i % 4, :],
                                                    ehr[:, k % 2, 0, m, :].bitcast(F32), ALU.subtract).then_inc(e_split, 1)
                        if m == 0 and k >= 2 + NC:
                            j = k - 2
                            dve.wait_ge(ey_masked, j + 1)
                            if j >= 2 * NC:
                                dve.wait_ge(acc_done, j - 2 * NC + 1)
                            nc.vector.tensor_tensor(chunk(acc, j), ey[:, j % 2, :], chunk(acc, j), ALU.add).then_inc(acc_done, 1)
                    if k == 0:
                        dve.wait_ge(lg_exp, 1)
                        ch.link(nc.vector.tensor_reduce(gs[:, 2, :], gt[:, 2, :, :], AX.X, ALU.add))
                        ch.link(nc.vector.reciprocal(gs[:, 3, :], gs[:, 2, :]))
                    if 1 <= k <= E * NC:
                        j = k - 1
                        dve.wait_ge(mask_mm, j + 1)
                        if j >= 2:
                            dve.wait_ge(ey_masked, j - 1)
                        if j >= 2 + NC:
                            dve.wait_ge(acc_done, j - 2 - NC + 1)
                        nc.vector.tensor_copy(mask[:, j % 2, :], ps[2 + j % 2][:, :]).then_inc(mask_copied, 1)
                        dve.wait_ge(mask_copied, j + 1)
                        dve.wait_ge(ey_mm, j + 1)
                        nc.vector.scalar_tensor_tensor(ey[:, j % 2, :] if j >= NC else chunk(acc, j), ps[j % 2][:, :],
                                                       mb2s[:, j // NC:j // NC + 1], mask[:, j % 2, :],
                                                       ALU.add, ALU.mult).then_inc(ey_masked, 1)
                for n in range(NB):
                    dve.wait_ge(o_mm, n // BPC + 1)
                    nc.vector.scalar_tensor_tensor(h0[:, blk(n)], ps[4 + n // BPC][:, blk(n % BPC)], gs[:, 3, n:n + 1],
                                                   h0[:, blk(n)], ALU.mult, ALU.add).then_inc(o_ready, 1)
                sg.meet()
                end_round(dve, b * ROUNDS + 1 + L)

        @block.tensor
        def _(pe):
            sg = Stages(pe)
            mm = nc.tensor.matmul
            pe.wait_ge(const_in, 16 * len(consts))
            pe.drain().then_inc(setup, 1)
            pe.wait_ge(setup, 5)

            def ln_transpose(j, zc, width):
                pe.wait_ge(z_ready, zc + 1)
                if zc >= 2:
                    pe.wait_ge(ln_out, zc - 1)
                bank = ps[4 + zc % 2]
                ins = nc.tensor.transpose(bank[:, 0:P], zt[:, zc % 2, 0:P], idf[:, :])
                if width > P:
                    ins = nc.tensor.transpose(bank[0:width - P, P:2 * P], zt[:, zc % 2, P:width], idf[:, :])
                ins.then_inc(z_mm, 1)

            with pe.Fori(0, B) as b:
                pe.wait_ge(onehot_ready, 1)
                for c in range(NC):
                    mm(ps[2 * c][:, :], embs[:, 0:DLO], oneh[:, c * CH:(c + 1) * CH], start=True, stop=True)
                    mm(ps[2 * c + 1][0:DHI, :], embs[:, DLO:D], oneh[:, c * CH:(c + 1) * CH], start=True,
                       stop=True).then_inc(emb_mm, 1)
                end_round(pe, b * ROUNDS)

                with pe.Fori(0, L) as l:
                    sg.restart()
                    pe.wait_ge(glob_ready, 1)
                    for n in range(NB):
                        if n >= 2:
                            pe.wait_ge(qk_res, n - 1)
                            pe.wait_ge(v_res, n - 1)
                        mm(ps[n % 2][:, 0:2 * D], xa[:, blk(n)], wqa[:, 0:2 * D], start=True, stop=False)
                        mm(ps[n % 2][:, 0:2 * D], xb[0:DHI + 1, blk(n)], wqb[0:DHI + 1, 0:2 * D], start=False,
                           stop=True).then_inc(qk_mm, 1)
                        mm(ps[2 + n % 2][:, 0:D], xa[:, blk(n)], wqa[:, 2 * D:3 * D], start=True, stop=False)
                        mm(ps[2 + n % 2][:, 0:D], xb[0:DHI + 1, blk(n)], wqb[0:DHI + 1, 2 * D:3 * D], start=False,
                           stop=True).then_inc(v_mm, 1)
                    pe.wait_ge(nat_ready, NB)
                    for k in range(2 * H):
                        if k >= 4:
                            pe.wait_ge(ev_dve if k % 2 else ev_act, (k - 4) // 2 + 1)
                        for n in range(NB):
                            ins = nc.tensor.transpose(psb[4 + k % 4][0:NPIECE, blk(n)], nat[:, n, k, :], idb[:, :])
                        ins.then_inc(tr_mm, 1)
                    sg.meet()
                    for g in range(2):
                        ins = mm(ps[6 + g][:, 0:HH * VW], onesb[0:1, :], vst[0:1, 0, half(g), :], start=True, stop=True)
                    ins.then_inc(v0_mm, 1)
                    pe.wait_ge(kb_out, 16 * H)
                    pe.wait_ge(rows_in, 32)
                    pe.wait_ge(glob_ready, 2)
                    for s in range(-LEAD, U + 18):
                        if ROW <= s < ROW + H:
                            h = s - ROW
                            if h == 0:
                                pe.wait_ge(max_done, U)
                            for c in range(NC):
                                ins = mm(ps[c][0:H, :], q0s[0:K_NAT, h, :], stack[0:K_NAT, H + h, c * CH:(c + 1) * CH],
                                         start=h == 0, stop=h == H - 1)
                            if h == H - 1:
                                ins.then_inc(f_mm, 1)
                        if s == ROW + 18:
                            pe.wait_ge(f_norm, 1)
                            for n in range(NB):
                                ins = nc.tensor.transpose(ps[0][:, n * H:(n + 1) * H], pfull[:, 1, blk(n)], idf[0:H, 0:H])
                            ins.then_inc(ft_mm, 1)
                        for n in range(NB):
                            if s != ROW + 22 + n // 2:
                                continue
                            if n == 0:
                                pe.wait_ge(f2_ready, 1)
                            for g in range(2):
                                for ft in (f1, f2):
                                    ins = mm(ps[1 - g][0:H, 0:HH * VW], ft[:, n, :], vst[:, n, half(g), :],
                                             start=n == 0 and ft is f1, stop=n == NB - 1 and ft is f2)
                            if n == NB - 1:
                                ins.then_inc(og_mm, 1)
                        if s == U + 6:
                            pe.wait_ge(og_ready, 1)
                            pe.wait_ge(p1_ready, U)
                            for i in range(3):
                                mm(ps[2][:, 0:1], og[:, i, 0:DLO], ones[0:H, 0:1], start=i == 0, stop=i == 2)
                            for i in range(3):
                                ins = mm(ps[2][0:DHI, 8:9], og[:, i, DLO:D], ones[0:H, 0:1], start=i == 0, stop=i == 2)
                            ins.then_inc(oc_mm, 1)
                        v = s + LEAD
                        if v < U:
                            n, h = divmod(v, H)
                            win = window(n)
                            if v >= LEAD:
                                pe.wait_ge(max_done, v - 1)
                            elif v >= 4:
                                pe.wait_ge(max_done, v - 3)
                            s_ps = nat_bank(v)
                            q = stack[0:K_NAT, h, blk(n)]
                            edges = [(i, m) for i, m in enumerate(win) if m != n]
                            mm(s_ps[:, 0:len(win) * P], q, stack[0:K_NAT, H + h, blk(win[0], len(win))], start=True,
                               stop=False)
                            for i, m in edges:
                                ins = mm(s_ps[:, blk(i)], idb[:, :], bandb[:, 0 if m < n else 1, :], start=False,
                                         stop=(i, m) == edges[-1])
                            ins.then_inc(nat_mm, 1)
                        for n in range(NB):
                            if s == H * n - 11:
                                if n >= 3:
                                    pe.wait_ge(at_copied, n - 2)
                                elif n >= 1:
                                    pe.wait_ge(mt_copied, n)
                                for g in range(H):
                                    ins = mm(ps[5][:, g:g + 1], stack[0:K_NAT, g, blk(n)], k0s[0:K_NAT, g:g + 1],
                                             start=True, stop=True)
                                ins.then_inc(sg_mm, 1)
                            if s == H * n - 6:
                                pe.wait_ge(dg_ready, n + 1)
                                nc.tensor.transpose(psb[5][0:3 * H, 64:64 + P],
                                                    mcat[:, :, :].rearrange("p i h -> p (i h)"), idb[:, :]).then_inc(mt_mm, 1)
                            if s == H * (n + 1) + 9:
                                if n + 2 < NB:
                                    pe.wait_ge(mt_copied, n + 3)
                                elif n >= 1:
                                    pe.wait_ge(at_copied, n)
                                pe.wait_ge(comb, 2 * n + 2)
                                nc.tensor.transpose(ps[5][:, P:2 * P], att[:, n % 2, 0:DLO], idf[:, :])
                                nc.tensor.transpose(ps[5][0:DHI, 2 * P:3 * P], att[:, n % 2, DLO:D],
                                                    idf[:, :]).then_inc(at_mm, 1)
                        if 0 <= s < U:
                            n, h = divmod(s, H)
                            if h == 0:
                                pe.wait_ge(m_in[n % 2], 48 * (n // 2 + 1))
                            if s == 0:
                                pe.wait_ge(max_done, LEAD)
                            if s >= 3:
                                pe.wait_ge(p1_ready, s - 2)
                            win = window(n)
                            for i, m in enumerate(win):
                                ins = mm(ps[2 + s % 3][:, blk(i)], stack[0:K_ALL, H + h, blk(m)],
                                         stack[0:K_ALL, h, blk(n)], start=True, stop=m == n)
                                if m != n:
                                    ins = mm(ps[2 + s % 3][:, blk(i)], idb[:, :], bandb[:, 1 if m < n else 0, :],
                                             start=False, stop=True)
                            ins.then_inc(t_mm, 1)
                        w = s - PV_LAG
                        if 0 <= w < U:
                            n, h = divmod(w, H)
                            g, i = divmod(h, HH)
                            if w == 0:
                                pe.wait_ge(v0_ready, 1)
                            if i == 0 and n >= 1:
                                pe.wait_ge(comb, 2 * (n - 1) + g + 1)
                            if w % SHARE == SHARE - 1:
                                pe.wait_ge(p2_dve, w // SHARE + 1)
                            else:
                                pe.wait_ge(p2_pool, w + 1 - w // SHARE)
                            win = window(n)
                            out_ps = ps[6 + g][:, i * VW:(i + 1) * VW]
                            for a, m in enumerate(win):
                                for pt in (p1, p2):
                                    ins = mm(out_ps, pt[:, w % RING, blk(a)], vst[:, m, h, :],
                                             start=a == 0 and pt is p1, stop=a == len(win) - 1 and pt is p2)
                            ins.then_inc(pv_mm, 1)
                    sg.meet()
                    pe.wait_ge(wrest_in, 128)
                    for kind, i in SEQ_C:
                        if kind == "y":
                            n = i % NB
                            if i >= 4:
                                pe.wait_ge(z_ready, i - 3)
                            y = ps[i % 4][:, 0:D]
                            if i < NB:
                                mm(y, ata[:, blk(n)], woa[:, :], start=True, stop=False)
                                mm(y, atb[0:DHI + 1, blk(n)], wob[0:DHI + 1, :], start=False, stop=False)
                                mm(ps[i % 4][:, 0:P], xa[:, blk(n)], idf[:, :], start=False, stop=False)
                                mm(ps[i % 4][:, P:D], xb[0:DHI, blk(n)], idf[0:DHI, 0:DHI], start=False,
                                   stop=True).then_inc(y_mm, 1)
                            else:
                                c = n // BPC
                                pe.wait_ge(h_relu, (c + 1) * (FF // P))
                                mm(y, xb[0:DHI + 1, blk(n)], rwb[0:DHI + 1, :], start=True, stop=False)
                                mm(ps[i % 4][:, 0:P], xa[:, blk(n)], idf[:, :], start=False, stop=False)
                                for m in range(FF // P):
                                    ins = mm(y, hid[:, m, blk(n % BPC)], w2s[:, m, :], start=False, stop=m == FF // P - 1)
                                ins.then_inc(y_mm, 1)
                        if kind == "tr":
                            ln_transpose(i, i, D)
                        if kind == "hid":
                            c, m = divmod(i, FF // P)
                            pe.wait_ge(ln_out, (c + 1) * BPC)
                            if i >= 2:
                                pe.wait_ge(h_relu, i - 1)
                            cs = slice(c * CH, (c + 1) * CH)
                            mm(ps[6 + i % 2][:, :], w1a[:, m * P:(m + 1) * P], xa[:, cs], start=True, stop=False)
                            mm(ps[6 + i % 2][:, :], w1b[0:DHI + 1, m * P:(m + 1) * P], xb[0:DHI + 1, cs], start=False,
                               stop=True).then_inc(h_mm, 1)
                    sg.meet()
                    end_round(pe, b * ROUNDS + 1 + l)

                sg.restart()
                for n in range(NB + 2):
                    if n < NB:
                        if n >= 4:
                            pe.wait_ge(z_ready, n - 3)
                        mm(ps[n % 4][:, 0:P], xa[:, blk(n)], idf[:, :], start=True, stop=True)
                        mm(ps[n % 4][:, P:D], xb[0:DHI, blk(n)], idf[0:DHI, 0:DHI], start=True, stop=True).then_inc(y_mm, 1)
                    if n >= 2:
                        ln_transpose(n - 2, n - 2, D)
                sg.meet()
                for n in range(NB):
                    h_ps = ps[n // BPC][:, blk(n % BPC)]
                    mm(h_ps, xa[:, blk(n)], wca[:, :], start=True, stop=False)
                    ins = mm(h_ps, xb[0:DHI + 1, blk(n)], wcb[0:DHI + 1, :], start=False, stop=True)
                    if n % BPC == BPC - 1:
                        ins.then_inc(h_sums, 1)
                for n in range(NB):
                    ln_transpose(0, NB + n, DM)
                sg.meet()

                def convolve(n):
                    for k in range(KC):
                        mm(ps[n % 4][:, 0:DM], xn[:, n * P + k:(n + 1) * P + k], diag[:, k, :], start=k == 0, stop=False)

                for n in range(4):
                    convolve(n)
                pe.wait_ge(s_ready, 1)
                for n in range(NB + 2):
                    if n < NB:
                        y = ps[n % 4][:, 0:DM]
                        if n >= 4:
                            pe.wait_ge(z_ready, 2 * NB + n - 3)
                            convolve(n)
                        mm(y, st[:, blk(n)], wos[:, :], start=False, stop=False)
                        mm(y, ones[0:2, :], bo2s[:, :], start=False, stop=True).then_inc(y_mm, 1)
                    if n >= 2:
                        ln_transpose(0, 2 * NB + n - 2, DM)
                sg.meet()
                for i in range(NC * 2):
                    c, m = divmod(i, 2)
                    if i >= 2:
                        pe.wait_ge(g_ready, i - 1)
                    mm(ps[6 + i % 2][:, :], aw1s[:, m * P:(m + 1) * P], ht[:, c * CH:(c + 1) * CH], start=True,
                       stop=True).then_inc(g_mm, 1)
                for n in range(NB):
                    c = n // BPC
                    if n % BPC == 0:
                        pe.wait_ge(g_ready, 2 * (c + 1))
                    y = ps[c][:, blk(n % BPC)]
                    for m in range(2):
                        mm(y, gl[:, m * T + n * P:m * T + (n + 1) * P], aw2s[:, m, :], start=m == 0, stop=False)
                    ins = mm(y, ones[0:1, :], ab2s[:, :], start=False, stop=True)
                    if n % BPC == BPC - 1:
                        ins.then_inc(mlp_mm, 1)
                for n in range(NB):
                    ln_transpose(0, 3 * NB + n, DM)
                sg.meet()
                for n in range(NB):
                    mm(ps[0][:, n * E:(n + 1) * E], xm[:, blk(n)], wgs[:, :], start=True, stop=False)
                    ins = mm(ps[0][:, n * E:(n + 1) * E], ones[0:1, :], bgs[:, :], start=False, stop=True)
                ins.then_inc(lg_mm, 1)
                pe.wait_ge(x_lo, 1)
                for k in range(E * NC + 1):
                    if k < E * NC:
                        e, c = divmod(k, NC)
                        pe.wait_ge(w1_split, e + 1)
                        for m in range(EH // P):
                            i = k * (EH // P) + m
                            if i >= 4:
                                pe.wait_ge(e_relu, i - 3)
                            for a, b_ in PARTS:
                                ins = mm(ps[4 + i % 4][:, :], w1r[:, e % 2, a, m * P:(m + 1) * P],
                                         xmr[:, b_, c * CH:(c + 1) * CH], start=(a, b_) == PARTS[0], stop=(a, b_) == PARTS[-1])
                            ins.then_inc(e_mm, 1)
                    if k == 0:
                        pe.wait_ge(sel_ready, 1)
                        for n in range(NB):
                            ins = nc.tensor.transpose(ps[2 + n // BPC][0:E, blk(n % BPC)], gt[:, 5, n, :], idf[:, :])
                        ins.then_inc(st_mm, 1)
                    if k >= 1:
                        j = k - 1
                        e, c = divmod(j, NC)
                        pe.wait_ge(w2_split, e + 1)
                        if j == 0:
                            pe.wait_ge(st_copied, 1)
                        else:
                            pe.wait_ge(e_split, k * (EH // P))
                        if j >= 2:
                            pe.wait_ge(ey_masked, j - 1)
                            pe.wait_ge(mask_copied, j - 1)
                        mm(ps[2 + j % 2][:, :], rowe[:, e, :], selt[:, c * CH:(c + 1) * CH], start=True,
                           stop=True).then_inc(mask_mm, 1)
                        if j == 0:
                            pe.wait_ge(e_split, k * (EH // P))
                        for m in range(EH // P):
                            for a, b_ in PARTS:
                                ins = mm(ps[j % 2][:, :], w2r[:, e % 2, a, m, :], ehr[:, j % 2, b_, m, :],
                                         start=m == 0 and (a, b_) == PARTS[0],
                                         stop=m == EH // P - 1 and (a, b_) == PARTS[-1])
                        ins.then_inc(ey_mm, 1)
                for c in range(NC):
                    pe.wait_ge(acc_done, NC * (E - 2) + 1 + c)
                    for n in range(BPC):
                        ins = nc.tensor.transpose(ps[4 + c][:, blk(n)], acc[:, blk(c * BPC + n)], idf[:, :])
                    ins.then_inc(o_mm, 1)
                sg.meet()
                end_round(pe, b * ROUNDS + 1 + L)


def _seq_c():
    seq = []

    def y(i):
        seq.append(("y", i))
        if i >= 1:
            seq.append(("z", i - 1))

    for i in range(4):
        y(i)
    for i in range(4):
        seq.append(("tr", i) if i < 3 else ("z", 3))
        if i < 3:
            y(4 + i)
    seq = [s for k, s in enumerate(seq) if s not in seq[:k]]
    seq.append(("tr", 3))
    y(7)
    seq.append(("z", 7))
    seq += [("hid", m) for m in range(3)] + [("tr", 4), ("tr", 5)] + [("hid", m) for m in range(3, 6)]
    seq += [("tr", 6), ("tr", 7)]
    seq += [("y", 8), ("y", 9), ("z", 8), ("y", 10), ("z", 9), ("y", 11), ("z", 10), ("z", 11)]
    seq += [("hid", m) for m in range(6, 9)] + [("tr", 8), ("tr", 9)] + [("hid", m) for m in range(9, 12)]
    seq += [("tr", 10), ("tr", 11)]
    seq += [("y", 12), ("y", 13), ("z", 12), ("y", 14), ("z", 13), ("tr", 12), ("y", 15), ("z", 14), ("tr", 13),
            ("z", 15), ("tr", 14), ("tr", 15)]
    return seq


SEQ_C = _seq_c()


_OUTS = [((2, 1024, 128), 'float32')]


def kernel(**inputs):
    import numpy as _np
    import concourse.bacc as _bacc
    from concourse import mybir as _mybir
    from concourse.bass_utils import run_bass_kernel_spmd as _run

    g = {k: _np.asarray(v) for k, v in inputs.items()}
    t = "L0_tok_"
    a = "L0_attn_"
    f = "L0_ffn_"

    def cat(ws, bs):
        w = _np.concatenate([_np.transpose(g[t + n], (0, 2, 1)) for n in ws], axis=2)
        r = _np.concatenate([g[t + n][:, None, :] for n in bs], axis=2)
        return _np.concatenate([w, r], axis=1)

    def row(v):
        return v.reshape(1, -1)

    def columns(*vs):
        return _np.stack(vs, axis=-1)

    p, q = _np.arange(P)[:, None], _np.arange(P)[None, :]
    low = _np.where(q < p, BAND_OUT, 0.0).astype(_np.float32)
    high = _np.where(q > p, BAND_OUT, 0.0).astype(_np.float32)
    cols = _np.zeros((P, 4), _np.float32)
    cols[:, 0] = _np.arange(P)
    cols[0:NPIECE, 1] = 1.0
    cols[R_FULL:R_MAX, 2] = 1.0
    cols[:, 3] = -0.5
    eye = _np.eye(D, dtype=_np.float32)
    arrays = {
        "x": g["x"], "pad": g["mask_BS_b0_1"].view(_np.int32), "emb": g[t + "emb"],
        "wqkv": cat(["Wq", "Wk", "Wv"], ["bq", "bk", "bv"]), "wo": cat(["Wo"], ["bo"]), "w1": cat(["W1"], ["b1"]),
        "w2": _np.transpose(g[t + "W2"], (0, 2, 1)),
        "rw": _np.stack([_np.concatenate([eye, g[t + "b2"][l][None, :]]) for l in range(L)]),
        "lnl": columns(*(g[t + n] for n in ("g1", "beta1", "g2", "beta2"))),
        "lnf": columns(g[t + "gf"], g[t + "betaf"]),
        "wc": _np.concatenate([g[t + "Wc"].T, row(g[t + "bc"])]),
        "ident": _np.eye(P, dtype=_np.float32), "band": _np.stack([low, high], axis=1), "cols": cols,
        "decay": g[a + "decay_logit"].reshape(-1, 1), "convw": g[a + "conv_w"].reshape(DM, KC),
        "wout": g[a + "W_out"].T, "bo2": _np.stack([g[a + "b_out"], g[a + "conv_b"]]),
        "ln12": columns(*(g[a + n] for n in ("ln1_g", "ln1_b", "ln2_g", "ln2_b"))),
        "aw1": g[a + "W1"].T, "ab1": g[a + "b1"].reshape(2, P).T,
        "aw2": g[a + "W2"].T.reshape(2, P, DM).transpose(1, 0, 2), "ab2": row(g[a + "b2"]),
        "wg": g[f + "Wg"], "bg": row(g[f + "bg"]),
        "mw1": g[f + "W1"].transpose(1, 0, 2), "mb1": g[f + "b1"].reshape(E, EH // P, P).transpose(2, 0, 1),
        "mw2": g[f + "W2"].reshape(E, EH // P, P, DM).transpose(2, 0, 1, 3), "mb2": g[f + "b2"].T,
        "qrows": _np.repeat([[1], [1], [0], [0]], H * T, axis=1).astype(_mybir.dt.np(_mybir.dt.bfloat16)),
        "krows": _np.ones((3, H * T), _mybir.dt.np(_mybir.dt.bfloat16)),
    }
    nc = _bacc.Bacc("TRN2", target_bir_lowering=False, num_devices=1)
    held, args = {}, []
    for name, v in arrays.items():
        v = _np.ascontiguousarray(v)
        held[f"in_{name}"] = v
        args.append(nc.dram_tensor(f"in_{name}", v.shape, _mybir.dt.from_np(v.dtype), kind="ExternalInput").ap())
    for i, (shape, dtype) in enumerate(_OUTS):
        args.append(nc.dram_tensor(f"out_{i}", shape, _mybir.dt.from_np(_np.dtype(dtype)), kind="ExternalOutput").ap())
    program(nc, *args)
    r = _run(nc, [held], core_ids=[0])
    return r.results[0]["out_0"]
```
